# Optimizing a Trainium2 kernel written in Bass

```python
import numpy as np
import jax
import jax.numpy as jnp

def _softmax(x, axis=-1):
    return jax.nn.softmax(x, axis=axis)

def _gelu(x):
    return jax.nn.gelu(x, approximate=True)

def _silu(x):
    return jax.nn.silu(x)

def _sigmoid(x):
    return jax.nn.sigmoid(x)

def _layernorm(x, axis=-1, eps=1e-05):
    m = jnp.mean(x, axis=axis, keepdims=True)
    v = jnp.var(x, axis=axis, keepdims=True)
    return (x - m) / jnp.sqrt(v + eps)

def _scatter_add(tgt, idx, src, axis=0):
    return tgt.at[idx].add(src)

def _segment_sum(src, seg, n):
    return jax.ops.segment_sum(src, seg, n)
kernel_name = 'mk_flamingo_gated_d2_seqx_r4_c56b54'

def setup_inputs(seed: int=0):
    np.random.seed(seed)
    _w = jnp.asarray

    def _rec_inputs():
        import jax
        import jax.numpy as jnp
        _rk = jax.random.key(seed)
        x = -0.0005146 + 1 * jax.random.normal(jax.random.fold_in(_rk, 1), (16, 112, 256), jnp.float32)
        _lenS = 112 - jax.random.randint(jax.random.fold_in(_rk, 7), (16,), 0, max(1, 112 // 4) + 1, jnp.int32)
        _lenS2 = 375 - jax.random.randint(jax.random.fold_in(_rk, 8), (16,), 0, max(1, 375 // 4) + 1, jnp.int32)
        _ctx_768P = jax.random.normal(jax.random.fold_in(_rk, 11), (16, 16, 192), jnp.float32)
        _ctx_768c = jax.random.dirichlet(jax.random.fold_in(_rk, 511), 0.3 * jnp.ones((16,), jnp.float32), (16, 375))
        _ctx_768t = jnp.einsum('bsk,bkd->bsd', _ctx_768c, _ctx_768P)
        _ctx_768t = _ctx_768t * jax.lax.rsqrt(jnp.mean(jnp.square(_ctx_768t)) + 1e-12) * 0.953939
        ctx_768 = -0.00040386 + 0.999972 * (_ctx_768t + 0.3 * jax.random.normal(jax.random.fold_in(_rk, 611), (16, 375, 192), jnp.float32))
        _validS = jnp.arange(112)[None, :] < _lenS[:, None]
        _validS2 = jnp.arange(375)[None, :] < _lenS2[:, None]
        _causal = jnp.tril(jnp.ones((112, 112), dtype=bool))
        mask_BxS2_bk0 = jnp.logical_not(jnp.broadcast_to(_validS2[:, :], (16, 375)))
        _g = jax.random.normal(jax.random.fold_in(_rk, 9001), (2, 2), jnp.float32)
        _g = jnp.sign(_g) * jnp.maximum(jnp.abs(_g), 1.0) + (_g == 0) * 1.0
        g_xattn = _g[0]
        g_ffn = _g[1]
        return (x, ctx_768, mask_BxS2_bk0, g_xattn, g_ffn)
    x, ctx_768, mask_BxS2_bk0, g_xattn, g_ffn = _rec_inputs()

    def _L0_xattn_setup():
        import jax, jax.numpy as jnp
        import numpy as np
        DIM_IN, DIM_LAT, DIM_HEAD = (192, 256, 64)
        INNER = max(DIM_LAT, DIM_IN)
        HEADS = INNER // DIM_HEAD
        SCALE = DIM_HEAD ** (-0.5)
        RMS_EPS = 1e-08
        LN_EPS = 1e-05

        def layernorm(x, g, b):
            mu = jnp.mean(x, axis=-1, keepdims=True)
            var = jnp.mean((x - mu) ** 2, axis=-1, keepdims=True)
            return (x - mu) * jax.lax.rsqrt(var + LN_EPS) * g + b

        def rmsnorm(x, gamma):
            norm = jnp.sqrt(jnp.sum(x * x, axis=-1, keepdims=True)) * x.shape[-1] ** (-0.5)
            return x / jnp.maximum(norm, RMS_EPS) * gamma
        key = jax.random.key(seed)
        ks = jax.random.split(key, 12)
        b, n, m = (4, 1024, 128)
        x = jax.random.normal(ks[0], (b, n, DIM_IN), jnp.float32)
        latents = jax.random.normal(ks[1], (b, m, DIM_LAT), jnp.float32)
        mask = jax.random.randint(ks[2], (b, n), 0, 2).astype(bool)
        s = lambda k, sh, fan: jax.random.normal(k, sh, jnp.float32) * fan ** (-0.5)
        return {'x': x, 'latents': latents, 'mask': mask, 'ln_x_g': jnp.ones((DIM_IN,), jnp.float32), 'ln_x_b': jnp.zeros((DIM_IN,), jnp.float32), 'ln_l_g': jnp.ones((DIM_LAT,), jnp.float32), 'ln_l_b': jnp.zeros((DIM_LAT,), jnp.float32), 'qn_g': jnp.ones((DIM_HEAD,), jnp.float32), 'kn_g': jnp.ones((DIM_HEAD,), jnp.float32), 'Wq': s(ks[3], (INNER, DIM_LAT), DIM_LAT), 'Wkv': s(ks[4], (2 * INNER, DIM_IN), DIM_IN), 'Wlkv': s(ks[5], (2 * INNER, DIM_LAT), DIM_LAT), 'Wo': s(ks[6], (DIM_LAT, INNER), INNER), 'bo': jnp.zeros((DIM_LAT,), jnp.float32)}
    _L0_xattn_all = _L0_xattn_setup()
    _L0_xattn_in = {k: v for k, v in _L0_xattn_all.items() if k in ('ln_x_g', 'ln_x_b', 'ln_l_g', 'ln_l_b', 'qn_g', 'kn_g', 'Wq', 'Wkv', 'Wlkv', 'Wo', 'bo')}
    del _L0_xattn_all

    def _L0_ffn_setup():
        import jax, jax.numpy as jnp
        import numpy as np
        B, N, D, E, DFF = (4, 512, 256, 16, 1024)
        CAPACITY_FACTOR = 2.0
        CAP = int(N * CAPACITY_FACTOR / E)
        SINKHORN_ITERS = 6

        def _sinkhorn(logits, n_iters=SINKHORN_ITERS, tau=1.0):
            t = logits / tau
            for _ in range(n_iters):
                t = t - jax.scipy.special.logsumexp(t, axis=-2, keepdims=True)
                t = t - jax.scipy.special.logsumexp(t, axis=-1, keepdims=True)
            return jnp.exp(t)
        key = jax.random.key(seed)
        ks = jax.random.split(key, 6)
        scaled = lambda k, sh, fan: (jax.random.normal(k, sh, jnp.float32) / np.sqrt(fan)).astype(jnp.float32)
        return {'x': jax.random.normal(ks[0], (B, N, D), jnp.float32), 'gate_query': scaled(ks[1], (E, D), D), 'log_temp': jnp.asarray(np.log(0.5), jnp.float32), 'w1': scaled(ks[2], (E, D, DFF), D), 'b1': jnp.zeros((E, DFF), jnp.float32), 'w2': scaled(ks[3], (E, DFF, D), DFF), 'b2': jnp.zeros((E, D), jnp.float32)}
    _L0_ffn_all = _L0_ffn_setup()
    _L0_ffn_in = {k: v for k, v in _L0_ffn_all.items() if k in ('gate_query', 'log_temp', 'w1', 'b1', 'w2', 'b2')}
    del _L0_ffn_all

    def _L1_xattn_setup():
        import jax, jax.numpy as jnp
        import numpy as np
        QUERY_DIM = 256
        KEY_DIM = 192
        NUM_HEADS = 16
        HEAD_DIM = QUERY_DIM // NUM_HEADS
        SCALE = HEAD_DIM ** (-0.5)
        key = jax.random.key(seed)
        ks = jax.random.split(key, 11)
        B, Nq, Nk = (4, 1024, 256)
        s_q = QUERY_DIM ** (-0.5)
        s_k = KEY_DIM ** (-0.5)
        return {'query': jax.random.normal(ks[0], (B, Nq, QUERY_DIM), jnp.float32), 'key': jax.random.normal(ks[1], (B, Nk, KEY_DIM), jnp.float32), 'value': jax.random.normal(ks[2], (B, Nk, KEY_DIM), jnp.float32), 'Wq': jax.random.normal(ks[3], (QUERY_DIM, QUERY_DIM), jnp.float32) * s_q, 'bq': jnp.zeros((QUERY_DIM,), jnp.float32), 'Wk': jax.random.normal(ks[4], (KEY_DIM, QUERY_DIM), jnp.float32) * s_k, 'bk': jnp.zeros((QUERY_DIM,), jnp.float32), 'Wv': jax.random.normal(ks[5], (KEY_DIM, QUERY_DIM), jnp.float32) * s_k, 'bv': jnp.zeros((QUERY_DIM,), jnp.float32), 'Wo': jax.random.normal(ks[6], (QUERY_DIM, QUERY_DIM), jnp.float32) * s_q, 'bo': jnp.zeros((QUERY_DIM,), jnp.float32)}
    _L1_xattn_all = _L1_xattn_setup()
    _L1_xattn_in = {k: v for k, v in _L1_xattn_all.items() if k in ('Wq', 'bq', 'Wk', 'bk', 'Wv', 'bv', 'Wo', 'bo')}
    del _L1_xattn_all

    def _L1_ffn_setup():
        import jax, jax.numpy as jnp
        import numpy as np
        H = 256
        I = 512
        NH = 16
        HD = H // NH
        E = 8
        TOPK = 2
        MAX_SEQ = 512
        EPS = 1e-06
        NEG = -1000000000.0

        def precompute_freqs_cis(dim, max_seq_len, theta=10000.0):
            pos = np.arange(max_seq_len, dtype=np.float32)
            freqs = np.arange(0, dim, 2, dtype=np.float32) / dim
            inv_freq = 1.0 / theta ** freqs
            f = np.einsum('i,j->ij', pos, inv_freq)
            return jnp.asarray(np.concatenate([np.cos(f), np.sin(f)], axis=-1), dtype=jnp.float32)

        def rmsnorm(x, w):
            rms = jnp.sqrt(jnp.mean(x * x, axis=-1, keepdims=True) + EPS)
            return w * (x / rms)

        def apply_rope(x, freqs_cis):
            B, S, nh, hd = x.shape
            xr = x.reshape(B, S, nh, hd // 2, 2)
            fr = freqs_cis[:S].reshape(1, S, 1, hd // 2, 2)
            a, b = (xr[..., 0], xr[..., 1])
            cr, ci = (fr[..., 0], fr[..., 1])
            out = jnp.stack([a * cr - b * ci, a * ci + b * cr], axis=-1)
            return out.reshape(B, S, nh, hd)

        def attention(x, wq, wk, wv, wo, freqs_cis):
            B, S, _ = x.shape
            q = (x @ wq).reshape(B, S, NH, HD)
            k = (x @ wk).reshape(B, S, NH, HD)
            v = (x @ wv).reshape(B, S, NH, HD)
            q = apply_rope(q, freqs_cis)
            k = apply_rope(k, freqs_cis)
            scores = jnp.einsum('bqhd,bkhd->bhqk', q, k) / np.sqrt(HD).astype(np.float32)
            causal = jnp.tril(jnp.ones((S, S), dtype=bool))
            scores = jnp.where(causal[None, None], scores, NEG)
            attn = jax.nn.softmax(scores, axis=-1)
            out = jnp.einsum('bhqk,bkhd->bqhd', attn, v).reshape(B, S, H)
            return out @ wo

        def moe_ffn(x, router_w, w1, w2, w3):
            B, S, _ = x.shape
            xt = x.reshape(B * S, H)
            logits = xt @ router_w
            probs = jax.nn.softmax(logits, axis=-1)
            topv, topi = jax.lax.top_k(probs, TOPK)
            topv = topv / jnp.sum(topv, axis=-1, keepdims=True)
            combine = jnp.sum(topv[..., None] * jax.nn.one_hot(topi, E, dtype=xt.dtype), axis=1)
            h1 = jnp.einsum('th,ehi->eti', xt, w1)
            h3 = jnp.einsum('th,ehi->eti', xt, w3)
            ye = jnp.einsum('eti,eih->eth', jax.nn.silu(h1) * h3, w2)
            out = jnp.einsum('te,eth->th', combine, ye)
            return out.reshape(B, S, H)
        key = jax.random.key(seed)
        ks = jax.random.split(key, 12)
        B, S = (2, 256)
        s = lambda fan: 1.0 / np.sqrt(fan)
        inp = {'x': jax.random.normal(ks[0], (B, S, H), dtype=jnp.float32), 'attn_norm_w': jnp.ones((H,), dtype=jnp.float32), 'ffn_norm_w': jnp.ones((H,), dtype=jnp.float32), 'wq': jax.random.normal(ks[1], (H, H), dtype=jnp.float32) * s(H), 'wk': jax.random.normal(ks[2], (H, H), dtype=jnp.float32) * s(H), 'wv': jax.random.normal(ks[3], (H, H), dtype=jnp.float32) * s(H), 'wo': jax.random.normal(ks[4], (H, H), dtype=jnp.float32) * s(H), 'router_w': jax.random.normal(ks[5], (H, E), dtype=jnp.float32) * s(H), 'w1': jax.random.normal(ks[6], (E, H, I), dtype=jnp.float32) * s(H), 'w3': jax.random.normal(ks[7], (E, H, I), dtype=jnp.float32) * s(H), 'w2': jax.random.normal(ks[8], (E, I, H), dtype=jnp.float32) * s(I), 'freqs_cis': precompute_freqs_cis(HD, MAX_SEQ)}
        return inp
    _L1_ffn_all = _L1_ffn_setup()
    _L1_ffn_in = {k: v for k, v in _L1_ffn_all.items() if k in ('attn_norm_w', 'ffn_norm_w', 'wq', 'wk', 'wv', 'wo', 'router_w', 'w1', 'w3', 'w2', 'freqs_cis')}
    del _L1_ffn_all
    return {'x': x, 'ctx_768': ctx_768, 'mask_BxS2_bk0': mask_BxS2_bk0, 'g_xattn': g_xattn, 'g_ffn': g_ffn, 'L0_xattn_ln_x_g': _L0_xattn_in['ln_x_g'], 'L0_xattn_ln_x_b': _L0_xattn_in['ln_x_b'], 'L0_xattn_ln_l_g': _L0_xattn_in['ln_l_g'], 'L0_xattn_ln_l_b': _L0_xattn_in['ln_l_b'], 'L0_xattn_qn_g': _L0_xattn_in['qn_g'], 'L0_xattn_kn_g': _L0_xattn_in['kn_g'], 'L0_xattn_Wq': _L0_xattn_in['Wq'], 'L0_xattn_Wkv': _L0_xattn_in['Wkv'], 'L0_xattn_Wlkv': _L0_xattn_in['Wlkv'], 'L0_xattn_Wo': _L0_xattn_in['Wo'], 'L0_xattn_bo': _L0_xattn_in['bo'], 'L0_ffn_gate_query': _L0_ffn_in['gate_query'], 'L0_ffn_log_temp': _L0_ffn_in['log_temp'], 'L0_ffn_w1': _L0_ffn_in['w1'], 'L0_ffn_b1': _L0_ffn_in['b1'], 'L0_ffn_w2': _L0_ffn_in['w2'], 'L0_ffn_b2': _L0_ffn_in['b2'], 'L1_xattn_Wq': _L1_xattn_in['Wq'], 'L1_xattn_bq': _L1_xattn_in['bq'], 'L1_xattn_Wk': _L1_xattn_in['Wk'], 'L1_xattn_bk': _L1_xattn_in['bk'], 'L1_xattn_Wv': _L1_xattn_in['Wv'], 'L1_xattn_bv': _L1_xattn_in['bv'], 'L1_xattn_Wo': _L1_xattn_in['Wo'], 'L1_xattn_bo': _L1_xattn_in['bo'], 'L1_ffn_attn_norm_w': _L1_ffn_in['attn_norm_w'], 'L1_ffn_ffn_norm_w': _L1_ffn_in['ffn_norm_w'], 'L1_ffn_wq': _L1_ffn_in['wq'], 'L1_ffn_wk': _L1_ffn_in['wk'], 'L1_ffn_wv': _L1_ffn_in['wv'], 'L1_ffn_wo': _L1_ffn_in['wo'], 'L1_ffn_router_w': _L1_ffn_in['router_w'], 'L1_ffn_w1': _L1_ffn_in['w1'], 'L1_ffn_w3': _L1_ffn_in['w3'], 'L1_ffn_w2': _L1_ffn_in['w2'], 'L1_ffn_freqs_cis': _L1_ffn_in['freqs_cis']}

def reference(x, ctx_768, mask_BxS2_bk0, g_xattn, g_ffn, L0_xattn_ln_x_g, L0_xattn_ln_x_b, L0_xattn_ln_l_g, L0_xattn_ln_l_b, L0_xattn_qn_g, L0_xattn_kn_g, L0_xattn_Wq, L0_xattn_Wkv, L0_xattn_Wlkv, L0_xattn_Wo, L0_xattn_bo, L0_ffn_gate_query, L0_ffn_log_temp, L0_ffn_w1, L0_ffn_b1, L0_ffn_w2, L0_ffn_b2, L1_xattn_Wq, L1_xattn_bq, L1_xattn_Wk, L1_xattn_bk, L1_xattn_Wv, L1_xattn_bv, L1_xattn_Wo, L1_xattn_bo, L1_ffn_attn_norm_w, L1_ffn_ffn_norm_w, L1_ffn_wq, L1_ffn_wk, L1_ffn_wv, L1_ffn_wo, L1_ffn_router_w, L1_ffn_w1, L1_ffn_w3, L1_ffn_w2, L1_ffn_freqs_cis):
    import jax
    import jax.numpy as jnp

    def _L0_xattn_ref(x, latents, mask, ln_x_g, ln_x_b, ln_l_g, ln_l_b, qn_g, kn_g, Wq, Wkv, Wlkv, Wo, bo):
        import jax, jax.numpy as jnp
        import numpy as np
        DIM_IN, DIM_LAT, DIM_HEAD = (192, 256, 64)
        INNER = max(DIM_LAT, DIM_IN)
        HEADS = INNER // DIM_HEAD
        SCALE = DIM_HEAD ** (-0.5)
        RMS_EPS = 1e-08
        LN_EPS = 1e-05

        def layernorm(x, g, b):
            mu = jnp.mean(x, axis=-1, keepdims=True)
            var = jnp.mean((x - mu) ** 2, axis=-1, keepdims=True)
            return (x - mu) * jax.lax.rsqrt(var + LN_EPS) * g + b

        def rmsnorm(x, gamma):
            norm = jnp.sqrt(jnp.sum(x * x, axis=-1, keepdims=True)) * x.shape[-1] ** (-0.5)
            return x / jnp.maximum(norm, RMS_EPS) * gamma
        b, n, _ = x.shape
        m = latents.shape[1]
        xn = layernorm(x, ln_x_g, ln_x_b)
        ln = layernorm(latents, ln_l_g, ln_l_b)
        q = ln @ Wq.T
        kv = jnp.concatenate([xn @ Wkv.T, ln @ Wlkv.T], axis=1)
        k, v = (kv[..., :INNER], kv[..., INNER:])
        split_heads = lambda t: t.reshape(t.shape[0], t.shape[1], HEADS, DIM_HEAD).transpose(0, 2, 1, 3)
        q, k, v = (split_heads(q), split_heads(k), split_heads(v))
        qn = rmsnorm(q, qn_g) * SCALE
        kn = rmsnorm(k, kn_g)
        attn = jnp.einsum('bhid,bhjd->bhij', qn, kn)
        full_mask = jnp.pad(mask, ((0, 0), (0, m)), constant_values=True)
        attn = jnp.where(full_mask[:, None, None, :], attn, -jnp.finfo(attn.dtype).max)
        attn = jax.nn.softmax(attn, axis=-1)
        out = jnp.einsum('bhij,bhjd->bhid', attn, v)
        out = out.transpose(0, 2, 1, 3).reshape(b, m, INNER)
        return out @ Wo.T + bo

    def _L0_ffn_ref(x, gate_query, log_temp, w1, b1, w2, b2):
        import jax, jax.numpy as jnp
        import numpy as np
        B, N, D, E, DFF = (4, 512, 256, 16, 1024)
        CAPACITY_FACTOR = 2.0
        CAP = int(N * CAPACITY_FACTOR / E)
        SINKHORN_ITERS = 6

        def _sinkhorn(logits, n_iters=SINKHORN_ITERS, tau=1.0):
            t = logits / tau
            for _ in range(n_iters):
                t = t - jax.scipy.special.logsumexp(t, axis=-2, keepdims=True)
                t = t - jax.scipy.special.logsumexp(t, axis=-1, keepdims=True)
            return jnp.exp(t)
        b, n, d = x.shape
        gate_logits = jnp.einsum('bnd,ed->ben', x, gate_query)
        affinity_logits = gate_logits / jnp.exp(log_temp)
        affinity = _sinkhorn(affinity_logits)
        gates, idx = jax.lax.top_k(affinity, CAP)
        expert_in = jnp.take_along_axis(x[:, None, :, :], idx[..., None], axis=2)
        h = jax.nn.gelu(jnp.einsum('becd,edf->becf', expert_in, w1) + b1[None, :, None, :])
        expert_out = jnp.einsum('becf,efd->becd', h, w2) + b2[None, :, None, :]
        out = jnp.zeros_like(x)
        out = out.at[jnp.arange(b)[:, None, None], idx].add(gates[..., None] * expert_out)
        return out

    def _L1_xattn_ref(query, key, value, Wq, bq, Wk, bk, Wv, bv, Wo, bo):
        import jax, jax.numpy as jnp
        import numpy as np
        QUERY_DIM = 256
        KEY_DIM = 192
        NUM_HEADS = 16
        HEAD_DIM = QUERY_DIM // NUM_HEADS
        SCALE = HEAD_DIM ** (-0.5)
        B, Nq, _ = query.shape
        Nk = key.shape[1]
        q = (query @ Wq + bq).reshape(B, Nq, NUM_HEADS, HEAD_DIM).transpose(0, 2, 1, 3)
        k = (key @ Wk + bk).reshape(B, Nk, NUM_HEADS, HEAD_DIM).transpose(0, 2, 1, 3)
        v = (value @ Wv + bv).reshape(B, Nk, NUM_HEADS, HEAD_DIM).transpose(0, 2, 1, 3)
        attn = jnp.einsum('bhqd,bhkd->bhqk', q, k) * SCALE
        attn = jax.nn.softmax(attn, axis=-1)
        out = jnp.einsum('bhqk,bhkd->bhqd', attn, v)
        out = out.transpose(0, 2, 1, 3).reshape(B, Nq, QUERY_DIM)
        return out @ Wo + bo

    def _L1_ffn_ref(x, attn_norm_w, ffn_norm_w, wq, wk, wv, wo, router_w, w1, w3, w2, freqs_cis):
        import jax, jax.numpy as jnp
        import numpy as np
        H = 256
        I = 512
        NH = 16
        HD = H // NH
        E = 8
        TOPK = 2
        MAX_SEQ = 512
        EPS = 1e-06
        NEG = -1000000000.0

        def precompute_freqs_cis(dim, max_seq_len, theta=10000.0):
            pos = np.arange(max_seq_len, dtype=np.float32)
            freqs = np.arange(0, dim, 2, dtype=np.float32) / dim
            inv_freq = 1.0 / theta ** freqs
            f = np.einsum('i,j->ij', pos, inv_freq)
            return jnp.asarray(np.concatenate([np.cos(f), np.sin(f)], axis=-1), dtype=jnp.float32)

        def rmsnorm(x, w):
            rms = jnp.sqrt(jnp.mean(x * x, axis=-1, keepdims=True) + EPS)
            return w * (x / rms)

        def apply_rope(x, freqs_cis):
            B, S, nh, hd = x.shape
            xr = x.reshape(B, S, nh, hd // 2, 2)
            fr = freqs_cis[:S].reshape(1, S, 1, hd // 2, 2)
            a, b = (xr[..., 0], xr[..., 1])
            cr, ci = (fr[..., 0], fr[..., 1])
            out = jnp.stack([a * cr - b * ci, a * ci + b * cr], axis=-1)
            return out.reshape(B, S, nh, hd)

        def attention(x, wq, wk, wv, wo, freqs_cis):
            B, S, _ = x.shape
            q = (x @ wq).reshape(B, S, NH, HD)
            k = (x @ wk).reshape(B, S, NH, HD)
            v = (x @ wv).reshape(B, S, NH, HD)
            q = apply_rope(q, freqs_cis)
            k = apply_rope(k, freqs_cis)
            scores = jnp.einsum('bqhd,bkhd->bhqk', q, k) / np.sqrt(HD).astype(np.float32)
            causal = jnp.tril(jnp.ones((S, S), dtype=bool))
            scores = jnp.where(causal[None, None], scores, NEG)
            attn = jax.nn.softmax(scores, axis=-1)
            out = jnp.einsum('bhqk,bkhd->bqhd', attn, v).reshape(B, S, H)
            return out @ wo

        def moe_ffn(x, router_w, w1, w2, w3):
            B, S, _ = x.shape
            xt = x.reshape(B * S, H)
            logits = xt @ router_w
            probs = jax.nn.softmax(logits, axis=-1)
            topv, topi = jax.lax.top_k(probs, TOPK)
            topv = topv / jnp.sum(topv, axis=-1, keepdims=True)
            combine = jnp.sum(topv[..., None] * jax.nn.one_hot(topi, E, dtype=xt.dtype), axis=1)
            h1 = jnp.einsum('th,ehi->eti', xt, w1)
            h3 = jnp.einsum('th,ehi->eti', xt, w3)
            ye = jnp.einsum('eti,eih->eth', jax.nn.silu(h1) * h3, w2)
            out = jnp.einsum('te,eth->th', combine, ye)
            return out.reshape(B, S, H)
        h = x + attention(rmsnorm(x, attn_norm_w), wq, wk, wv, wo, freqs_cis)
        out = h + moe_ffn(rmsnorm(h, ffn_norm_w), router_w, w1, w2, w3)
        return out
    x = x + jnp.tanh(g_xattn[0]) * _L0_xattn_ref(ctx_768, _layernorm(x, axis=-1), mask_BxS2_bk0, L0_xattn_ln_x_g, L0_xattn_ln_x_b, L0_xattn_ln_l_g, L0_xattn_ln_l_b, L0_xattn_qn_g, L0_xattn_kn_g, L0_xattn_Wq, L0_xattn_Wkv, L0_xattn_Wlkv, L0_xattn_Wo, L0_xattn_bo)
    x = x + jnp.tanh(g_ffn[0]) * _L0_ffn_ref(_layernorm(x, axis=-1), L0_ffn_gate_query, L0_ffn_log_temp, L0_ffn_w1, L0_ffn_b1, L0_ffn_w2, L0_ffn_b2)
    x = x + jnp.tanh(g_xattn[1]) * _L1_xattn_ref(_layernorm(x, axis=-1), ctx_768, ctx_768, L1_xattn_Wq, L1_xattn_bq, L1_xattn_Wk, L1_xattn_bk, L1_xattn_Wv, L1_xattn_bv, L1_xattn_Wo, L1_xattn_bo)
    x = x + jnp.tanh(g_ffn[1]) * _L1_ffn_ref(_layernorm(x, axis=-1), L1_ffn_attn_norm_w, L1_ffn_ffn_norm_w, L1_ffn_wq, L1_ffn_wk, L1_ffn_wv, L1_ffn_wo, L1_ffn_router_w, L1_ffn_w1, L1_ffn_w3, L1_ffn_w2, L1_ffn_freqs_cis)
    return x

_drawn_inputs = setup_inputs


def setup_inputs(seed=0):
    import zlib

    import numpy as np

    out = dict(_drawn_inputs(seed))
    spreads = {'g_ffn': (-1.0, 0.2),
     'L0_xattn_ln_x_g': (1.0, 0.2),
     'L0_xattn_ln_x_b': (0.0, 0.1),
     'L0_xattn_ln_l_g': (1.0, 0.2),
     'L0_xattn_ln_l_b': (0.0, 0.1),
     'L0_xattn_qn_g': (1.0, 0.2),
     'L0_xattn_kn_g': (1.0, 0.2),
     'L0_xattn_bo': (0.0, 0.1),
     'L0_ffn_b1': (0.0, 0.27),
     'L0_ffn_b2': (0.0, 0.1),
     'L1_xattn_bq': (0.0, 0.1),
     'L1_xattn_bk': (0.0, 0.8),
     'L1_xattn_bv': (0.0, 0.1),
     'L1_xattn_bo': (0.0, 0.1),
     'L1_ffn_attn_norm_w': (1.0, 0.2),
     'L1_ffn_ffn_norm_w': (1.0, 0.2)}
    factors = {}
    for name, (base, spread) in spreads.items():
        noise = np.random.default_rng([zlib.crc32(name.encode()), seed]).standard_normal(out[name].shape)
        drawn = base * np.exp(spread * noise) if base else spread * noise
        out[name] = jnp.asarray(drawn.astype(out[name].dtype))
    for name, factor in factors.items():
        out[name] = (out[name] * factor).astype(out[name].dtype)
    return out
```

```python
from contextlib import ExitStack

import concourse.bass as bass
from concourse import mybir

F32 = mybir.dt.float32
F16 = mybir.dt.float16
U8 = mybir.dt.uint8
ALU = mybir.AluOpType
ACT = mybir.ActivationFunctionType
AX = mybir.AxisListType

B, S, D = 16, 112, 256
C, CD = 375, 192
CT, CP = 3, 125
CF = CD // 2
DC = D // 128
H0, HD0 = 4, 64
KEYS0 = C + S
H1, HD1 = 16, 16
PAD = 32
HG = 128 // PAD
E0, F0, CAP = 16, 1024, 64
SINKHORN = 6
E1, F1, TOP = 8, 512, 2
LN_EPS = 1e-5
RMS_EPS = 1e-6
RMS_MIN_SQ = 1e-16
NEG = -1e9
MASKED = 1e30

COLS, ROWS = {}, {}
for _name, _n in (("lnx_g", 2), ("lnx_b", 2), ("lnl_g", 2), ("lnl_b", 2), ("qn_g", 1), ("kn_g", 1),
                  ("bq", 4), ("bk", 4), ("attn_w", 2), ("ffn_w", 2)):
    COLS[_name] = (sum(n for _, n in COLS.values()), _n)
for _name, _n in (("g_xattn", 2), ("g_ffn", 2), ("log_temp", 1), ("bo0", D), ("bo1", D), ("bv1", D),
                  ("iota", CAP)):
    ROWS[_name] = (sum(n for _, n in ROWS.values()), _n)
NCOLS = sum(n for _, n in COLS.values())
NROWS = sum(n for _, n in ROWS.values())


def widen(ap, axis, n):
    ap = ap.unsqueeze(axis)
    shape = list(ap.shape)
    shape[axis] = n
    return ap.broadcast_to(shape)


class Chain:

    def __init__(self, eng, sem, base=0):
        self.eng, self.sem, self.base, self.n = eng, sem, base, 0

    def __call__(self, instruction):
        self.n += 1
        instruction.then_inc(self.sem, 1)
        self.eng.wait_ge(self.sem, self.base + self.n)


class Core:

    def __init__(self, nc, inputs, out):
        self.nc, self.inp, self.out = nc, inputs, out
        self.stack, self.ctx_stack = ExitStack(), ExitStack()

    def col(self, name, c=0, n=1, parts=128):
        at = COLS[name][0] + c
        return self.cols[0:parts, at:at + n]

    def row(self, name, c=0, n=None, parts=S):
        at, width = ROWS[name]
        return self.rows[0:parts, at + c:at + c + (width - c if n is None else n)]


class Stage:

    def __init__(self, core, name):
        self.nc, self.name, self.stack = core.nc, name, ExitStack()

    def __enter__(self):
        self.stack.__enter__()
        return self

    def __exit__(self, *a):
        return self.stack.__exit__(*a)

    def sb(self, name, shape, dt=F32):
        return self.stack.enter_context(self.nc.sbuf_tensor(f"{self.name}_{name}", shape, dt))

    def bank(self, name, dt=F32, cols=512):
        return self.stack.enter_context(self.nc.psum_tensor(f"{self.name}_{name}", [128, cols], dt))

    def sem(self, name):
        return self.stack.enter_context(self.nc.semaphore(f"{self.name}_{name}"))

    def block(self):
        return self.stack.enter_context(self.nc.Block())


def load_stage(core):
    nc, inp = core.nc, core.inp

    def keep(name, shape, dt=F32):
        return core.stack.enter_context(nc.sbuf_tensor(name, shape, dt))

    core.x = keep("x_tokens", [S, B, D])
    core.ident = keep("ident", [128, 128])
    core.cols = keep("cols", [128, NCOLS])
    core.rows = keep("rows", [128, NROWS])
    core.half = keep("minus_half", [128, 64])
    core.gate = keep("gate_tanh", [128, 4])
    core.ctx = core.ctx_stack.enter_context(nc.sbuf_tensor("ctx_tokens", [CP, B * CT, CD], F32))
    with Stage(core, "load") as st:
        loaded = st.sem("loaded")
        with nc.Block() as block:

            @block.sync
            def _(sp):
                sp.dma_start(core.x[:], inp["x"].rearrange("b s d -> s b d")).then_inc(loaded, 16)
                sp.dma_start(core.ident[:], inp["ident"]).then_inc(loaded, 16)
                sp.dma_start(core.cols[:], inp["cols"]).then_inc(loaded, 16)
                sp.dma_start(core.rows[:], inp["rows"].broadcast_to([128, NROWS])).then_inc(loaded, 16)
                sp.dma_start(core.ctx[:].rearrange("p (b t) d -> p b t d", t=CT),
                             inp["ctx"].rearrange("b (t p) d -> p b t d", p=CP)).then_inc(loaded, 16)
                sp.wait_ge(loaded, 80)

            @block.gpsimd
            def _(pool):
                pool.memset(core.half[:], -0.5)

            @block.scalar
            def _(act):
                act.wait_ge(loaded, 80)
                act.activation(core.gate[:], core.rows[:, 0:4], ACT.Tanh)


def stats_stage(core, name, x, parts, tiles, mean, var_eps, rstd):
    nc = core.nc
    n = x.shape[2]
    with Stage(core, name) as st:
        raw = st.sb("raw", [parts, tiles, 6])
        tmp = st.sb("tmp", [parts, tiles])
        dev = st.sb("dev", [parts, tiles])
        dve_step, var_ready = st.sem("dve_step"), st.sem("var_ready")
        with nc.Block() as block:

            @block.vector
            def _(dve):
                step = Chain(dve, dve_step)
                with dve.Fori(0, tiles) as t:
                    dve.bn_stats(raw[:, bass.ds(t, 1), :].rearrange("p a b -> p (a b)"),
                                 x[:, bass.ds(t, 1), :].rearrange("p a b -> p (a b)")).then_inc(dve_step, 1)
                dve.wait_ge(dve_step, tiles)
                step.n = tiles
                step(dve.tensor_tensor(mean, raw[:, :, 1], raw[:, :, 4], ALU.add))
                step(dve.tensor_scalar(mean, mean, 0.5, None, ALU.mult))
                step(dve.tensor_tensor(dev[:], raw[:, :, 1], raw[:, :, 4], ALU.subtract))
                step(dve.scalar_tensor_tensor(out=dev[:], in0=dev[:], scalar=0.25, in1=dev[:],
                                              op0=ALU.mult, op1=ALU.mult))
                step(dve.tensor_tensor(tmp[:], raw[:, :, 2], raw[:, :, 5], ALU.add))
                step(dve.scalar_tensor_tensor(out=dev[:], in0=tmp[:], scalar=1.0 / n, in1=dev[:],
                                              op0=ALU.mult, op1=ALU.add))
                dve.tensor_scalar(var_eps, dev[:], LN_EPS, None, ALU.add).then_inc(var_ready, 1)

            @block.gpsimd
            def _(pool):
                pool.wait_ge(var_ready, 1)
                pool.tensor_tensor(rstd, var_eps, core.half[0:parts, 0:tiles], ALU.pow)


def l0_xattn_stage(core):
    nc, inp = core.nc, core.inp
    with Stage(core, "xa0") as st:
        xmean, xve, xrstd = (st.sb(n, [S, B]) for n in ("xmean", "xve", "xrstd"))
        cmean, cve, crstd = (st.sb(n, [CP, B * CT]) for n in ("cmean", "cve", "crstd"))
        stats_stage(core, "xa0_xs", core.x, S, B, xmean[:], xve[:], xrstd[:])
        stats_stage(core, "xa0_cs", core.ctx, CP, B * CT, cmean[:], cve[:], crstd[:])

        wkv = st.sb("wkv", [CF, 2, 2 * D])
        wl = st.sb("wl", [128, DC, 3 * D])
        wo = st.sb("wo", [128, DC, D])
        masks = st.sb("masks", [S, B, C], U8)
        maskadd = st.sb("maskadd", [S, KEYS0])
        bo = st.sb("bo", [S, D])
        gq = st.sb("gq", [128, 1])
        cn = st.sb("cn", [CP, CT, CD])
        xn = st.sb("xn", [S, D])
        cT = st.sb("cT", [CF, 2, C])
        xT = st.sb("xT", [128, DC, S])
        kv = st.sb("kv", [CP, CT, 2 * D])
        lat = st.sb("lat", [S, 3 * D])
        sqc = st.sb("sqc", [CP, CT, D])
        sql = st.sb("sql", [S, 2 * D])
        ssc, rrc = st.sb("ssc", [CP, CT * H0]), st.sb("rrc", [CP, CT * H0])
        ssl, rrl = st.sb("ssl", [S, 2 * H0]), st.sb("rrl", [S, 2 * H0])
        kT = st.sb("kT", [128, DC, KEYS0])
        qT = st.sb("qT", [128, DC, S])
        scores = st.sb("scores", [S, 2, KEYS0])
        top = st.sb("top", [S, H0])
        probs = st.sb("probs", [S, 2, KEYS0])
        total, rtotal = st.sb("total", [S, H0]), st.sb("rtotal", [S, H0])
        pT = st.sb("pT", [CP, 2, 4 * S])
        heads = st.sb("heads", [S, D])
        headsT = st.sb("headsT", [128, DC, S])
        add = st.sb("add", [S, D])
        trans = [st.bank("trans0"), st.bank("trans1")]
        proj = [st.bank("proj0"), st.bank("proj1")]
        score = [st.bank("score0"), st.bank("score1")]
        ptb, outb = st.bank("ptb"), st.bank("outb")

        names = ("weights_in dve_step ready_once cn_ready trans_written cT_ready xT_ready proj_written "
                 "kv_ready ss_ready rr_ready kqn_ready kT_written kT_ready qT_ready score_written "
                 "scores_ready probs_ready pT_written pT_ready out_written heads_ready headsT_written "
                 "headsT_ready wo_written x_updated held").split()
        (weights_in, dve_step, ready_once, cn_ready, trans_written, cT_ready, xT_ready, proj_written,
         kv_ready, ss_ready, rr_ready, kqn_ready, kT_written, kT_ready, qT_ready, score_written,
         scores_ready, probs_ready, pT_written, pT_ready, out_written, heads_ready, headsT_written,
         headsT_ready, wo_written, x_updated, held) = (st.sem(n) for n in names)

        with nc.Block() as block:

            @block.sync
            def _(sp):
                sp.dma_start(wkv[:], inp["w0kv"].rearrange("(c p) n -> p c n", p=CF)).then_inc(weights_in, 16)
                sp.dma_start(wl[:], inp["w0l"].rearrange("(c p) n -> p c n", p=128)).then_inc(weights_in, 16)
                sp.dma_start(wo[:], inp["w0o"].rearrange("(c p) n -> p c n", p=128)).then_inc(weights_in, 16)
                sp.dma_start(masks[:].rearrange("p b c -> p (b c)"),
                             inp["mask"].broadcast_to([S, B * C])).then_inc(weights_in, 16)
                sp.wait_ge(weights_in, 64)

            @block.vector
            def _(dve):
                step = Chain(dve, dve_step)
                dve.wait_ge(weights_in, 64)
                step(dve.tensor_scalar(xve[:], xve[:], -LN_EPS, None, ALU.add))
                step(dve.tensor_tensor(xve[:], xve[:], xrstd[:], ALU.mult))
                step(dve.tensor_tensor(xve[:], xve[:], xrstd[:], ALU.mult))
                dve.tensor_scalar(xve[:], xve[:], LN_EPS, None, ALU.add).then_inc(ready_once, 1)
                dve.tensor_scalar(gq[:], core.col("qn_g"), HD0 ** -0.5, None, ALU.mult).then_inc(ready_once, 1)
                dve.memset(maskadd[:], 0.0).then_inc(ready_once, 1)
                dve.tensor_scalar(bo[:], core.row("bo0"), core.gate[0:S, 0:1], None, ALU.mult)\
                   .then_inc(ready_once, 1)
                dve.memset(ptb[:], 0.0).then_inc(ready_once, 1)
                dve.wait_ge(ready_once, 6)
                step(dve.tensor_tensor(xrstd[:], xrstd[:], xve[:], ALU.mult))
                fixed = step.n
                PER = 3
                with dve.Fori(0, B) as b:
                    step = Chain(dve, dve_step, PER * b + fixed)
                    if True:
                        dve.tensor_scalar(maskadd[:, 0:C], masks[:, bass.ds(b, 1), :].rearrange("p a c -> p (a c)"),
                                          -1.0, MASKED, ALU.add, ALU.mult).then_inc(dve_step, 1)
                        step.n += 1
                    for t in range(CT):
                        dve.tensor_scalar(cn[:, t, :],
                                          core.ctx[:, bass.ds(b * CT + t, 1), :].rearrange("p a c -> p (a c)"),
                                          cmean[:, bass.ds(b * CT + t, 1)], crstd[:, bass.ds(b * CT + t, 1)],
                                          ALU.subtract, ALU.mult).then_inc(cn_ready, 1)
                    dve.tensor_scalar(xn[:], core.x[:, bass.ds(b, 1), :].rearrange("p a c -> p (a c)"),
                                      xmean[:, bass.ds(b, 1)], xrstd[:, bass.ds(b, 1)],
                                      ALU.subtract, ALU.mult).then_inc(cn_ready, 1)
                    dve.wait_ge(kv_ready, 5 * b + 3)
                    kc = kv[:, :, 0:D]
                    step(dve.tensor_tensor(sqc[:], kc, kc, ALU.mult))
                    dve.tensor_reduce(ssc[:], sqc[:].rearrange("p t (h d) -> p (t h) d", h=H0), AX.X, ALU.add)\
                       .then_inc(ss_ready, 1)
                    dve.wait_ge(kv_ready, 5 * b + 4)
                    step(dve.tensor_tensor(sql[:], lat[:, 0:2 * D], lat[:, 0:2 * D], ALU.mult))
                    dve.tensor_reduce(ssl[:], sql[:].rearrange("p (h d) -> p h d", h=2 * H0), AX.X, ALU.add)\
                       .then_inc(ss_ready, 1)
                    dve.wait_ge(ss_ready, 4 * b + 2)
                    dve.tensor_scalar(ssc[:], ssc[:], 1.0 / HD0, RMS_MIN_SQ, ALU.mult, ALU.max).then_inc(ss_ready, 1)
                    dve.tensor_scalar(ssl[:], ssl[:], 1.0 / HD0, RMS_MIN_SQ, ALU.mult, ALU.max).then_inc(ss_ready, 1)
                    dve.wait_ge(rr_ready, 2 * b + 2)
                    for t in range(CT):
                        k4 = kv[:, t, 0:D].rearrange("p (h d) -> p h d", h=H0)
                        dve.tensor_tensor(sqc[:, t, :].rearrange("p (h d) -> p h d", h=H0), k4,
                                          widen(rrc[:, t * H0:(t + 1) * H0], 2, HD0), ALU.mult).then_inc(kqn_ready, 1)
                    dve.tensor_tensor(sql[:].rearrange("p (h d) -> p h d", h=2 * H0),
                                      lat[:, 0:2 * D].rearrange("p (h d) -> p h d", h=2 * H0),
                                      widen(rrl[:], 2, HD0), ALU.mult).then_inc(kqn_ready, 1)

                    def mask_and_max(h):
                        dve.wait_ge(score_written, H0 * b + h + 1)
                        if h == 0:
                            dve.wait_ge(dve_step, PER * b + fixed + 1)
                        if h >= 2:
                            dve.wait_ge(probs_ready, H0 * b + h - 1)
                        dve.sem_inc(held, 1)
                        dve.tensor_tensor_reduce(out=scores[:, h % 2, :], in0=score[h % 2][0:S, 0:KEYS0],
                                                 in1=maskadd[:], scale=-1.0, scalar=3e38, op0=ALU.add,
                                                 op1=ALU.min, accum_out=top[:, h:h + 1]).then_inc(scores_ready, 1)

                    mask_and_max(0)
                    mask_and_max(1)
                    for h in range(H0):
                        dve.wait_ge(pT_written, H0 * b + h + 1)
                        dve.tensor_copy(pT[:, h % 2, :], ptb[0:CP, 0:4 * S]).then_inc(pT_ready, 1)
                        if h + 2 < H0:
                            mask_and_max(h + 2)
                    dve.wait_ge(probs_ready, H0 * b + H0)
                    dve.reciprocal(rtotal[:], total[:]).then_inc(heads_ready, 1)
                    dve.wait_ge(heads_ready, 2 * b + 1)
                    dve.wait_ge(out_written, b + 1)
                    dve.tensor_tensor(heads[:].rearrange("p (h d) -> p h d", h=H0),
                                      outb[0:S, 0:D].rearrange("p (h d) -> p h d", h=H0),
                                      widen(rtotal[:], 2, HD0), ALU.mult).then_inc(heads_ready, 1)
                    dve.wait_ge(wo_written, b + 1)
                    dve.scalar_tensor_tensor(out=add[:], in0=proj[1][0:S, 0:D], scalar=core.gate[0:S, 0:1],
                                             in1=bo[:], op0=ALU.mult, op1=ALU.add).then_inc(x_updated, 1)
                    dve.wait_ge(x_updated, 2 * b + 1)
                    xb = core.x[:, bass.ds(b, 1), :].rearrange("p a c -> p (a c)")
                    dve.tensor_tensor(xb, xb, add[:], ALU.add).then_inc(x_updated, 1)
                    assert step.n == PER, step.n

            @block.gpsimd
            def _(pool):
                pool.wait_ge(ready_once, 1)
                pool.tensor_tensor(xve[:], xve[:], core.half[0:S, 0:B], ALU.pow).then_inc(ready_once, 1)
                with pool.Fori(0, B) as b:
                    pool.wait_ge(ss_ready, 4 * b + 4)
                    pool.tensor_tensor(rrc[:], ssc[:], core.half[0:CP, 0:CT * H0], ALU.pow).then_inc(rr_ready, 1)
                    pool.tensor_tensor(rrl[:], ssl[:], core.half[0:S, 0:2 * H0], ALU.pow).then_inc(rr_ready, 1)

            @block.scalar
            def _(act):
                act.wait_ge(ready_once, 6)
                with act.Fori(0, B) as b:
                    for c in range(2):
                        act.wait_ge(trans_written, 3 * b + c + 1)
                        act.activation(cT[:, c, :], trans[c][0:CF, 0:C], ACT.Identity,
                                       scale=core.col("lnx_g", c, parts=CF), bias=core.col("lnx_b", c, parts=CF))\
                           .then_inc(cT_ready, 1)
                    act.wait_ge(trans_written, 3 * b + 3)
                    for c in range(DC):
                        act.activation(xT[:, c, :], proj[0][:, c * S:(c + 1) * S], ACT.Identity,
                                       scale=core.col("lnl_g", c), bias=core.col("lnl_b", c)).then_inc(xT_ready, 1)
                    for t in range(CT):
                        act.wait_ge(proj_written, 5 * b + t + 1)
                        act.activation(kv[:, t, :], proj[(t + 1) % 2][0:CP, :], ACT.Copy).then_inc(kv_ready, 1)
                    act.wait_ge(proj_written, 5 * b + 4)
                    act.activation(lat[:, 0:2 * D], proj[0][0:S, :], ACT.Copy).then_inc(kv_ready, 1)
                    act.wait_ge(proj_written, 5 * b + 5)
                    act.activation(lat[:, 2 * D:3 * D], proj[1][0:S, 0:D], ACT.Copy).then_inc(kv_ready, 1)
                    for c in range(DC):
                        act.wait_ge(kT_written, 3 * b + c + 1)
                        act.activation(kT[:, c, :], trans[c][:, 0:KEYS0], ACT.Copy, scale=core.col("kn_g"))\
                           .then_inc(kT_ready, 1)
                    act.wait_ge(kT_written, 3 * b + 3)
                    act.activation(qT[:].rearrange("p c s -> p (c s)"), proj[0][:, 0:DC * S], ACT.Copy,
                                   scale=gq[:]).then_inc(qT_ready, 1)
                    for h in range(H0):
                        act.wait_ge(scores_ready, H0 * b + h + 1)
                        if h >= 2:
                            act.wait_ge(pT_written, H0 * b + h - 1)
                        act.activation(probs[:, h % 2, :], scores[:, h % 2, :], ACT.Exp, scale=-1.0,
                                       bias=top[:, h:h + 1], accum_out=total[:, h:h + 1]).then_inc(probs_ready, 1)
                    act.wait_ge(headsT_written, b + 1)
                    act.activation(headsT[:].rearrange("p c s -> p (c s)"), proj[0][:, 0:DC * S], ACT.Copy)\
                       .then_inc(headsT_ready, 1)

            @block.tensor
            def _(pe):
                idc, ids = core.ident[0:CP, 0:CP], core.ident[0:S, 0:S]
                pe.wait_ge(weights_in, 64)
                pe.wait_ge(ready_once, 6)
                with pe.Fori(0, B) as b:
                    pe.wait_ge(cn_ready, 4 * b + 4)
                    for c in range(2):
                        for t in range(CT):
                            last = pe.transpose(trans[c][0:CF, t * CP:(t + 1) * CP], cn[:, t, c * CF:(c + 1) * CF], idc)
                        last.then_inc(trans_written, 1)
                    for c in range(DC):
                        last = pe.transpose(proj[0][:, c * S:(c + 1) * S], xn[:, c * 128:(c + 1) * 128], ids)
                    last.then_inc(trans_written, 1)
                    pe.wait_ge(cT_ready, 2 * b + 2)
                    for t in range(CT):
                        if t == 1:
                            pe.wait_ge(xT_ready, 2 * b + 2)
                        if t == 2:
                            pe.wait_ge(kv_ready, 5 * b + 1)
                        for c in range(2):
                            last = pe.matmul(proj[(t + 1) % 2][0:CP, :], cT[:, c, t * CP:(t + 1) * CP], wkv[:, c, :],
                                             start=(c == 0), stop=(c == 1))
                        last.then_inc(proj_written, 1)
                    pe.wait_ge(kv_ready, 5 * b + 2)
                    for c in range(DC):
                        last = pe.matmul(proj[0][0:S, :], xT[:, c, :], wl[:, c, 0:2 * D], start=(c == 0),
                                         stop=(c == DC - 1))
                    last.then_inc(proj_written, 1)
                    pe.wait_ge(kv_ready, 5 * b + 3)
                    for c in range(DC):
                        last = pe.matmul(proj[1][0:S, 0:D], xT[:, c, :], wl[:, c, 2 * D:3 * D], start=(c == 0),
                                         stop=(c == DC - 1))
                    last.then_inc(proj_written, 1)
                    pe.wait_ge(kqn_ready, 4 * b + 4)
                    for c in range(DC):
                        for t in range(CT):
                            pe.transpose(trans[c][:, t * CP:(t + 1) * CP], sqc[:, t, c * 128:(c + 1) * 128], idc)
                        pe.transpose(trans[c][:, C:KEYS0], sql[:, c * 128:(c + 1) * 128], ids)\
                          .then_inc(kT_written, 1)
                    pe.wait_ge(kv_ready, 5 * b + 4)
                    for c in range(DC):
                        last = pe.transpose(proj[0][:, c * S:(c + 1) * S], sql[:, D + c * 128:D + (c + 1) * 128], ids)
                    last.then_inc(kT_written, 1)
                    pe.wait_ge(kT_ready, 2 * b + 2)
                    pe.wait_ge(qT_ready, b + 1)

                    def score_head(h):
                        if h >= 2:
                            pe.wait_ge(scores_ready, H0 * b + h - 1)
                        r = HD0 * (h % 2)
                        pe.matmul(score[h % 2][0:S, 0:KEYS0], qT[r:r + HD0, h // 2, :], kT[r:r + HD0, h // 2, :],
                                  start=True, stop=True).then_inc(score_written, 1)

                    score_head(0)
                    score_head(1)
                    for h in range(H0):
                        pe.wait_ge(probs_ready, H0 * b + h + 1)
                        if h >= 1:
                            pe.wait_ge(pT_ready, H0 * b + h)
                        for t in range(CT):
                            pe.transpose(ptb[0:CP, t * S:(t + 1) * S], probs[:, h % 2, t * CP:(t + 1) * CP], ids)
                        pe.transpose(ptb[0:S, CT * S:(CT + 1) * S], probs[:, h % 2, C:KEYS0], ids)\
                          .then_inc(pT_written, 1)
                        if h + 2 < H0:
                            score_head(h + 2)
                        pe.wait_ge(pT_ready, H0 * b + h + 1)
                        if h == 0:
                            pe.wait_ge(kv_ready, 5 * b + 5)
                        o = outb[0:S, h * HD0:(h + 1) * HD0]
                        for t in range(CT):
                            pe.matmul(o, pT[:, h % 2, t * S:(t + 1) * S], kv[:, t, D + h * HD0:D + (h + 1) * HD0],
                                      start=(t == 0), stop=False)
                        last = pe.matmul(o, pT[0:S, h % 2, CT * S:(CT + 1) * S],
                                         lat[:, 2 * D + h * HD0:2 * D + (h + 1) * HD0], start=False, stop=True)
                    last.then_inc(out_written, 1)
                    pe.wait_ge(heads_ready, 2 * b + 2)
                    for c in range(DC):
                        last = pe.transpose(proj[0][:, c * S:(c + 1) * S], heads[:, c * 128:(c + 1) * 128], ids)
                    last.then_inc(headsT_written, 1)
                    pe.wait_ge(headsT_ready, b + 1)
                    for c in range(DC):
                        last = pe.matmul(proj[1][0:S, 0:D], headsT[:, c, :], wo[:, c, :], start=(c == 0),
                                         stop=(c == DC - 1))
                    last.then_inc(wo_written, 1)


def routing_stage(core, keep):
    nc, inp = core.nc, core.inp
    BE = B * E0
    HALF = BE // 2
    core.norm_hi = keep("norm_hi", [S, B, D], F16)
    core.norm_lo = keep("norm_lo", [S, B, D], F16)
    core.place = keep("place", [S, BE])
    core.gates = keep("gates", [S, BE])
    with Stage(core, "route") as st:
        mean, ve, rstd = (st.sb(n, [S, B]) for n in ("mean", "ve", "rstd"))
        stats_stage(core, "route_s", core.x, S, B, mean[:], ve[:], rstd[:])
        gq = st.sb("gq", [128, DC, E0])
        xn = st.sb("xn", [S, 2, D])
        xT = st.sb("xT", [128, 2, DC * S])
        invt = st.sb("invt", [S, 1])
        t = st.sb("t", [S, BE])
        e = st.sb("e", [S, BE])
        m, s, ln = (st.sb(n, [S, B]) for n in ("m", "s", "ln"))
        u = st.sb("u", [HALF, 2, S])
        v = st.sb("v", [HALF, 2, S])
        um, us, ul = (st.sb(n, [HALF, 2]) for n in ("um", "us", "ul"))
        aff = st.sb("aff", [HALF, 2, S])
        left = st.sb("left", [HALF, 2, S])
        best = st.sb("best", [HALF, 2, 8])
        taken = st.sb("taken", [HALF, 2, S])
        order = st.sb("order", [HALF, 2, S])
        ones = st.sb("ones", [HALF, S])
        logits = st.bank("logits")
        xTb = [st.bank("xTb0"), st.bank("xTb1")]
        by_row = st.bank("by_row")
        by_token = st.bank("by_token")
        by_token2 = st.bank("by_token2")
        (loaded, dve_step, normed, split, xT_written, xT_ready, logits_written, t_ready, row_ready, row_written,
         m_ready, e_ready, s_ready, l_ready, token_written, aff_ready, place_written, tscale) = (
            st.sem(n) for n in "loaded dve_step normed split xT_written xT_ready logits_written t_ready row_ready "
            "row_written m_ready e_ready s_ready l_ready token_written aff_ready place_written tscale".split())
        with nc.Block() as block:

            @block.sync
            def _(sp):
                sp.dma_start(gq[:], inp["gate_query"].rearrange("(c p) n -> p c n", p=128)).then_inc(loaded, 16)
                sp.wait_ge(loaded, 16)

            @block.vector
            def _(dve):
                with dve.Fori(0, B // 2) as i:
                    for k in range(2):
                        xb = core.x[:, bass.ds(2 * i + k, 1), :].rearrange("p a c -> p (a c)")
                        hi = core.norm_hi[:, bass.ds(2 * i + k, 1), :].rearrange("p a c -> p (a c)")
                        lo = core.norm_lo[:, bass.ds(2 * i + k, 1), :].rearrange("p a c -> p (a c)")
                        dve.wait_ge(xT_written, 2 * i + k + 1)
                        dve.tensor_scalar(xn[:, k, :], xb, mean[:, bass.ds(2 * i + k, 1)],
                                          rstd[:, bass.ds(2 * i + k, 1)], ALU.subtract, ALU.mult).then_inc(normed, 1)
                        dve.wait_ge(normed, 2 * i + k + 1)
                        dve.tensor_scalar(hi, xn[:, k, :], 1.0, None, ALU.mult).then_inc(split, 1)
                        dve.wait_ge(split, 2 * i + k + 1)
                        dve.tensor_tensor(lo, xn[:, k, :], hi, ALU.subtract)
                step = Chain(dve, dve_step)
                step(dve.memset(ones[:], 1.0))
                dve.wait_ge(logits_written, B)
                dve.wait_ge(tscale, 1)
                dve.tensor_scalar(t[:], logits[0:S, 0:BE], invt[:], None, ALU.mult).then_inc(t_ready, 1)
                fixed = step.n
                PER = 2
                with dve.Fori(0, SINKHORN) as i:
                    step = Chain(dve, dve_step, PER * i + fixed)
                    dve.wait_ge(t_ready, 2 * i + 1)
                    t3 = t[:].rearrange("p (b e) -> p b e", e=E0)
                    step(dve.tensor_reduce(m[:], t3, AX.X, ALU.max))
                    dve.tensor_tensor(t3, t3, widen(m[:], 2, E0), ALU.subtract).then_inc(t_ready, 1)
                    dve.wait_ge(e_ready, 2 * i + 1)
                    dve.tensor_reduce(s[:], e[:].rearrange("p (b e) -> p b e", e=E0), AX.X, ALU.add)\
                       .then_inc(s_ready, 1)
                    dve.wait_ge(l_ready, 2 * i + 1)
                    dve.tensor_tensor(t3, t3, widen(ln[:], 2, E0), ALU.subtract).then_inc(row_ready, 1)
                    dve.wait_ge(row_written, i + 1)
                    r3 = by_row[0:HALF, 0:2 * S].rearrange("p (c s) -> p c s", c=2)
                    step(dve.tensor_reduce(um[:], r3, AX.X, ALU.max))
                    dve.tensor_tensor(u[:], r3, widen(um[:], 2, S), ALU.subtract).then_inc(row_ready, 1)
                    dve.wait_ge(e_ready, 2 * i + 2)
                    dve.tensor_reduce(us[:], v[:], AX.X, ALU.add).then_inc(s_ready, 1)
                    dve.wait_ge(l_ready, 2 * i + 2)
                    dve.tensor_tensor(u[:], u[:], widen(ul[:], 2, S), ALU.subtract).then_inc(row_ready, 1)
                    dve.wait_ge(token_written, i + 1)
                    dve.tensor_copy(t[:], by_token[0:S, 0:BE]).then_inc(t_ready, 1)
                    assert step.n == PER
                step = Chain(dve, dve_step, 0)
                step.n = PER * SINKHORN + fixed
                dve.wait_ge(aff_ready, 1)
                step(dve.tensor_copy(left[:], aff[:]))
                for r in range(CAP // 8):
                    for c in range(2):
                        last = dve.max(best[:, c, :], left[:, c, :])
                    step(last)
                    for c in range(2):
                        last = dve.match_replace(left[:, c, :], best[:, c, :], left[:, c, :], -1.0)
                    step(last)
                step(dve.tensor_scalar(taken[:], left[:], 0.0, None, ALU.is_lt))
                for c in range(2):
                    last = dve.tensor_tensor_scan(order[:, c, :], ones[:], taken[:, c, :], 0.0, ALU.mult, ALU.add)
                step(last)
                step(dve.tensor_tensor(order[:], order[:], taken[:], ALU.mult))
                step(dve.tensor_tensor(taken[:], aff[:], taken[:], ALU.mult))
                dve.tensor_scalar(order[:], order[:], -1.0, None, ALU.add).then_inc(aff_ready, 1)
                dve.wait_ge(place_written, 1)
                dve.tensor_copy(core.place[:], by_token[0:S, 0:BE])
                dve.wait_ge(place_written, 2)
                dve.tensor_scalar(core.gates[:], by_token2[0:S, 0:BE], core.gate[0:S, 2:3], None, ALU.mult)

            @block.scalar
            def _(act):
                act.activation(invt[:], core.row("log_temp"), ACT.Exp, scale=-1.0).then_inc(tscale, 1)
                with act.Fori(0, B // 2) as i:
                    for k in range(2):
                        act.wait_ge(xT_written, 2 * i + k + 3)
                        act.activation(xT[:, k, :], xTb[k][:, 0:DC * S], ACT.Copy).then_inc(xT_ready, 1)
                with act.Fori(0, SINKHORN) as i:
                    act.wait_ge(t_ready, 2 * i + 2)
                    act.activation(e[:], t[:], ACT.Exp).then_inc(e_ready, 1)
                    act.wait_ge(s_ready, 2 * i + 1)
                    act.activation(ln[:], s[:], ACT.Ln).then_inc(l_ready, 1)
                    act.wait_ge(row_ready, 3 * i + 2)
                    act.activation(v[:], u[:], ACT.Exp).then_inc(e_ready, 1)
                    act.wait_ge(s_ready, 2 * i + 2)
                    act.activation(ul[:], us[:], ACT.Ln).then_inc(l_ready, 1)
                act.wait_ge(row_ready, 3 * SINKHORN)
                act.activation(aff[:], u[:], ACT.Exp).then_inc(aff_ready, 1)

            @block.tensor
            def _(pe):
                ids, idn = core.ident[0:S, 0:S], core.ident[:]
                pe.sem_inc(xT_written, 2)
                pe.wait_ge(loaded, 16)
                with pe.Fori(0, B // 2) as i:
                    for k in range(2):
                        pe.wait_ge(normed, 2 * i + k + 1)
                        for c in range(DC):
                            last = pe.transpose(xTb[k][:, c * S:(c + 1) * S], xn[:, k, c * 128:(c + 1) * 128], ids)
                        last.then_inc(xT_written, 1)
                        pe.wait_ge(xT_ready, 2 * i + k + 1)
                        for c in range(DC):
                            last = pe.matmul(logits[0:S, bass.ds((2 * i + k) * E0, E0)], xT[:, k, c * S:(c + 1) * S],
                                             gq[:, c, :], start=(c == 0), stop=(c == DC - 1))
                        last.then_inc(logits_written, 1)
                with pe.Fori(0, SINKHORN) as i:
                    pe.wait_ge(row_ready, 3 * i + 1)
                    for c in range(2):
                        last = pe.transpose(by_row[0:HALF, c * S:(c + 1) * S], t[:, c * HALF:(c + 1) * HALF], ids)
                    last.then_inc(row_written, 1)
                    pe.wait_ge(row_ready, 3 * i + 3)
                    for c in range(2):
                        last = pe.transpose(by_token[0:S, c * HALF:(c + 1) * HALF], u[:, c, :], idn)
                    last.then_inc(token_written, 1)
                pe.wait_ge(aff_ready, 2)
                pe.wait_ge(t_ready, 2 * SINKHORN + 1)
                for c in range(2):
                    last = pe.transpose(by_token[0:S, c * HALF:(c + 1) * HALF], order[:, c, :], idn)
                last.then_inc(place_written, 1)
                for c in range(2):
                    last = pe.transpose(by_token2[0:S, c * HALF:(c + 1) * HALF], taken[:, c, :], idn)
                last.then_inc(place_written, 1)


def experts0_stage(core, keep):
    nc, inp = core.nc, core.inp
    FC = F0 // 128
    SLOTS = B * CAP
    NH = SLOTS // 512
    SEQH = B // NH
    NT = SLOTS // 128
    G = 2 * DC * NH
    with Stage(core, "ex0") as st:
        w1f = st.sb("w1f", [128, DC, F0])
        w2f = st.sb("w2f", [128, FC, D])
        w1 = st.sb("w1", [128, 2, 2, DC * F0], F16)
        w2 = st.sb("w2", [128, 2, 2, FC * D], F16)
        b1 = st.sb("b1", [128, 2, FC])
        b2 = st.sb("b2", [128, 2, D])
        pick = st.sb("pick", [S, B, CAP], F16)
        iota = st.sb("iota16", [S, CAP])
        pickT = st.sb("pickT", [128, NT * S], F16)
        identh = st.sb("identh", [S, S], F16)
        xT = st.sb("xT", [128, 2, DC, SLOTS], F16)
        h = st.sb("h", [128, 2, 512])
        hh = st.sb("hh", [128, 2, FC, SLOTS], F16)
        yf = st.sb("yf", [128, 2, D])
        y = st.sb("y", [128, 2, 2, D], F16)
        gat = [st.bank("gat0"), st.bank("gat1")]
        hid = [st.bank("hid0"), st.bank("hid1")]
        yb = [st.bank("y0"), st.bank("y1")]
        sc = [st.bank("sc0"), st.bank("sc1")]
        pTb = sc[0][:].bitcast(F16)
        (w_in, w_split, pick_ready, gat_written, xT0_ready, xT1_ready, picks_written, pickT_ready, hid_written,
         h_ready, hi_ready, lo_ready, y_written, yf_ready, yhi_ready, ylo_ready, sc_written, x_updated, const,
         held) = (st.sem(n) for n in
            "w_in w_split pick_ready gat_written xT0_ready xT1_ready picks_written pickT_ready hid_written "
            "h_ready hi_ready lo_ready y_written yf_ready yhi_ready ylo_ready sc_written x_updated const held".split())
        NJ = FC * NH

        with nc.Block() as block:

            @block.sync
            def _(sp):
                with sp.Fori(0, E0 // 2) as i:
                    for k in range(2):
                        e = bass.ds(2 * i + k, 1)
                        sp.wait_ge(w_split, 4 * (2 * i + k) + 4)
                        sp.dma_start(w1f[:], inp["w1"][e, :, :].rearrange("a (c p) f -> p (a c) f", p=128))\
                          .then_inc(w_in, 16)
                        sp.dma_start(w2f[:], inp["w2"][e, :, :].rearrange("a (c p) f -> p (a c) f", p=128))\
                          .then_inc(w_in, 16)
                        sp.wait_ge(x_updated, B * (2 * i + k) + 2)
                        sp.dma_start(b1[:, k, :], inp["b1"][e, :, :].rearrange("a p c -> p (a c)")).then_inc(w_in, 16)
                        sp.dma_start(b2[:, k, :], inp["b2"][e, :].broadcast_to([128, D])).then_inc(w_in, 16)

            @block.gpsimd
            def _(pool):
                pool.sem_inc(w_split, 4)
                with pool.Fori(0, E0 // 2) as i:
                    for k in range(2):
                        n = 4 * (2 * i + k) + 4
                        pool.wait_ge(w_in, 64 * (2 * i + k) + 64)
                        w1r, w2r = (w[:].rearrange("p c f -> p (c f)") for w in (w1f, w2f))
                        pool.sem_inc(held, 1)
                        pool.tensor_copy(w1[:, k, 0, :], w1r).then_inc(w_split, 1)
                        pool.tensor_copy(w2[:, k, 0, :], w2r).then_inc(w_split, 1)
                        pool.wait_ge(w_split, n + 2)
                        pool.tensor_tensor(w1[:, k, 1, :], w1r, w1[:, k, 0, :], ALU.subtract).then_inc(w_split, 1)
                        pool.tensor_tensor(w2[:, k, 1, :], w2r, w2[:, k, 0, :], ALU.subtract).then_inc(w_split, 1)

            @block.vector
            def _(dve):
                dve.tensor_copy(identh[:], core.ident[0:S, 0:S]).then_inc(const, 1)
                dve.tensor_copy(iota[:], core.row("iota")).then_inc(const, 1)
                dve.wait_ge(const, 2)
                dve.sem_inc(x_updated, B + 2)
                dve.sem_inc(lo_ready, 2)
                dve.sem_inc(yf_ready, 2)
                dve.sem_inc(ylo_ready, 2)
                with dve.Fori(0, E0 // 2) as i:
                    for k in range(2):
                        e = 2 * i + k
                        at = core.place[:].rearrange("p (b e) -> p b e", e=E0)[:, :, bass.ds(e, 1)]
                        dve.wait_ge(picks_written, e + 1)
                        dve.tensor_tensor(pick[:], widen(iota[:], 1, B), at.broadcast_to([S, B, CAP]), ALU.is_equal)\
                           .then_inc(pick_ready, 1)
                        for g in range(1, G, 2):
                            dve.wait_ge(gat_written, G * e + g + 1)
                            dve.tensor_copy(xT[:, g // (DC * NH), g // NH % DC, g % NH * 512:(g % NH + 1) * 512],
                                            gat[1][:]).then_inc(xT1_ready, 1)
                        for j in range(NJ):
                            f, n = j % FC, j // FC
                            at = slice(n * 512, (n + 1) * 512)
                            dve.wait_ge(hi_ready, NJ * e + j + 1)
                            dve.tensor_tensor(hh[:, 1, f, at], h[:, j % 2, :], hh[:, 0, f, at], ALU.subtract)\
                               .then_inc(lo_ready, 1)
                        for t in range(NT + 1):
                            if t < NT:
                                dve.wait_ge(y_written, NT * e + t + 1)
                                dve.wait_ge(ylo_ready, NT * e + t + 1)
                                dve.tensor_tensor(yf[:, t % 2, :], yb[t % 2][:, 0:D], b2[:, k, :], ALU.add)\
                                   .then_inc(yf_ready, 1)
                            if t >= 1:
                                for q in range(2):
                                    b = 2 * (t - 1) + q
                                    dve.wait_ge(sc_written, B * e + b + 4)
                                    dve.scalar_tensor_tensor(
                                        out=core.x[:, b, :], in0=sc[q][0:S, 0:D],
                                        scalar=core.gates[:, bass.ds(b * E0 + e, 1)], in1=core.x[:, b, :],
                                        op0=ALU.mult, op1=ALU.add).then_inc(x_updated, 1)
                            if t < NT:
                                dve.wait_ge(yhi_ready, NT * e + t + 1)
                                dve.tensor_tensor(y[:, t % 2, 1, :], yf[:, t % 2, :], y[:, t % 2, 0, :], ALU.subtract)\
                                   .then_inc(ylo_ready, 1)

            @block.scalar
            def _(act):
                act.sem_inc(h_ready, 2)
                with act.Fori(0, E0 // 2) as i:
                    for k in range(2):
                        e = 2 * i + k
                        for g in range(0, G, 2):
                            act.wait_ge(gat_written, G * e + g + 1)
                            act.activation(xT[:, g // (DC * NH), g // NH % DC, g % NH * 512:(g % NH + 1) * 512],
                                           gat[0][:], ACT.Copy).then_inc(xT0_ready, 1)
                        act.wait_ge(picks_written, e + 2)
                        act.activation(pickT[:], pTb[:, 0:NT * S], ACT.Copy).then_inc(pickT_ready, 1)
                        act.wait_ge(w_in, 64 * e + 64)
                        for j in range(NJ):
                            f, n = j % FC, j // FC
                            at = slice(n * 512, (n + 1) * 512)
                            act.wait_ge(hid_written, NJ * e + j + 1)
                            act.wait_ge(lo_ready, NJ * e + j + 1)
                            act.activation(h[:, j % 2, :], hid[j % 2][:], ACT.Gelu_apprx_tanh, bias=b1[:, k, f:f + 1])\
                               .then_inc(h_ready, 1)
                            act.wait_ge(h_ready, NJ * e + j + 3)
                            act.activation(hh[:, 0, f, at], h[:, j % 2, :], ACT.Copy).then_inc(hi_ready, 1)
                        for t in range(NT):
                            act.wait_ge(yf_ready, NT * e + t + 3)
                            act.wait_ge(sc_written, B * e + 2 * t + 1)
                            act.activation(y[:, t % 2, 0, :], yf[:, t % 2, :], ACT.Copy).then_inc(yhi_ready, 1)

            @block.tensor
            def _(pe):
                pe.sem_inc(picks_written, 1)
                pe.sem_inc(sc_written, 3)
                pe.wait_ge(const, 2)
                with pe.Fori(0, E0 // 2) as i:
                    for k in range(2):
                        e = 2 * i + k
                        pe.wait_ge(pick_ready, e + 1)
                        for g in range(G):
                            src = (core.norm_hi, core.norm_lo)[g // (DC * NH)]
                            c, n = g // NH % DC, g % NH
                            if g >= 2:
                                pe.wait_ge((xT0_ready, xT1_ready)[g % 2], G // 2 * e + g // 2)
                            for b in range(SEQH):
                                last = pe.matmul(gat[g % 2][:, b * CAP:(b + 1) * CAP],
                                                 src[:, n * SEQH + b, c * 128:(c + 1) * 128],
                                                 pick[:, n * SEQH + b, :], start=True, stop=True)
                            last.then_inc(gat_written, 1)
                        pe.wait_ge(x_updated, B * e + B + 2)
                        for t in range(NT):
                            last = pe.transpose(pTb[:, t * S:(t + 1) * S],
                                                pick[:, 2 * t:2 * t + 2, :].rearrange("p a c -> p (a c)"), identh[:])
                        last.then_inc(picks_written, 1)
                        pe.wait_ge(w_split, 4 * e + 8)
                        pe.wait_ge(xT0_ready, G // 2 * (e + 1))
                        pe.wait_ge(xT1_ready, G // 2 * (e + 1))
                        for j in range(NJ):
                            f, n = j % FC, j // FC
                            pe.wait_ge(h_ready, NJ * e + j + 1)
                            terms = [(c, a, z) for c in range(DC) for a, z in ((0, 0), (0, 1), (1, 0))]
                            for q, (c, a, z) in enumerate(terms):
                                last = pe.matmul(hid[j % 2][:], w1[:, k, a, c * F0 + f * 128:c * F0 + (f + 1) * 128],
                                                 xT[:, z, c, n * 512:(n + 1) * 512], start=(q == 0),
                                                 stop=(q == len(terms) - 1))
                            last.then_inc(hid_written, 1)
                        for t in range(NT + 1):
                            if t < NT:
                                pe.wait_ge(lo_ready, NJ * e + (FC if t < NT // NH else NJ) + 2)
                                pe.wait_ge(yf_ready, NT * e + t + 1)
                                terms = [(f, a, z) for f in range(FC) for a, z in ((0, 0), (0, 1), (1, 0))]
                                for q, (f, a, z) in enumerate(terms):
                                    last = pe.matmul(yb[t % 2][:, 0:D], hh[:, a, f, t * 128:(t + 1) * 128],
                                                     w2[:, k, z, f * D:(f + 1) * D], start=(q == 0),
                                                     stop=(q == len(terms) - 1))
                                last.then_inc(y_written, 1)
                            if t >= 1:
                                pe.wait_ge(ylo_ready, NT * e + t + 2)
                                if t == 1:
                                    pe.wait_ge(pickT_ready, e + 1)
                                for q in range(2):
                                    pe.wait_ge(x_updated, B * e + B + 2 * (t - 1) + q + 1)
                                    for z in range(2):
                                        last = pe.matmul(sc[q][0:S, 0:D],
                                                         pickT[CAP * q:CAP * (q + 1), (t - 1) * S:t * S],
                                                         y[CAP * q:CAP * (q + 1), (t - 1) % 2, z, :],
                                                         start=(z == 0), stop=(z == 1))
                                    last.then_inc(sc_written, 1)


def l1_xattn_stage(core, keep):
    nc, inp = core.nc, core.inp
    NC = H1 // HG
    with Stage(core, "xa1") as st:
        mean, ve, rstd = (st.sb(n, [S, B]) for n in ("mean", "ve", "rstd"))
        stats_stage(core, "xa1_s", core.x, S, B, mean[:], ve[:], rstd[:])
        wq = st.sb("wq", [128, DC, H1 * PAD])
        wk = st.sb("wk", [CF, 2, H1 * PAD])
        wv = st.sb("wv", [CF, 2, D])
        wo = st.sb("wo", [128, DC, D])
        bo = st.sb("bo", [S, D])
        bq = st.sb("bq", [128, NC])
        cx = st.sb("cx", [CP, CT, CD])
        xn = st.sb("xn", [S, D])
        xT = st.sb("xT", [128, DC, S])
        cT = st.sb("cT", [CF, 2, C])
        qT = st.sb("qT", [128, NC, S])
        kT = st.sb("kT", [128, NC, C])
        v = st.sb("v", [CP, CT, D])
        top = st.sb("top", [S, H1])
        probs = st.sb("probs", [S, 2, C])
        total, rtotal = st.sb("total", [S, H1]), st.sb("rtotal", [S, H1])
        pT = st.sb("pT", [CP, 2, CT * S])
        heads = st.sb("heads", [S, D])
        headsT = st.sb("headsT", [128, DC, S])
        add = st.sb("add", [S, D])
        front = [st.bank("front0"), st.bank("front1")]
        score = [st.bank("score0"), st.bank("score1")]
        ptb = [st.bank("pt0"), st.bank("pt1")]
        outb, projb = st.bank("outb"), st.bank("projb")
        (loaded, cx_in, ready_once, normed, cT_written, cT_ready, xT_written, xT_ready, q_written, qT_ready, k_written,
         kT_ready, v_written, v_ready, score_written, top_ready, probs_ready, pT_written, pT_ready, out_written,
         heads_ready, headsT_written, headsT_ready, wo_written, x_updated) = (st.sem(n) for n in
            "loaded cx_in ready_once normed cT_written cT_ready xT_written xT_ready q_written qT_ready k_written "
            "kT_ready v_written v_ready score_written top_ready probs_ready pT_written pT_ready out_written "
            "heads_ready headsT_written headsT_ready wo_written x_updated".split())
        with nc.Block() as block:

            @block.sync
            def _(sp):
                sp.dma_start(wq[:], inp["w1q"].rearrange("(c p) n -> p c n", p=128)).then_inc(loaded, 16)
                sp.dma_start(wk[:], inp["w1k"].rearrange("(c p) n -> p c n", p=CF)).then_inc(loaded, 16)
                sp.dma_start(wv[:], inp["w1v"].rearrange("(c p) n -> p c n", p=CF)).then_inc(loaded, 16)
                sp.dma_start(wo[:], inp["w1o"].rearrange("(c p) n -> p c n", p=128)).then_inc(loaded, 16)
                sp.wait_ge(loaded, 64)
                with sp.Fori(0, B) as b:
                    sp.wait_ge(cT_written, 2 * b + 2)
                    sp.dma_start(cx[:], inp["ctx"][bass.ds(b, 1), :, :].rearrange("a (t p) d -> p (a t) d", p=CP))\
                      .then_inc(cx_in, 16)

            @block.vector
            def _(dve):
                dve.tensor_scalar(bo[:], core.row("bo1"), core.gate[0:S, 1:2], None, ALU.mult).then_inc(ready_once, 1)
                dve.tensor_scalar(bq[:], core.col("bq", n=NC), HD1 ** -0.5, None, ALU.mult).then_inc(ready_once, 1)
                dve.wait_ge(ready_once, 2)
                with dve.Fori(0, B) as b:
                    xb = core.x[:, bass.ds(b, 1), :].rearrange("p a c -> p (a c)")
                    dve.tensor_scalar(xn[:], xb, mean[:, bass.ds(b, 1)], rstd[:, bass.ds(b, 1)],
                                      ALU.subtract, ALU.mult).then_inc(normed, 1)
                    dve.wait_ge(q_written, b + 1)
                    dve.scalar_tensor_tensor(out=qT[:], in0=projb[:, 0:NC * S].rearrange("p (c s) -> p c s", c=NC),
                                             scalar=HD1 ** -0.5, in1=widen(bq[:], 2, S), op0=ALU.mult,
                                             op1=ALU.add).then_inc(qT_ready, 1)

                    def maximum(h):
                        dve.wait_ge(score_written, H1 * b + h + 1)
                        dve.tensor_reduce(top[:, h:h + 1], score[h % 2][0:S, 0:C], AX.X, ALU.max, negate=True)\
                           .then_inc(top_ready, 1)

                    maximum(0)
                    maximum(1)
                    for h in range(H1):
                        dve.wait_ge(pT_written, H1 * b + h + 1)
                        dve.tensor_copy(pT[:, h % 2, :], ptb[h % 2][0:CP, 0:CT * S]).then_inc(pT_ready, 1)
                        if h + 2 < H1:
                            maximum(h + 2)
                    dve.wait_ge(probs_ready, H1 * (b + 1))
                    dve.reciprocal(rtotal[:], total[:]).then_inc(heads_ready, 1)
                    dve.wait_ge(heads_ready, 3 * b + 1)
                    dve.wait_ge(out_written, b + 1)
                    dve.tensor_tensor(heads[:].rearrange("p (h d) -> p h d", h=H1),
                                      outb[0:S, 0:D].rearrange("p (h d) -> p h d", h=H1),
                                      widen(rtotal[:], 2, HD1), ALU.mult).then_inc(heads_ready, 1)
                    dve.wait_ge(heads_ready, 3 * b + 2)
                    dve.tensor_tensor(heads[:], heads[:], core.row("bv1"), ALU.add).then_inc(heads_ready, 1)
                    dve.wait_ge(wo_written, b + 1)
                    dve.scalar_tensor_tensor(out=add[:], in0=projb[0:S, 0:D], scalar=core.gate[0:S, 1:2],
                                             in1=bo[:], op0=ALU.mult, op1=ALU.add).then_inc(x_updated, 1)
                    dve.wait_ge(x_updated, 2 * b + 1)
                    dve.tensor_tensor(xb, xb, add[:], ALU.add).then_inc(x_updated, 1)

            @block.scalar
            def _(act):
                act.wait_ge(ready_once, 2)
                with act.Fori(0, B) as b:
                    for c in range(2):
                        act.wait_ge(cT_written, 2 * b + c + 3)
                        act.activation(cT[:, c, :], front[c][0:CF, 0:C], ACT.Copy).then_inc(cT_ready, 1)
                    act.wait_ge(xT_written, b + 1)
                    act.activation(xT[:].rearrange("p c s -> p (c s)"), projb[:, 0:DC * S], ACT.Copy)\
                       .then_inc(xT_ready, 1)
                    for j in range(NC):
                        act.wait_ge(k_written, NC * b + j + 1)
                        act.activation(kT[:, j, :], front[j % 2][:, 0:C], ACT.Identity, bias=core.col("bk", j))\
                           .then_inc(kT_ready, 1)
                    for t in range(CT):
                        act.wait_ge(v_written, CT * b + t + 1)
                        act.activation(v[:, t, :], front[t % 2][0:CP, 0:D], ACT.Copy).then_inc(v_ready, 1)
                    for h in range(H1):
                        act.wait_ge(top_ready, H1 * b + h + 1)
                        if h >= 2:
                            act.wait_ge(pT_written, H1 * b + h - 1)
                        act.activation(probs[:, h % 2, :], score[h % 2][0:S, 0:C], ACT.Exp,
                                       bias=top[:, h:h + 1], accum_out=total[:, h:h + 1]).then_inc(probs_ready, 1)
                    act.wait_ge(headsT_written, b + 1)
                    act.activation(headsT[:].rearrange("p c s -> p (c s)"), front[0][:, 0:DC * S], ACT.Copy)\
                       .then_inc(headsT_ready, 1)

            @block.tensor
            def _(pe):
                idc, ids = core.ident[0:CP, 0:CP], core.ident[0:S, 0:S]
                pe.wait_ge(loaded, 64)
                pe.sem_inc(cT_written, 2)
                with pe.Fori(0, B) as b:
                    pe.wait_ge(cx_in, 16 * b + 16)
                    for c in range(2):
                        for t in range(CT):
                            last = pe.transpose(front[c][0:CF, t * CP:(t + 1) * CP], cx[:, t, c * CF:(c + 1) * CF], idc)
                        last.then_inc(cT_written, 1)
                    pe.wait_ge(normed, b + 1)
                    for c in range(DC):
                        last = pe.transpose(projb[:, c * S:(c + 1) * S], xn[:, c * 128:(c + 1) * 128], ids)
                    last.then_inc(xT_written, 1)
                    pe.wait_ge(cT_ready, 2 * b + 2)
                    for j in range(NC):
                        if j >= 2:
                            pe.wait_ge(kT_ready, NC * b + j - 1)
                        for c in range(2):
                            last = pe.matmul(front[j % 2][:, 0:C], wk[:, c, j * 128:(j + 1) * 128], cT[:, c, :],
                                             start=(c == 0), stop=(c == 1))
                        last.then_inc(k_written, 1)
                    pe.wait_ge(xT_ready, b + 1)
                    for j in range(NC):
                        for c in range(DC):
                            last = pe.matmul(projb[:, j * S:(j + 1) * S], wq[:, c, j * 128:(j + 1) * 128], xT[:, c, :],
                                             start=(c == 0), stop=(c == DC - 1))
                    last.then_inc(q_written, 1)
                    for t in range(CT):
                        if t < 2:
                            pe.wait_ge(kT_ready, NC * b + NC - 1 + t)
                        else:
                            pe.wait_ge(v_ready, CT * b + t - 1)
                        for c in range(2):
                            last = pe.matmul(front[t % 2][0:CP, 0:D], cT[:, c, t * CP:(t + 1) * CP], wv[:, c, :],
                                             start=(c == 0), stop=(c == 1))
                        last.then_inc(v_written, 1)
                    pe.wait_ge(qT_ready, b + 1)

                    def score_head(h):
                        if h >= 2:
                            pe.wait_ge(probs_ready, H1 * b + h - 1)
                        r = PAD * (h % HG)
                        pe.matmul(score[h % 2][0:S, 0:C], qT[r:r + HD1, h // HG, :], kT[r:r + HD1, h // HG, :],
                                  start=True, stop=True, tile_position=(r, 0)).then_inc(score_written, 1)

                    score_head(0)
                    score_head(1)
                    for h in range(H1 + 1):
                        if h < H1:
                            pe.wait_ge(probs_ready, H1 * b + h + 1)
                            for t in range(CT):
                                last = pe.transpose(ptb[h % 2][0:CP, t * S:(t + 1) * S],
                                                    probs[:, h % 2, t * CP:(t + 1) * CP], ids)
                            last.then_inc(pT_written, 1)
                            if h + 2 < H1:
                                score_head(h + 2)
                        if h >= 1:
                            pe.wait_ge(pT_ready, H1 * b + h)
                            if h == 1:
                                pe.wait_ge(v_ready, CT * (b + 1))
                            g = h - 1
                            for t in range(CT):
                                last = pe.matmul(outb[0:S, g * HD1:(g + 1) * HD1], pT[:, g % 2, t * S:(t + 1) * S],
                                                 v[:, t, g * HD1:(g + 1) * HD1], start=(t == 0), stop=(t == CT - 1))
                    last.then_inc(out_written, 1)
                    pe.wait_ge(heads_ready, 3 * b + 3)
                    for c in range(DC):
                        last = pe.transpose(front[0][:, c * S:(c + 1) * S], heads[:, c * 128:(c + 1) * 128], ids)
                    last.then_inc(headsT_written, 1)
                    pe.wait_ge(headsT_ready, b + 1)
                    for c in range(DC):
                        last = pe.matmul(projb[0:S, 0:D], headsT[:, c, :], wo[:, c, :], start=(c == 0),
                                         stop=(c == DC - 1))
                    last.then_inc(wo_written, 1)


def l1_self_attn_stage(core, keep):
    nc, inp = core.nc, core.inp
    NC = H1 // HG
    core.base = keep("base", [S, B, D])
    core.hT = keep("hT", [128, 2, DC, B * S], F16)
    core.logits = keep("logits", [S, B, E1])
    with Stage(core, "sa") as st:
        mean, ve, rstd, ms, rms = (st.sb(n, [S, B]) for n in ("mean", "ve", "rstd", "ms", "rms"))
        stats_stage(core, "sa_s", core.x, S, B, mean[:], ve[:], rstd[:])
        wqk = st.sb("wqk", [128, DC, 2 * D])
        wv = st.sb("wv", [128, DC, D])
        wo = st.sb("wo", [128, DC, D])
        router = st.sb("router", [128, DC, E1])
        freqs = st.sb("freqs", [S, HD1])
        cosr, sinr = st.sb("cosr", [S, HD1]), st.sb("sinr", [S, HD1])
        causal = st.sb("causal", [S, S])
        xr = st.sb("xr", [S, D])
        xT = st.sb("xT", [128, DC, S])
        t1, t2 = st.sb("t1", [S, 2 * D]), st.sb("t2", [S, 2 * D])
        qk = st.sb("qk", [S, 2 * H1, PAD])
        qkT = st.sb("qkT", [128, 2 * NC, S])
        v = st.sb("v", [S, D])
        sm = st.sb("sm", [S, H1, S])
        top = st.sb("top", [S, H1])
        probs = st.sb("probs", [S, H1, S])
        total, rtotal = st.sb("total", [S, H1]), st.sb("rtotal", [S, H1])
        pT = st.sb("pT", [S, NC, HG * S])
        heads = st.sb("heads", [S, D])
        headsT = st.sb("headsT", [128, DC, S])
        sq = st.sb("sq", [S, D])
        hss, hrr = st.sb("hss", [S, 1]), st.sb("hrr", [S, 1])
        n, h = st.sb("n", [S, D]), st.sb("h", [S, D])
        hn = st.sb("hn", [S, D])
        hTf = st.sb("hTf", [128, DC, S])
        big = [st.bank(f"big{r}") for r in range(HG)]
        pa, pb, po, pr = st.bank("pa"), st.bank("pb"), st.bank("po"), st.bank("pr")
        (loaded, ready_once, xr_ready, xT_written, xT_ready, qk_written, qk_step, qk_ready, v_written, v_ready,
         qkT_written, qkT_ready, score_written, sm_ready, top_ready, probs_ready, pT_written, pT_ready, out_written,
         heads_ready, headsT_written, headsT_ready, wo_written, h_ready, hss_ready, hrr_ready, hn_ready, hnT_written,
         hTf_ready, hTh_ready, router_written, dve_step, hT_kept, held) = (st.sem(n) for n in
            "loaded ready_once xr_ready xT_written xT_ready qk_written qk_step qk_ready v_written v_ready "
            "qkT_written qkT_ready score_written sm_ready top_ready probs_ready pT_written pT_ready out_written "
            "heads_ready headsT_written headsT_ready wo_written h_ready hss_ready hrr_ready hn_ready hnT_written "
            "hTf_ready hTh_ready router_written dve_step hT_kept held".split())
        with nc.Block() as block:

            @block.sync
            def _(sp):
                for dst, src in ((wqk, "s_wqk"), (wv, "s_wv"), (wo, "s_wo"), (router, "router")):
                    sp.dma_start(dst[:], inp[src].rearrange("(c p) n -> p c n", p=128)).then_inc(loaded, 16)
                sp.dma_start(freqs[:], inp["freqs"][0:S, :]).then_inc(loaded, 16)
                sp.dma_start(causal[:], inp["causal"]).then_inc(loaded, 16)
                sp.wait_ge(loaded, 96)

            @block.vector
            def _(dve):
                step = Chain(dve, dve_step)
                dve.wait_ge(loaded, 96)
                pair = lambda a: a[:].rearrange("p (k two) -> p k two", two=2)
                cos, sin = pair(freqs)[:, :, 0:1], pair(freqs)[:, :, 1:2]
                step(dve.tensor_copy(pair(cosr), cos.broadcast_to([S, HD1 // 2, 2])))
                step(dve.tensor_scalar(pair(sinr)[:, :, 0:1], sin, -1.0, None, ALU.mult))
                step(dve.tensor_copy(pair(sinr)[:, :, 1:2], sin))
                step(dve.memset(qk[:], 0.0))
                step(dve.tensor_scalar(ms[:], ve[:], -LN_EPS, None, ALU.add))
                step(dve.tensor_tensor(ms[:], ms[:], rstd[:], ALU.mult))
                step(dve.tensor_tensor(ms[:], ms[:], rstd[:], ALU.mult))
                dve.tensor_scalar(ms[:], ms[:], RMS_EPS, None, ALU.add).then_inc(ready_once, 1)
                dve.wait_ge(ready_once, 2)
                fixed = step.n
                PER = 1
                with dve.Fori(0, B) as b:
                    step = Chain(dve, dve_step, PER * b + fixed)
                    xb = core.x[:, bass.ds(b, 1), :].rearrange("p a c -> p (a c)")
                    nb = core.base[:, bass.ds(b, 1), :].rearrange("p a c -> p (a c)")
                    step(dve.tensor_scalar(n[:], xb, mean[:, bass.ds(b, 1)], rstd[:, bass.ds(b, 1)],
                                           ALU.subtract, ALU.mult))
                    dve.tensor_scalar(xr[:], n[:], rms[:, bass.ds(b, 1)], None, ALU.mult).then_inc(xr_ready, 1)
                    dve.wait_ge(qk_written, b + 1)
                    src = pa[0:S, :].rearrange("p (h d) -> p h d", d=HD1)
                    src2 = pa[0:S, :].rearrange("p (h k two) -> p h k two", k=HD1 // 2, two=2)
                    rot = t2[:].rearrange("p (h k two) -> p h k two", k=HD1 // 2, two=2)
                    s2 = pair(sinr)
                    dve.tensor_tensor(t1[:].rearrange("p (h d) -> p h d", d=HD1), src,
                                      widen(cosr[:], 1, 2 * H1), ALU.mult).then_inc(qk_step, 1)
                    for z in range(2):
                        dve.tensor_tensor(rot[:, :, :, z], src2[:, :, :, 1 - z], widen(s2[:, :, z], 1, 2 * H1),
                                          ALU.mult).then_inc(qk_step, 1)
                    dve.wait_ge(qk_step, 3 * b + 3)
                    dve.tensor_tensor(qk[:, :, 0:HD1], t1[:].rearrange("p (h d) -> p h d", d=HD1),
                                      t2[:].rearrange("p (h d) -> p h d", d=HD1), ALU.add).then_inc(qk_ready, 1)
                    for r in range(HG):
                        dve.wait_ge(score_written, HG * b + r + 1)
                        dve.scalar_tensor_tensor(out=sm[:, r * NC:(r + 1) * NC, :],
                                                 in0=big[r][0:S, 0:NC * S].rearrange("p (j s) -> p j s", j=NC),
                                                 scalar=HD1 ** -0.5, in1=widen(causal[:], 1, NC), op0=ALU.mult,
                                                 op1=ALU.add).then_inc(sm_ready, 1)
                    for r in range(HG):
                        dve.wait_ge(sm_ready, HG * b + r + 1)
                        dve.tensor_reduce(top[:, r * NC:(r + 1) * NC], sm[:, r * NC:(r + 1) * NC, :], AX.X, ALU.max,
                                          negate=True).then_inc(top_ready, 1)
                    for r in range(HG):
                        dve.wait_ge(pT_written, HG * b + r + 1)
                        dve.tensor_copy(pT[:, r, :], big[r][0:S, 0:NC * S]).then_inc(pT_ready, 1)
                    dve.reciprocal(rtotal[:], total[:]).then_inc(heads_ready, 1)
                    dve.wait_ge(heads_ready, 2 * b + 1)
                    dve.wait_ge(out_written, b + 1)
                    dve.tensor_tensor(heads[:].rearrange("p (j r d) -> p r j d", r=HG, d=HD1),
                                      po[0:S, 0:D].rearrange("p (r j d) -> p r j d", r=HG, d=HD1),
                                      widen(rtotal[:].rearrange("p (r j) -> p r j", r=HG), 3, HD1), ALU.mult)\
                       .then_inc(heads_ready, 1)
                    dve.wait_ge(wo_written, b + 1)
                    dve.tensor_tensor(h[:], n[:], pb[0:S, 0:D], ALU.add).then_inc(h_ready, 1)
                    dve.wait_ge(h_ready, b + 1)
                    dve.sem_inc(held, 1)
                    dve.tensor_tensor_reduce(out=sq[:], in0=h[:], in1=h[:], scale=1.0, scalar=0.0, op0=ALU.mult,
                                             op1=ALU.add, accum_out=hss[:]).then_inc(hss_ready, 1)
                    dve.wait_ge(hss_ready, 2 * b + 1)
                    dve.tensor_scalar(hss[:], hss[:], 1.0 / D, RMS_EPS, ALU.mult, ALU.add).then_inc(hss_ready, 1)
                    dve.wait_ge(hrr_ready, b + 1)
                    dve.tensor_scalar(nb, h[:], 1.0, None, ALU.mult)
                    dve.tensor_scalar(hn[:], h[:], hrr[:], None, ALU.mult).then_inc(hn_ready, 1)
                    dve.wait_ge(hTf_ready, 2 * b + 2)
                    hi, lo = (core.hT[:, z, :, bass.ds(b * S, S)] for z in range(2))
                    dve.tensor_scalar(hi, hTf[:], 1.0, None, ALU.mult).then_inc(hTh_ready, 1)
                    dve.wait_ge(hTh_ready, b + 1)
                    dve.tensor_tensor(lo, hTf[:], hi, ALU.subtract).then_inc(hT_kept, 1)
                    dve.wait_ge(router_written, b + 1)
                    dve.tensor_scalar(core.logits[:, bass.ds(b, 1), :].rearrange("p a e -> p (a e)"), pr[0:S, 0:E1],
                                      1.0, None, ALU.mult).then_inc(hT_kept, 1)
                    assert step.n == PER

            @block.gpsimd
            def _(pool):
                pool.wait_ge(ready_once, 1)
                pool.tensor_tensor(rms[:], ms[:], core.half[0:S, 0:B], ALU.pow).then_inc(ready_once, 1)
                with pool.Fori(0, B) as b:
                    pool.wait_ge(hss_ready, 2 * b + 2)
                    pool.tensor_tensor(hrr[:], hss[:], core.half[0:S, 0:1], ALU.pow).then_inc(hrr_ready, 1)

            @block.scalar
            def _(act):
                with act.Fori(0, B) as b:
                    act.wait_ge(xT_written, b + 1)
                    for c in range(DC):
                        act.activation(xT[:, c, :], pb[:, c * S:(c + 1) * S], ACT.Copy, scale=core.col("attn_w", c))\
                           .then_inc(xT_ready, 1)
                    act.wait_ge(v_written, b + 1)
                    act.activation(v[:], pb[0:S, 0:D], ACT.Copy).then_inc(v_ready, 1)
                    for c in range(2):
                        act.wait_ge(qkT_written, 2 * b + c + 1)
                        act.activation(qkT[:, c * NC:(c + 1) * NC, :].rearrange("p c s -> p (c s)"),
                                       (pb, pr)[c][:, 0:NC * S], ACT.Copy).then_inc(qkT_ready, 1)
                    for h in range(H1):
                        act.wait_ge(top_ready, HG * b + h // NC + 1)
                        act.activation(probs[:, h, :], sm[:, h, :], ACT.Exp, bias=top[:, h:h + 1],
                                       accum_out=total[:, h:h + 1]).then_inc(probs_ready, 1)
                    act.wait_ge(headsT_written, b + 1)
                    act.activation(headsT[:].rearrange("p c s -> p (c s)"), pa[:, 0:DC * S], ACT.Copy)\
                       .then_inc(headsT_ready, 1)
                    act.wait_ge(hnT_written, b + 1)
                    for c in range(DC):
                        act.activation(hTf[:, c, :], pa[:, c * S:(c + 1) * S], ACT.Copy, scale=core.col("ffn_w", c))\
                           .then_inc(hTf_ready, 1)

            @block.tensor
            def _(pe):
                ids = core.ident[0:S, 0:S]
                pe.wait_ge(loaded, 96)
                pe.sem_inc(hT_kept, 1)
                with pe.Fori(0, B) as b:
                    pe.wait_ge(xr_ready, b + 1)
                    for c in range(DC):
                        last = pe.transpose(pb[:, c * S:(c + 1) * S], xr[:, c * 128:(c + 1) * 128], ids)
                    last.then_inc(xT_written, 1)
                    pe.wait_ge(xT_ready, 2 * b + 2)
                    for c in range(DC):
                        last = pe.matmul(pa[0:S, :], xT[:, c, :], wqk[:, c, :], start=(c == 0), stop=(c == DC - 1))
                    last.then_inc(qk_written, 1)
                    for c in range(DC):
                        last = pe.matmul(pb[0:S, 0:D], xT[:, c, :], wv[:, c, :], start=(c == 0), stop=(c == DC - 1))
                    last.then_inc(v_written, 1)
                    pe.wait_ge(qk_ready, b + 1)
                    pe.wait_ge(v_ready, b + 1)
                    pe.wait_ge(hT_kept, 2 * b + 1)
                    for c in range(2):
                        for j in range(NC):
                            q = c * NC + j
                            last = pe.transpose((pb, pr)[c][:, j * S:(j + 1) * S],
                                                qk[:, q * HG:(q + 1) * HG, :].rearrange("p h d -> p (h d)"), ids)
                        last.then_inc(qkT_written, 1)
                    pe.wait_ge(qkT_ready, 2 * b + 2)
                    for r in range(HG):
                        at = slice(PAD * r, PAD * r + HD1)
                        for j in range(NC):
                            last = pe.matmul(big[r][0:S, j * S:(j + 1) * S], qkT[at, j, :], qkT[at, NC + j, :],
                                             start=True, stop=True, tile_position=(PAD * r, 0))
                        last.then_inc(score_written, 1)
                    for r in range(HG):
                        pe.wait_ge(probs_ready, H1 * b + NC * (r + 1))
                        for j in range(NC):
                            last = pe.transpose(big[r][0:S, j * S:(j + 1) * S], probs[:, r * NC + j, :], ids)
                        last.then_inc(pT_written, 1)
                    for r in range(HG):
                        pe.wait_ge(pT_ready, HG * b + r + 1)
                        for j in range(NC):
                            h = HG * j + r
                            o = (r * NC + j) * HD1
                            last = pe.matmul(po[0:S, o:o + HD1], pT[:, r, j * S:(j + 1) * S],
                                             v[:, h * HD1:(h + 1) * HD1], start=True, stop=True)
                    last.then_inc(out_written, 1)
                    pe.wait_ge(heads_ready, 2 * b + 2)
                    for c in range(DC):
                        last = pe.transpose(pa[:, c * S:(c + 1) * S], heads[:, c * 128:(c + 1) * 128], ids)
                    last.then_inc(headsT_written, 1)
                    pe.wait_ge(headsT_ready, b + 1)
                    for c in range(DC):
                        last = pe.matmul(pb[0:S, 0:D], headsT[:, c, :], wo[:, c, :], start=(c == 0), stop=(c == DC - 1))
                    last.then_inc(wo_written, 1)
                    pe.wait_ge(hn_ready, b + 1)
                    for c in range(DC):
                        last = pe.transpose(pa[:, c * S:(c + 1) * S], hn[:, c * 128:(c + 1) * 128], ids)
                    last.then_inc(hnT_written, 1)
                    pe.wait_ge(hTf_ready, 2 * b + 2)
                    for c in range(DC):
                        last = pe.matmul(pr[0:S, 0:E1], hTf[:, c, :], router[:, c, :], start=(c == 0),
                                         stop=(c == DC - 1))
                    last.then_inc(router_written, 1)


def experts1_stage(core, keep):
    nc, inp = core.nc, core.inp
    FC = F1 // 128
    SEQ = 4
    NB = B // SEQ
    W = SEQ * S
    NJ = FC * NB
    with Stage(core, "ex1") as st:
        combine = st.sb("combine", [S, B, E1])
        l2, eq, run, sel = (st.sb(n, [S, B, E1]) for n in ("l2", "eq", "run", "sel"))
        mx, tot = st.sb("mx", [S, B]), st.sb("tot", [S, B])
        wf = [st.sb("w1f", [128, DC * F1]), st.sb("w3f", [128, DC * F1]), st.sb("w2f", [128, FC * D])]
        w = [st.sb(n, [128, 2, 2, 1024], F16) for n in ("w1", "w3", "w2")]
        g = st.sb("g", [128, 2, W])
        p = st.sb("p", [128, 2, W])
        ph = st.sb("ph", [128, 2, FC, B * S], F16)
        ub = [st.bank("u0"), st.bank("u1")]
        zb = [st.bank("z0"), st.bank("z1")]
        yb = [st.bank(f"y{n}") for n in range(4)]
        (w_in, w_split, u_written, z_written, g_ready, p_ready, ph_ready, pl_ready, y_written, x_updated, dve_step,
         exp_ready, diff_ready, held) = (st.sem(n) for n in
            "w_in w_split u_written z_written g_ready p_ready ph_ready pl_ready y_written x_updated dve_step "
            "exp_ready diff_ready held".split())
        with nc.Block() as block:

            @block.sync
            def _(sp):
                with sp.Fori(0, E1 // 2) as i:
                    for k in range(2):
                        e = 2 * i + k
                        sp.wait_ge(w_split, 6 * e + 6)
                        sp.wait_ge(x_updated, B * e + 4)
                        for dst, name in zip(wf, ("m_w1", "m_w3", "m_w2")):
                            sp.dma_start(dst[:].rearrange("p (c f) -> p c f", f=F1 if name != "m_w2" else D),
                                         inp[name][bass.ds(e, 1), :, :].rearrange("a (c p) f -> p (a c) f", p=128))\
                              .then_inc(w_in, 16)

            @block.gpsimd
            def _(pool):
                pool.sem_inc(w_split, 6)
                with pool.Fori(0, E1 // 2) as i:
                    for k in range(2):
                        e = 2 * i + k
                        pool.wait_ge(w_in, 48 * e + 48)
                        pool.sem_inc(held, 1)
                        for n in range(3):
                            pool.tensor_copy(w[n][:, k, 0, :], wf[n][:]).then_inc(w_split, 1)
                        pool.wait_ge(w_split, 6 * e + 9)
                        for n in range(3):
                            pool.tensor_tensor(w[n][:, k, 1, :], wf[n][:], w[n][:, k, 0, :], ALU.subtract)\
                                .then_inc(w_split, 1)

            @block.vector
            def _(dve):
                dve.sem_inc(x_updated, B + 4)
                dve.sem_inc(p_ready, 2)
                dve.sem_inc(pl_ready, 2)
                step = Chain(dve, dve_step)
                step(dve.tensor_reduce(mx[:], core.logits[:], AX.X, ALU.max))
                dve.tensor_tensor(l2[:], core.logits[:], widen(mx[:], 2, E1), ALU.subtract).then_inc(diff_ready, 1)
                dve.wait_ge(diff_ready, 1)
                step(dve.memset(sel[:], 0.0))
                for n in range(TOP):
                    step(dve.tensor_reduce(mx[:], l2[:], AX.X, ALU.max))
                    step(dve.tensor_tensor(eq[:], l2[:], widen(mx[:], 2, E1), ALU.is_equal))
                    step(dve.tensor_copy(run[:, :, 0:1], eq[:, :, 0:1]))
                    for c in range(1, E1):
                        step(dve.tensor_tensor(run[:, :, c:c + 1], run[:, :, c - 1:c], eq[:, :, c:c + 1], ALU.add))
                    step(dve.tensor_scalar(run[:], run[:], 1.0, None, ALU.is_equal))
                    step(dve.tensor_tensor(eq[:], eq[:], run[:], ALU.mult))
                    step(dve.tensor_tensor(sel[:], sel[:], eq[:], ALU.add))
                    if n == 0:
                        dve.wait_ge(exp_ready, 1)
                    step(dve.scalar_tensor_tensor(out=l2[:], in0=eq[:], scalar=-MASKED, in1=l2[:], op0=ALU.mult,
                                                  op1=ALU.add))
                step(dve.tensor_tensor(combine[:], combine[:], sel[:], ALU.mult))
                step(dve.tensor_reduce(tot[:], combine[:], AX.X, ALU.add))
                step(dve.reciprocal(tot[:], tot[:]))
                step(dve.tensor_scalar(tot[:], tot[:], core.gate[0:S, 3:4], None, ALU.mult))
                step(dve.tensor_tensor(combine[:], combine[:], widen(tot[:], 2, E1), ALU.mult))
                step(dve.scalar_tensor_tensor(out=core.x[:], in0=core.base[:], scalar=core.gate[0:S, 3:4],
                                              in1=core.x[:], op0=ALU.mult, op1=ALU.add))
                with dve.Fori(0, E1 // 2) as i:
                    for k in range(2):
                        e = 2 * i + k

                        def low_half(j):
                            f, n = j % FC, j // FC
                            at = slice(n * W, (n + 1) * W)
                            dve.wait_ge(ph_ready, NJ * e + j + 1)
                            dve.tensor_tensor(ph[:, 1, f, at], p[:, j % 2, :], ph[:, 0, f, at], ALU.subtract)\
                               .then_inc(pl_ready, 1)

                        for j in range(NJ):
                            dve.wait_ge(z_written, NJ * e + j + 1)
                            dve.wait_ge(g_ready, NJ * e + j + 3)
                            dve.wait_ge(pl_ready, NJ * e + j + 1)
                            dve.tensor_tensor(p[:, j % 2, :], zb[j % 2][:, 0:W], g[:, j % 2, :], ALU.mult)\
                               .then_inc(p_ready, 1)
                            if j >= 1:
                                low_half(j - 1)
                        low_half(NJ - 1)
                        for b in range(B):
                            dve.wait_ge(y_written, B * e + b + 1)
                            dve.scalar_tensor_tensor(
                                out=core.x[:, b, :], in0=yb[b % 4][0:S, 0:D],
                                scalar=combine[:, b, :][:, bass.ds(e, 1)], in1=core.x[:, b, :],
                                op0=ALU.mult, op1=ALU.add).then_inc(x_updated, 1)

            @block.scalar
            def _(act):
                act.sem_inc(g_ready, 2)
                act.wait_ge(diff_ready, 1)
                act.activation(combine[:], l2[:], ACT.Exp).then_inc(exp_ready, 1)
                with act.Fori(0, E1 // 2) as i:
                    for k in range(2):
                        e = 2 * i + k

                        def silu(j):
                            act.wait_ge(u_written, NJ * e + j + 1)
                            act.wait_ge(p_ready, NJ * e + j + 1)
                            act.activation(g[:, j % 2, :], ub[j % 2][:, 0:W], ACT.Silu).then_inc(g_ready, 1)

                        silu(0)
                        for j in range(NJ):
                            if j + 1 < NJ:
                                silu(j + 1)
                            f, n = j % FC, j // FC
                            act.wait_ge(p_ready, NJ * e + j + 3)
                            act.activation(ph[:, 0, f, n * W:(n + 1) * W], p[:, j % 2, :], ACT.Copy)\
                               .then_inc(ph_ready, 1)

            @block.tensor
            def _(pe):
                three = ((0, 0), (0, 1), (1, 0))
                with pe.Fori(0, E1 // 2) as i:
                    for k in range(2):
                        e = 2 * i + k
                        pe.wait_ge(w_split, 6 * e + 12)
                        for j in range(NJ):
                            f, n = j % FC, j // FC
                            terms = [(c, a, z) for c in range(DC) for a, z in three]
                            for m, banks, ready, written in ((0, ub, g_ready, u_written), (1, zb, p_ready, z_written)):
                                pe.wait_ge(ready, NJ * e + j + 1)
                                for q, (c, a, z) in enumerate(terms):
                                    last = pe.matmul(banks[j % 2][:, 0:W],
                                                     w[m][:, k, a, c * F1 + f * 128:c * F1 + (f + 1) * 128],
                                                     core.hT[:, z, c, n * W:(n + 1) * W], start=(q == 0),
                                                     stop=(q == len(terms) - 1))
                                last.then_inc(written, 1)
                        for b in range(B):
                            pe.wait_ge(pl_ready, NJ * e + FC * (b // SEQ + 1) + 2)
                            pe.wait_ge(x_updated, B * e + B + b + 1)
                            terms = [(f, a, z) for f in range(FC) for a, z in three]
                            for q, (f, a, z) in enumerate(terms):
                                last = pe.matmul(yb[b % 4][0:S, 0:D], ph[:, a, f, b * S:(b + 1) * S],
                                                 w[2][:, k, z, f * D:(f + 1) * D], start=(q == 0),
                                                 stop=(q == len(terms) - 1))
                            last.then_inc(y_written, 1)



def build(nc, inputs, out):
    core = Core(nc, inputs, out)
    with core.stack:
        with core.ctx_stack:
            load_stage(core)
            l0_xattn_stage(core)
        for stages in ((routing_stage, experts0_stage), (l1_xattn_stage,), (l1_self_attn_stage, experts1_stage)):
            with ExitStack() as kept:
                def keep(name, shape, dt=F32):
                    return kept.enter_context(nc.sbuf_tensor(name, shape, dt))

                for stage in stages:
                    stage(core, keep)
        store_stage(core)


def store_stage(core):
    with Stage(core, "store") as st:
        stored = st.sem("stored")
        with core.nc.Block() as block:

            @block.sync
            def _(sp):
                sp.dma_start(core.out.rearrange("b s d -> s b d"), core.x[:]).then_inc(stored, 16)
                sp.wait_ge(stored, 16)


def kernel(**inputs):
    import numpy as _np
    import concourse.bacc as _bacc
    from concourse import mybir as _mybir
    from concourse.bass_utils import run_bass_kernel_spmd as _run

    def take(name):
        return _np.asarray(inputs[name])

    def column(a, parts):
        out = _np.zeros((128, a.size // parts), _np.float32)
        out[:parts] = a.reshape(-1, parts).T
        return out

    def padded(a):
        heads = a.reshape(*a.shape[:-1], H1, HD1)
        return _np.concatenate([heads, _np.zeros((*heads.shape[:-1], PAD - HD1), _np.float32)], -1)\
                  .reshape(*a.shape[:-1], H1 * PAD)

    cols = {
        "lnx_g": column(take("L0_xattn_ln_x_g"), CF), "lnx_b": column(take("L0_xattn_ln_x_b"), CF),
        "lnl_g": column(take("L0_xattn_ln_l_g"), 128), "lnl_b": column(take("L0_xattn_ln_l_b"), 128),
        "qn_g": _np.tile(take("L0_xattn_qn_g"), 2)[:, None], "kn_g": _np.tile(take("L0_xattn_kn_g"), 2)[:, None],
        "bq": column(padded(take("L1_xattn_bq")), 128), "bk": column(padded(take("L1_xattn_bk")), 128),
        "attn_w": column(take("L1_ffn_attn_norm_w"), 128), "ffn_w": column(take("L1_ffn_ffn_norm_w"), 128),
    }
    rows = {
        "g_xattn": take("g_xattn"), "g_ffn": take("g_ffn"), "log_temp": take("L0_ffn_log_temp").reshape(1),
        "bo0": take("L0_xattn_bo"), "bo1": take("L1_xattn_bo"), "bv1": take("L1_xattn_bv"),
        "iota": _np.arange(CAP, dtype=_np.float32),
    }
    wlkv = take("L0_xattn_Wlkv")
    arrays = {
        "x": take("x"),
        "ctx": take("ctx_768"),
        "mask": take("mask_BxS2_bk0").reshape(1, B * C),
        "ident": _np.eye(128, dtype=_np.float32),
        "cols": _np.concatenate([cols[n] for n in COLS], 1),
        "rows": _np.concatenate([rows[n] for n in ROWS])[None, :],
        "w0kv": take("L0_xattn_Wkv").T,
        "w0l": _np.concatenate([wlkv[:D], take("L0_xattn_Wq"), wlkv[D:]]).T,
        "w0o": take("L0_xattn_Wo").T,
    }
    arrays.update(more_arrays(take, padded, _np))
    arrays = {f"in_{n}": _np.ascontiguousarray(a) for n, a in arrays.items()}
    nc = _bacc.Bacc("TRN2", target_bir_lowering=False, num_devices=1)
    given = {n[3:]: nc.dram_tensor(n, a.shape, _mybir.dt.from_np(a.dtype), kind="ExternalInput").ap()
             for n, a in arrays.items()}
    out = nc.dram_tensor("out", (B, S, D), F32, kind="ExternalOutput").ap()
    build(nc, given, out)
    r = _run(nc, [arrays], core_ids=[0])
    return r.results[0]["out"]


def more_arrays(take, padded, np):
    return {
        "w1q": padded(take("L1_xattn_Wq")), "w1k": padded(take("L1_xattn_Wk")), "w1v": take("L1_xattn_Wv"),
        "w1o": take("L1_xattn_Wo"),
        "s_wqk": np.concatenate([take("L1_ffn_wq"), take("L1_ffn_wk")], 1), "s_wv": take("L1_ffn_wv"),
        "s_wo": take("L1_ffn_wo"), "router": take("L1_ffn_router_w"), "freqs": take("L1_ffn_freqs_cis"),
        "causal": np.triu(np.full((S, S), NEG, np.float32), 1),
        "m_w1": take("L1_ffn_w1"), "m_w3": take("L1_ffn_w3"), "m_w2": take("L1_ffn_w2"),
        "gate_query": take("L0_ffn_gate_query").T,
        "w1": take("L0_ffn_w1"), "w2": take("L0_ffn_w2"),
        "b1": take("L0_ffn_b1").reshape(E0, F0 // 128, 128).transpose(0, 2, 1), "b2": take("L0_ffn_b2"),
    }
```

```python
from contextlib import ExitStack

import concourse.bass as bass
from concourse import mybir

F32 = mybir.dt.float32
F16 = mybir.dt.float16
U8 = mybir.dt.uint8
ALU = mybir.AluOpType
ACT = mybir.ActivationFunctionType
AX = mybir.AxisListType

B, S, D = 16, 112, 256
C, CD = 375, 192
CT, CP = 3, 125
CF = CD // 2
DC = D // 128
H0, HD0 = 4, 64
KEYS0 = C + S
H1, HD1 = 16, 16
PAD = 32
HG = 128 // PAD
E0, F0, CAP = 16, 1024, 64
SINKHORN = 6
E1, F1, TOP = 8, 512, 2
LN_EPS = 1e-5
RMS_EPS = 1e-6
RMS_MIN_SQ = 1e-16
NEG = -1e9
MASKED = 1e30

COLS, ROWS = {}, {}
for _name, _n in (("lnx_g", 2), ("lnx_b", 2), ("lnl_g", 2), ("lnl_b", 2), ("qn_g", 1), ("kn_g", 1),
                  ("bk", 4), ("pad_masks", 3), ("attn_w", 2), ("ffn_w", 2)):
    COLS[_name] = (sum(n for _, n in COLS.values()), _n)
for _name, _n in (("g_xattn", 2), ("g_ffn", 2), ("log_temp", 1), ("bo0", D), ("bo1", D), ("bv1", D), ("bq1", D),
                  ("iota", CAP)):
    ROWS[_name] = (sum(n for _, n in ROWS.values()), _n)
NCOLS = sum(n for _, n in COLS.values())
NROWS = sum(n for _, n in ROWS.values())


def widen(ap, axis, n):
    ap = ap.unsqueeze(axis)
    shape = list(ap.shape)
    shape[axis] = n
    return ap.broadcast_to(shape)


class Chain:

    def __init__(self, eng, sem, base=0):
        self.eng, self.sem, self.base, self.n = eng, sem, base, 0

    def __call__(self, instruction):
        self.n += 1
        instruction.then_inc(self.sem, 1)
        self.eng.wait_ge(self.sem, self.base + self.n)


class Core:

    def __init__(self, nc, inputs, out):
        self.nc, self.inp, self.out = nc, inputs, out
        self.stack, self.ctx_stack = ExitStack(), ExitStack()
        self.spent = []

    def clear_semaphores(self):
        self.nc.clear_and_free_semaphores(self.spent)
        self.nc.all_engine_barrier()
        self.spent = []

    def col(self, name, c=0, n=1, parts=128):
        at = COLS[name][0] + c
        return self.cols[0:parts, at:at + n]

    def row(self, name, c=0, n=None, parts=S):
        at, width = ROWS[name]
        return self.rows[0:parts, at + c:at + c + (width - c if n is None else n)]


class Stage:

    def __init__(self, core, name):
        self.core, self.nc, self.name, self.stack = core, core.nc, name, ExitStack()

    def __enter__(self):
        self.stack.__enter__()
        return self

    def __exit__(self, *a):
        return self.stack.__exit__(*a)

    def sb(self, name, shape, dt=F32):
        return self.stack.enter_context(self.nc.sbuf_tensor(f"{self.name}_{name}", shape, dt))

    def bank(self, name, dt=F32, cols=512):
        return self.stack.enter_context(self.nc.psum_tensor(f"{self.name}_{name}", [128, cols], dt))

    def sem(self, name):
        self.core.spent.append(self.nc.alloc_semaphore(name=f"{self.name}_{name}"))
        return self.core.spent[-1]

    def block(self):
        return self.stack.enter_context(self.nc.Block())


def load_stage(core):
    nc, inp = core.nc, core.inp

    def keep(name, shape, dt=F32):
        return core.stack.enter_context(nc.sbuf_tensor(name, shape, dt))

    core.stored = core.stack.enter_context(nc.semaphore("stored"))
    core.x = keep("x_tokens", [S, B, D])
    core.ident = keep("ident", [128, 128])
    core.cols = keep("cols", [128, NCOLS])
    core.rows = keep("rows", [128, NROWS])
    core.half = keep("minus_half", [128, 64])
    core.gate = keep("gate_tanh", [128, 4])
    core.ctx = core.ctx_stack.enter_context(nc.sbuf_tensor("ctx_tokens", [CP, B * CT, CD], F32))
    with Stage(core, "load") as st:
        loaded = st.sem("loaded")
        with nc.Block() as block:

            @block.sync
            def _(sp):
                sp.dma_start(core.x[:], inp["x"].rearrange("b s d -> s b d")).then_inc(loaded, 16)
                sp.dma_start(core.ident[:], inp["ident"]).then_inc(loaded, 16)
                sp.dma_start(core.cols[:], inp["cols"]).then_inc(loaded, 16)
                sp.dma_start(core.rows[:], inp["rows"].broadcast_to([128, NROWS])).then_inc(loaded, 16)
                sp.dma_start(core.ctx[:].rearrange("p (b t) d -> p b t d", t=CT),
                             inp["ctx"].rearrange("b (t p) d -> p b t d", p=CP)).then_inc(loaded, 16)
                sp.wait_ge(loaded, 80)

            @block.gpsimd
            def _(pool):
                pool.memset(core.half[:], -0.5)

            @block.scalar
            def _(act):
                act.wait_ge(loaded, 80)
                act.activation(core.gate[:], core.rows[:, 0:4], ACT.Tanh)


def stats_stage(core, name, x, parts, tiles, mean, var_eps, rstd):
    nc = core.nc
    n = x.shape[2]
    with Stage(core, name) as st:
        raw = st.sb("raw", [parts, tiles, 6])
        tmp = st.sb("tmp", [parts, tiles])
        dev = st.sb("dev", [parts, tiles])
        dve_step, var_ready = st.sem("dve_step"), st.sem("var_ready")
        with nc.Block() as block:

            @block.vector
            def _(dve):
                step = Chain(dve, dve_step)
                with dve.Fori(0, tiles) as t:
                    dve.bn_stats(raw[:, bass.ds(t, 1), :].rearrange("p a b -> p (a b)"),
                                 x[:, bass.ds(t, 1), :].rearrange("p a b -> p (a b)")).then_inc(dve_step, 1)
                dve.wait_ge(dve_step, tiles)
                step.n = tiles
                step(dve.tensor_tensor(mean, raw[:, :, 1], raw[:, :, 4], ALU.add))
                step(dve.tensor_scalar(mean, mean, 0.5, None, ALU.mult))
                step(dve.tensor_tensor(dev[:], raw[:, :, 1], raw[:, :, 4], ALU.subtract))
                step(dve.scalar_tensor_tensor(out=dev[:], in0=dev[:], scalar=0.25, in1=dev[:],
                                              op0=ALU.mult, op1=ALU.mult))
                step(dve.tensor_tensor(tmp[:], raw[:, :, 2], raw[:, :, 5], ALU.add))
                step(dve.scalar_tensor_tensor(out=dev[:], in0=tmp[:], scalar=1.0 / n, in1=dev[:],
                                              op0=ALU.mult, op1=ALU.add))
                dve.tensor_scalar(var_eps, dev[:], LN_EPS, None, ALU.add).then_inc(var_ready, 1)

            @block.gpsimd
            def _(pool):
                pool.wait_ge(var_ready, 1)
                pool.tensor_tensor(rstd, var_eps, core.half[0:parts, 0:tiles], ALU.pow)


def after(eng, sem, value):
    if not (isinstance(value, int) and value <= 0):
        eng.wait_ge(sem, value)


def rounds(eng, one_round, first, last):
    one_round(-1, 1, False, True, False)
    one_round(0, 0, True, True, False)
    with eng.Fori(0, B // 2 - 1) as i:
        one_round(2 * i + 1, 1, True, True, True)
        one_round(2 * i + 2, 0, True, True, True)
    one_round(B - 1, 1, True, False, True)
    one_round(B, 0, False, False, True)


XA0_ORDER = [
    ("F", "norm", 0), ("H", "sc", 0), ("F", "tr", 0), ("H", "sc", 1), ("T", "hT", 0), ("F", "kv", 0),
    ("H", "pt", 0), ("T", "wo", 0), ("F", "kv", 1), ("H", "pv", 0), ("F", "kv", 2), ("H", "sc", 2), ("H", "pt", 1),
    ("F", "ssc", 0), ("F", "lat", 0), ("H", "pv", 1), ("F", "ssl", 0), ("F", "lat", 1), ("H", "sc", 3), ("H", "pt", 2),
    ("H", "pv", 2), ("F", "unit", 0), ("H", "pt", 3), ("H", "pv", 3), ("F", "kqT", 0), ("H", "out", 0),
]


def l0_xattn_stage(core):
    nc, inp = core.nc, core.inp
    with Stage(core, "xa0") as st:
        xmean, xve, xrstd = (st.sb(n, [S, B]) for n in ("xmean", "xve", "xrstd"))
        cmean, cve, crstd = (st.sb(n, [CP, B * CT]) for n in ("cmean", "cve", "crstd"))
        stats_stage(core, "xa0_xs", core.x, S, B, xmean[:], xve[:], xrstd[:])
        stats_stage(core, "xa0_cs", core.ctx, CP, B * CT, cmean[:], cve[:], crstd[:])

        wkv = st.sb("wkv", [CF, 2, 2 * D])
        wl = st.sb("wl", [128, DC, 3 * D])
        wo = st.sb("wo", [128, DC, D])
        masks = st.sb("masks", [S, B, C], U8)
        maskadd = st.sb("maskadd", [S, 2, KEYS0])
        bo = st.sb("bo", [S, D])
        gq = st.sb("gq", [128, 1])
        cn = st.sb("cn", [CP, CT, CD])
        xn = st.sb("xn", [S, D])
        cT = st.sb("cT", [CF, 2, C])
        xT = st.sb("xT", [128, DC, S])
        kv = st.sb("kv", [CP, 2, CT, 2 * D])
        lat = st.sb("lat", [S, 2, 3 * D])
        sqc = st.sb("sqc", [CP, CT, D])
        sql = st.sb("sql", [S, 2 * D])
        ssc, rrc = st.sb("ssc", [CP, CT * H0]), st.sb("rrc", [CP, CT * H0])
        ssl, rrl = st.sb("ssl", [S, 2 * H0]), st.sb("rrl", [S, 2 * H0])
        kT = st.sb("kT", [128, 2, DC, KEYS0])
        qT = st.sb("qT", [128, 2, DC, S])
        scores = st.sb("scores", [S, 2, KEYS0])
        top = st.sb("top", [S, H0])
        probs = st.sb("probs", [S, 2, KEYS0])
        total, rtotal = st.sb("total", [S, H0]), st.sb("rtotal", [S, H0])
        pT = st.sb("pT", [CP, 2, 4 * S])
        heads = st.sb("heads", [S, D])
        headsT = st.sb("headsT", [128, DC, S])
        add = st.sb("add", [S, D])
        trans = [st.bank("trans0"), st.bank("trans1")]
        proj = [st.bank("proj0"), st.bank("proj1")]
        score = [st.bank("score0"), st.bank("score1")]
        ptb, outb = st.bank("ptb"), st.bank("outb")

        (weights_in, dve_step, ready_once, mask_ready, cn_ready, trans_written, cT_ready, xT_ready, proj_written,
         kv_ready, sq_ready, ss_ready, rr_ready, kqn_ready, kT_written, kT_ready, qT_ready, score_written,
         scores_ready, probs_ready, pT_written, pT_ready, out_written, heads_ready, headsT_written,
         headsT_ready, wo_written, x_updated, held) = (st.sem(n) for n in
            "weights_in dve_step ready_once mask_ready cn_ready trans_written cT_ready xT_ready proj_written "
            "kv_ready sq_ready ss_ready rr_ready kqn_ready kT_written kT_ready qT_ready score_written "
            "scores_ready probs_ready pT_written pT_ready out_written heads_ready headsT_written "
            "headsT_ready wo_written x_updated held".split())

        with nc.Block() as block:

            @block.sync
            def _(sp):
                sp.dma_start(wkv[:], inp["w0kv"].rearrange("(c p) n -> p c n", p=CF)).then_inc(weights_in, 16)
                sp.dma_start(wl[:], inp["w0l"].rearrange("(c p) n -> p c n", p=128)).then_inc(weights_in, 16)
                sp.dma_start(wo[:], inp["w0o"].rearrange("(c p) n -> p c n", p=128)).then_inc(weights_in, 16)
                sp.dma_start(masks[:].rearrange("p b c -> p (b c)"),
                             inp["mask"].broadcast_to([S, B * C])).then_inc(weights_in, 16)
                sp.wait_ge(weights_in, 64)

            @block.vector
            def _(dve):
                step = Chain(dve, dve_step)
                dve.wait_ge(weights_in, 64)
                step(dve.tensor_scalar(xve[:], xve[:], -LN_EPS, None, ALU.add))
                step(dve.tensor_tensor(xve[:], xve[:], xrstd[:], ALU.mult))
                step(dve.tensor_tensor(xve[:], xve[:], xrstd[:], ALU.mult))
                dve.tensor_scalar(xve[:], xve[:], LN_EPS, None, ALU.add).then_inc(ready_once, 1)
                dve.tensor_scalar(gq[:], core.col("qn_g"), HD0 ** -0.5, None, ALU.mult).then_inc(ready_once, 1)
                dve.memset(maskadd[:], 0.0).then_inc(ready_once, 1)
                dve.tensor_scalar(bo[:], core.row("bo0"), core.gate[0:S, 0:1], None, ALU.mult)\
                   .then_inc(ready_once, 1)
                dve.memset(ptb[:], 0.0).then_inc(ready_once, 1)
                dve.wait_ge(ready_once, 6)
                step(dve.tensor_tensor(xrstd[:], xrstd[:], xve[:], ALU.mult))

                def one_round(b, k, heads_on, front_on, tail_on):
                    n, m = b + 1, 1 - k
                    on = {"H": heads_on, "F": front_on, "T": tail_on}
                    for part, what, j in XA0_ORDER:
                        if not on[part]:
                            continue
                        if what == "norm":
                            after(dve, trans_written, 3 * n)
                            for t in range(CT):
                                dve.tensor_scalar(cn[:, t, :],
                                                  core.ctx[:, bass.ds(n * CT + t, 1), :].rearrange("p a c -> p (a c)"),
                                                  cmean[:, bass.ds(n * CT + t, 1)], crstd[:, bass.ds(n * CT + t, 1)],
                                                  ALU.subtract, ALU.mult).then_inc(cn_ready, 1)
                            dve.tensor_scalar(xn[:], core.x[:, bass.ds(n, 1), :].rearrange("p a c -> p (a c)"),
                                              xmean[:, bass.ds(n, 1)], xrstd[:, bass.ds(n, 1)],
                                              ALU.subtract, ALU.mult).then_inc(cn_ready, 1)
                            dve.tensor_scalar(maskadd[:, m, 0:C],
                                              masks[:, bass.ds(n, 1), :].rearrange("p a c -> p (a c)"),
                                              -1.0, MASKED, ALU.add, ALU.mult).then_inc(mask_ready, 1)
                        if what == "ssc":
                            dve.wait_ge(kv_ready, 5 * n + 3)
                            kc = kv[:, m, :, 0:D]
                            dve.tensor_tensor(sqc[:], kc, kc, ALU.mult).then_inc(sq_ready, 1)
                            dve.wait_ge(sq_ready, 2 * n + 1)
                            dve.tensor_reduce(ssc[:], sqc[:].rearrange("p t (h d) -> p (t h) d", h=H0), AX.X,
                                              ALU.add).then_inc(ss_ready, 1)
                            dve.wait_ge(ss_ready, 4 * n + 1)
                            dve.tensor_scalar(ssc[:], ssc[:], 1.0 / HD0, RMS_MIN_SQ, ALU.mult, ALU.max)\
                               .then_inc(ss_ready, 1)
                        if what == "ssl":
                            dve.wait_ge(kv_ready, 5 * n + 4)
                            kq = lat[:, m, 0:2 * D]
                            dve.tensor_tensor(sql[:], kq, kq, ALU.mult).then_inc(sq_ready, 1)
                            dve.wait_ge(sq_ready, 2 * n + 2)
                            dve.tensor_reduce(ssl[:], sql[:].rearrange("p (h d) -> p h d", h=2 * H0), AX.X, ALU.add)\
                               .then_inc(ss_ready, 1)
                            dve.wait_ge(ss_ready, 4 * n + 3)
                            dve.tensor_scalar(ssl[:], ssl[:], 1.0 / HD0, RMS_MIN_SQ, ALU.mult, ALU.max)\
                               .then_inc(ss_ready, 1)
                        if what == "unit":
                            dve.wait_ge(rr_ready, 2 * n + 1)
                            for t in range(CT):
                                k4 = kv[:, m, t, 0:D].rearrange("p (h d) -> p h d", h=H0)
                                dve.tensor_tensor(sqc[:, t, :].rearrange("p (h d) -> p h d", h=H0), k4,
                                                  widen(rrc[:, t * H0:(t + 1) * H0], 2, HD0), ALU.mult)\
                                   .then_inc(kqn_ready, 1)
                            dve.wait_ge(rr_ready, 2 * n + 2)
                            dve.tensor_tensor(sql[:].rearrange("p (h d) -> p h d", h=2 * H0),
                                              lat[:, m, 0:2 * D].rearrange("p (h d) -> p h d", h=2 * H0),
                                              widen(rrl[:], 2, HD0), ALU.mult).then_inc(kqn_ready, 1)
                        if what == "sc":
                            dve.wait_ge(score_written, H0 * b + j + 1)
                            dve.wait_ge(mask_ready, b + 1)
                            after(dve, probs_ready, H0 * b + j - 1)
                            dve.sem_inc(held, 1)
                            dve.tensor_tensor_reduce(out=scores[:, j % 2, :], in0=score[j % 2][0:S, 0:KEYS0],
                                                     in1=maskadd[:, k, :], scale=-1.0, scalar=3e38, op0=ALU.add,
                                                     op1=ALU.min, accum_out=top[:, j:j + 1]).then_inc(scores_ready, 1)
                        if what == "pt":
                            dve.wait_ge(pT_written, H0 * b + j + 1)
                            dve.tensor_copy(pT[:, j % 2, :], ptb[0:CP, 0:4 * S]).then_inc(pT_ready, 1)
                        if what == "out":
                            dve.wait_ge(probs_ready, H0 * b + H0)
                            dve.reciprocal(rtotal[:], total[:]).then_inc(heads_ready, 1)
                            dve.wait_ge(heads_ready, 2 * b + 1)
                            dve.wait_ge(out_written, b + 1)
                            dve.tensor_tensor(heads[:].rearrange("p (h d) -> p h d", h=H0),
                                              outb[0:S, 0:D].rearrange("p (h d) -> p h d", h=H0),
                                              widen(rtotal[:], 2, HD0), ALU.mult).then_inc(heads_ready, 1)
                        if what == "wo":
                            dve.wait_ge(wo_written, b)
                            dve.scalar_tensor_tensor(out=add[:], in0=outb[0:S, 0:D], scalar=core.gate[0:S, 0:1],
                                                     in1=bo[:], op0=ALU.mult, op1=ALU.add).then_inc(x_updated, 1)
                            dve.wait_ge(x_updated, 2 * b - 1)
                            xb = core.x[:, bass.ds(b - 1, 1), :].rearrange("p a c -> p (a c)")
                            dve.tensor_tensor(xb, xb, add[:], ALU.add).then_inc(x_updated, 1)

                rounds(dve, one_round, 0, B)

            @block.gpsimd
            def _(pool):
                pool.wait_ge(ready_once, 1)
                pool.tensor_tensor(xve[:], xve[:], core.half[0:S, 0:B], ALU.pow).then_inc(ready_once, 1)
                with pool.Fori(0, B) as b:
                    pool.wait_ge(ss_ready, 4 * b + 2)
                    pool.tensor_tensor(rrc[:], ssc[:], core.half[0:CP, 0:CT * H0], ALU.pow).then_inc(rr_ready, 1)
                    pool.wait_ge(ss_ready, 4 * b + 4)
                    pool.tensor_tensor(rrl[:], ssl[:], core.half[0:S, 0:2 * H0], ALU.pow).then_inc(rr_ready, 1)

            @block.scalar
            def _(act):
                act.wait_ge(ready_once, 6)

                def one_round(b, k, heads_on, front_on, tail_on):
                    n, m = b + 1, 1 - k
                    on = {"H": heads_on, "F": front_on, "T": tail_on}
                    for part, what, j in XA0_ORDER:
                        if not on[part]:
                            continue
                        if what == "tr":
                            for c in range(2):
                                act.wait_ge(trans_written, 3 * n + c + 1)
                                act.activation(cT[:, c, :], trans[c][0:CF, 0:C], ACT.Identity,
                                               scale=core.col("lnx_g", c, parts=CF),
                                               bias=core.col("lnx_b", c, parts=CF)).then_inc(cT_ready, 1)
                            act.wait_ge(trans_written, 3 * n + 3)
                            for c in range(DC):
                                act.activation(xT[:, c, :], proj[0][:, c * S:(c + 1) * S], ACT.Identity,
                                               scale=core.col("lnl_g", c), bias=core.col("lnl_b", c))\
                                   .then_inc(xT_ready, 1)
                        if what == "kv":
                            act.wait_ge(proj_written, 5 * n + j + 1)
                            act.activation(kv[:, m, j, :], proj[(j + 1) % 2][0:CP, :], ACT.Copy).then_inc(kv_ready, 1)
                        if what == "lat" and j == 0:
                            act.wait_ge(proj_written, 5 * n + 4)
                            act.activation(lat[:, m, 0:2 * D], proj[0][0:S, :], ACT.Copy).then_inc(kv_ready, 1)
                        if what == "lat" and j == 1:
                            act.wait_ge(proj_written, 5 * n + 5)
                            act.activation(lat[:, m, 2 * D:3 * D], proj[1][0:S, 0:D], ACT.Copy).then_inc(kv_ready, 1)
                        if what == "kqT":
                            for c in range(DC):
                                act.wait_ge(kT_written, 3 * n + c + 1)
                                act.activation(kT[:, m, c, :], trans[c][:, 0:KEYS0], ACT.Copy, scale=core.col("kn_g"))\
                                   .then_inc(kT_ready, 1)
                            act.wait_ge(kT_written, 3 * n + 3)
                            act.activation(qT[:, m, :, :].rearrange("p c s -> p (c s)"), proj[0][:, 0:DC * S],
                                           ACT.Copy, scale=gq[:]).then_inc(qT_ready, 1)
                        if what == "sc":
                            act.wait_ge(scores_ready, H0 * b + j + 1)
                            after(act, pT_written, H0 * b + j - 1)
                            act.activation(probs[:, j % 2, :], scores[:, j % 2, :], ACT.Exp, scale=-1.0,
                                           bias=top[:, j:j + 1], accum_out=total[:, j:j + 1]).then_inc(probs_ready, 1)
                        if what == "hT":
                            act.wait_ge(headsT_written, b)
                            act.activation(headsT[:].rearrange("p c s -> p (c s)"), outb[:, 0:DC * S], ACT.Copy)\
                               .then_inc(headsT_ready, 1)

                rounds(act, one_round, 0, B)

            @block.tensor
            def _(pe):
                idc, ids = core.ident[0:CP, 0:CP], core.ident[0:S, 0:S]
                pe.wait_ge(weights_in, 64)
                pe.wait_ge(ready_once, 6)

                def one_round(b, k, heads_on, front_on, tail_on):
                    n, m = b + 1, 1 - k
                    on = {"H": heads_on, "F": front_on, "T": tail_on}
                    for part, what, j in XA0_ORDER:
                        if not on[part]:
                            continue
                        if what == "tr":
                            pe.wait_ge(cn_ready, 4 * n + 4)
                            after(pe, kT_ready, 2 * n)
                            after(pe, qT_ready, n)
                            for c in range(2):
                                for t in range(CT):
                                    last = pe.transpose(trans[c][0:CF, t * CP:(t + 1) * CP],
                                                        cn[:, t, c * CF:(c + 1) * CF], idc)
                                last.then_inc(trans_written, 1)
                            for c in range(DC):
                                last = pe.transpose(proj[0][:, c * S:(c + 1) * S], xn[:, c * 128:(c + 1) * 128], ids)
                            last.then_inc(trans_written, 1)
                        if what == "kv":
                            if j == 0:
                                pe.wait_ge(cT_ready, 2 * n + 2)
                                after(pe, kv_ready, 5 * n)
                            if j == 1:
                                pe.wait_ge(xT_ready, 2 * n + 2)
                            if j == 2:
                                pe.wait_ge(kv_ready, 5 * n + 1)
                            for c in range(2):
                                last = pe.matmul(proj[(j + 1) % 2][0:CP, :], cT[:, c, j * CP:(j + 1) * CP],
                                                 wkv[:, c, :], start=(c == 0), stop=(c == 1))
                            last.then_inc(proj_written, 1)
                        if what == "lat":
                            pe.wait_ge(kv_ready, 5 * n + 2 + j)
                            o, of = ((proj[0][0:S, :], slice(0, 2 * D)), (proj[1][0:S, 0:D], slice(2 * D, 3 * D)))[j]
                            for c in range(DC):
                                last = pe.matmul(o, xT[:, c, :], wl[:, c, of], start=(c == 0), stop=(c == DC - 1))
                            last.then_inc(proj_written, 1)
                        if what == "kqT":
                            pe.wait_ge(kqn_ready, 4 * n + 4)
                            for c in range(DC):
                                for t in range(CT):
                                    pe.transpose(trans[c][:, t * CP:(t + 1) * CP], sqc[:, t, c * 128:(c + 1) * 128],
                                                 idc)
                                pe.transpose(trans[c][:, C:KEYS0], sql[:, c * 128:(c + 1) * 128], ids)\
                                  .then_inc(kT_written, 1)
                            pe.wait_ge(kv_ready, 5 * n + 4)
                            for c in range(DC):
                                last = pe.transpose(proj[0][:, c * S:(c + 1) * S],
                                                    sql[:, D + c * 128:D + (c + 1) * 128], ids)
                            last.then_inc(kT_written, 1)
                        if what == "sc":
                            if j == 0:
                                pe.wait_ge(kT_ready, 2 * b + 2)
                                pe.wait_ge(qT_ready, b + 1)
                            after(pe, scores_ready, H0 * b + j - 1)
                            r = HD0 * (j % 2)
                            pe.matmul(score[j % 2][0:S, 0:KEYS0], qT[r:r + HD0, k, j // 2, :],
                                      kT[r:r + HD0, k, j // 2, :], start=True, stop=True).then_inc(score_written, 1)
                        if what == "pt":
                            pe.wait_ge(probs_ready, H0 * b + j + 1)
                            after(pe, pT_ready, H0 * b + j)
                            for t in range(CT):
                                pe.transpose(ptb[0:CP, t * S:(t + 1) * S], probs[:, j % 2, t * CP:(t + 1) * CP], ids)
                            pe.transpose(ptb[0:S, CT * S:(CT + 1) * S], probs[:, j % 2, C:KEYS0], ids)\
                              .then_inc(pT_written, 1)
                        if what == "pv":
                            pe.wait_ge(pT_ready, H0 * b + j + 1)
                            if j == 0:
                                pe.wait_ge(kv_ready, 5 * b + 5)
                                after(pe, x_updated, 2 * b - 1)
                            o = outb[0:S, j * HD0:(j + 1) * HD0]
                            for t in range(CT):
                                pe.matmul(o, pT[:, j % 2, t * S:(t + 1) * S],
                                          kv[:, k, t, D + j * HD0:D + (j + 1) * HD0], start=(t == 0), stop=False)
                            last = pe.matmul(o, pT[0:S, j % 2, CT * S:(CT + 1) * S],
                                             lat[:, k, 2 * D + j * HD0:2 * D + (j + 1) * HD0], start=False, stop=True)
                            if j == H0 - 1:
                                last.then_inc(out_written, 1)
                        if what == "hT":
                            pe.wait_ge(heads_ready, 2 * b)
                            for c in range(DC):
                                last = pe.transpose(outb[:, c * S:(c + 1) * S], heads[:, c * 128:(c + 1) * 128], ids)
                            last.then_inc(headsT_written, 1)
                        if what == "wo":
                            pe.wait_ge(headsT_ready, b)
                            for c in range(DC):
                                last = pe.matmul(outb[0:S, 0:D], headsT[:, c, :], wo[:, c, :], start=(c == 0),
                                                 stop=(c == DC - 1))
                            last.then_inc(wo_written, 1)

                rounds(pe, one_round, 0, B)


def routing_stage(core, keep):
    nc, inp = core.nc, core.inp
    BE = B * E0
    HALF = BE // 2
    core.norm_hi = keep("norm_hi", [S, B, D], F16)
    core.norm_lo = keep("norm_lo", [S, B, D], F16)
    core.place = keep("place", [S, BE])
    core.gates = keep("gates", [S, BE])
    with Stage(core, "route") as st:
        mean, ve, rstd = (st.sb(n, [S, B]) for n in ("mean", "ve", "rstd"))
        stats_stage(core, "route_s", core.x, S, B, mean[:], ve[:], rstd[:])
        gq = st.sb("gq", [128, DC, E0])
        xn = st.sb("xn", [S, 2, D])
        xT = st.sb("xT", [128, 2, DC * S])
        invt = st.sb("invt", [S, 1])
        t = st.sb("t", [S, BE])
        e = st.sb("e", [S, BE])
        m, s, ln = (st.sb(n, [S, B]) for n in ("m", "s", "ln"))
        u = st.sb("u", [HALF, 2, S])
        v = st.sb("v", [HALF, 2, S])
        um, us, ul = (st.sb(n, [HALF, 2]) for n in ("um", "us", "ul"))
        aff = st.sb("aff", [HALF, 2, S])
        left = st.sb("left", [HALF, 2, S])
        best = st.sb("best", [HALF, 2, 8])
        taken = st.sb("taken", [HALF, 2, S])
        order = st.sb("order", [HALF, 2, S])
        ones = st.sb("ones", [HALF, S])
        logits = st.bank("logits")
        xTb = [st.bank("xTb0"), st.bank("xTb1")]
        by_row = st.bank("by_row")
        by_token = st.bank("by_token")
        by_token2 = st.bank("by_token2")
        (loaded, dve_step, normed, split, xT_written, xT_ready, logits_written, t_ready, row_ready, row_written,
         m_ready, e_ready, s_ready, l_ready, token_written, aff_ready, place_written, tscale) = (
            st.sem(n) for n in "loaded dve_step normed split xT_written xT_ready logits_written t_ready row_ready "
            "row_written m_ready e_ready s_ready l_ready token_written aff_ready place_written tscale".split())
        with nc.Block() as block:

            @block.sync
            def _(sp):
                sp.dma_start(gq[:], inp["gate_query"].rearrange("(c p) n -> p c n", p=128)).then_inc(loaded, 16)
                sp.wait_ge(loaded, 16)

            @block.vector
            def _(dve):
                with dve.Fori(0, B // 2) as i:
                    for k in range(2):
                        xb = core.x[:, bass.ds(2 * i + k, 1), :].rearrange("p a c -> p (a c)")
                        hi = core.norm_hi[:, bass.ds(2 * i + k, 1), :].rearrange("p a c -> p (a c)")
                        lo = core.norm_lo[:, bass.ds(2 * i + k, 1), :].rearrange("p a c -> p (a c)")
                        dve.wait_ge(xT_written, 2 * i + k + 1)
                        dve.tensor_scalar(xn[:, k, :], xb, mean[:, bass.ds(2 * i + k, 1)],
                                          rstd[:, bass.ds(2 * i + k, 1)], ALU.subtract, ALU.mult).then_inc(normed, 1)
                        dve.wait_ge(normed, 2 * i + k + 1)
                        dve.tensor_scalar(hi, xn[:, k, :], 1.0, None, ALU.mult).then_inc(split, 1)
                        dve.wait_ge(split, 2 * i + k + 1)
                        dve.tensor_tensor(lo, xn[:, k, :], hi, ALU.subtract)
                step = Chain(dve, dve_step)
                step(dve.memset(ones[:], 1.0))
                dve.wait_ge(logits_written, B)
                dve.wait_ge(tscale, 1)
                dve.tensor_scalar(t[:], logits[0:S, 0:BE], invt[:], None, ALU.mult).then_inc(t_ready, 1)
                fixed = step.n
                PER = 2
                with dve.Fori(0, SINKHORN) as i:
                    step = Chain(dve, dve_step, PER * i + fixed)
                    dve.wait_ge(t_ready, 2 * i + 1)
                    t3 = t[:].rearrange("p (b e) -> p b e", e=E0)
                    step(dve.tensor_reduce(m[:], t3, AX.X, ALU.max))
                    dve.tensor_tensor(t3, t3, widen(m[:], 2, E0), ALU.subtract).then_inc(t_ready, 1)
                    dve.wait_ge(e_ready, 2 * i + 1)
                    dve.tensor_reduce(s[:], e[:].rearrange("p (b e) -> p b e", e=E0), AX.X, ALU.add)\
                       .then_inc(s_ready, 1)
                    dve.wait_ge(l_ready, 2 * i + 1)
                    dve.tensor_tensor(t3, t3, widen(ln[:], 2, E0), ALU.subtract).then_inc(row_ready, 1)
                    dve.wait_ge(row_written, i + 1)
                    r3 = by_row[0:HALF, 0:2 * S].rearrange("p (c s) -> p c s", c=2)
                    step(dve.tensor_reduce(um[:], r3, AX.X, ALU.max))
                    dve.tensor_tensor(u[:], r3, widen(um[:], 2, S), ALU.subtract).then_inc(row_ready, 1)
                    dve.wait_ge(e_ready, 2 * i + 2)
                    dve.tensor_reduce(us[:], v[:], AX.X, ALU.add).then_inc(s_ready, 1)
                    dve.wait_ge(l_ready, 2 * i + 2)
                    dve.tensor_tensor(u[:], u[:], widen(ul[:], 2, S), ALU.subtract).then_inc(row_ready, 1)
                    dve.wait_ge(token_written, i + 1)
                    dve.tensor_copy(t[:], by_token[0:S, 0:BE]).then_inc(t_ready, 1)
                    assert step.n == PER
                step = Chain(dve, dve_step, 0)
                step.n = PER * SINKHORN + fixed
                dve.wait_ge(aff_ready, 1)
                step(dve.tensor_copy(left[:], aff[:]))
                for r in range(CAP // 8):
                    for c in range(2):
                        last = dve.max(best[:, c, :], left[:, c, :])
                    step(last)
                    for c in range(2):
                        last = dve.match_replace(left[:, c, :], best[:, c, :], left[:, c, :], -1.0)
                    step(last)
                step(dve.tensor_scalar(taken[:], left[:], 0.0, None, ALU.is_lt))
                for c in range(2):
                    last = dve.tensor_tensor_scan(order[:, c, :], ones[:], taken[:, c, :], 0.0, ALU.mult, ALU.add)
                step(last)
                step(dve.tensor_tensor(order[:], order[:], taken[:], ALU.mult))
                step(dve.tensor_tensor(taken[:], aff[:], taken[:], ALU.mult))
                dve.tensor_scalar(order[:], order[:], -1.0, None, ALU.add).then_inc(aff_ready, 1)
                dve.wait_ge(place_written, 1)
                dve.tensor_copy(core.place[:], by_token[0:S, 0:BE])
                dve.wait_ge(place_written, 2)
                dve.tensor_scalar(core.gates[:], by_token2[0:S, 0:BE], core.gate[0:S, 2:3], None, ALU.mult)

            @block.scalar
            def _(act):
                act.activation(invt[:], core.row("log_temp"), ACT.Exp, scale=-1.0).then_inc(tscale, 1)
                with act.Fori(0, B // 2) as i:
                    for k in range(2):
                        act.wait_ge(xT_written, 2 * i + k + 3)
                        act.activation(xT[:, k, :], xTb[k][:, 0:DC * S], ACT.Copy).then_inc(xT_ready, 1)
                with act.Fori(0, SINKHORN) as i:
                    act.wait_ge(t_ready, 2 * i + 2)
                    act.activation(e[:], t[:], ACT.Exp).then_inc(e_ready, 1)
                    act.wait_ge(s_ready, 2 * i + 1)
                    act.activation(ln[:], s[:], ACT.Ln).then_inc(l_ready, 1)
                    act.wait_ge(row_ready, 3 * i + 2)
                    act.activation(v[:], u[:], ACT.Exp).then_inc(e_ready, 1)
                    act.wait_ge(s_ready, 2 * i + 2)
                    act.activation(ul[:], us[:], ACT.Ln).then_inc(l_ready, 1)
                act.wait_ge(row_ready, 3 * SINKHORN)
                act.activation(aff[:], u[:], ACT.Exp).then_inc(aff_ready, 1)

            @block.tensor
            def _(pe):
                ids, idn = core.ident[0:S, 0:S], core.ident[:]
                pe.sem_inc(xT_written, 2)
                pe.wait_ge(loaded, 16)
                with pe.Fori(0, B // 2) as i:
                    for k in range(2):
                        pe.wait_ge(normed, 2 * i + k + 1)
                        for c in range(DC):
                            last = pe.transpose(xTb[k][:, c * S:(c + 1) * S], xn[:, k, c * 128:(c + 1) * 128], ids)
                        last.then_inc(xT_written, 1)
                        pe.wait_ge(xT_ready, 2 * i + k + 1)
                        for c in range(DC):
                            last = pe.matmul(logits[0:S, bass.ds((2 * i + k) * E0, E0)], xT[:, k, c * S:(c + 1) * S],
                                             gq[:, c, :], start=(c == 0), stop=(c == DC - 1))
                        last.then_inc(logits_written, 1)
                with pe.Fori(0, SINKHORN) as i:
                    pe.wait_ge(row_ready, 3 * i + 1)
                    for c in range(2):
                        last = pe.transpose(by_row[0:HALF, c * S:(c + 1) * S], t[:, c * HALF:(c + 1) * HALF], ids)
                    last.then_inc(row_written, 1)
                    pe.wait_ge(row_ready, 3 * i + 3)
                    for c in range(2):
                        last = pe.transpose(by_token[0:S, c * HALF:(c + 1) * HALF], u[:, c, :], idn)
                    last.then_inc(token_written, 1)
                pe.wait_ge(aff_ready, 2)
                pe.wait_ge(t_ready, 2 * SINKHORN + 1)
                for c in range(2):
                    last = pe.transpose(by_token[0:S, c * HALF:(c + 1) * HALF], order[:, c, :], idn)
                last.then_inc(place_written, 1)
                for c in range(2):
                    last = pe.transpose(by_token2[0:S, c * HALF:(c + 1) * HALF], taken[:, c, :], idn)
                last.then_inc(place_written, 1)


def experts0_stage(core, keep):
    nc, inp = core.nc, core.inp
    FC = F0 // 128
    SLOTS = B * CAP
    NH = SLOTS // 512
    SEQH = B // NH
    NT = SLOTS // 128
    G = 2 * DC * NH
    with Stage(core, "ex0") as st:
        w1f = st.sb("w1f", [128, DC, F0])
        w2f = st.sb("w2f", [128, FC, D])
        w1 = st.sb("w1", [128, 2, 2, DC * F0], F16)
        w2 = st.sb("w2", [128, 2, 2, FC * D], F16)
        b1 = st.sb("b1", [128, 2, FC])
        b2 = st.sb("b2", [128, 2, D])
        pick = st.sb("pick", [S, B, CAP], F16)
        iota = st.sb("iota16", [S, CAP])
        pickT = st.sb("pickT", [128, NT * S], F16)
        identh = st.sb("identh", [S, S], F16)
        xT = st.sb("xT", [128, 2, DC, SLOTS], F16)
        h = st.sb("h", [128, 2, 512])
        hh = st.sb("hh", [128, 2, FC, SLOTS], F16)
        yf = st.sb("yf", [128, 2, D])
        y = st.sb("y", [128, 2, 2, D], F16)
        gat = [st.bank("gat0"), st.bank("gat1")]
        hid = [st.bank("hid0"), st.bank("hid1")]
        yb = [st.bank("y0"), st.bank("y1")]
        sc = [st.bank("sc0"), st.bank("sc1")]
        pTb = sc[0][:].bitcast(F16)
        (w_in, w_split, pick_ready, gat_written, xT0_ready, xT1_ready, picks_written, pickT_ready, hid_written,
         h_ready, hi_ready, lo_ready, y_written, yf_ready, yhi_ready, ylo_ready, sc_written, x_updated, const,
         held) = (st.sem(n) for n in
            "w_in w_split pick_ready gat_written xT0_ready xT1_ready picks_written pickT_ready hid_written "
            "h_ready hi_ready lo_ready y_written yf_ready yhi_ready ylo_ready sc_written x_updated const held".split())
        NJ = FC * NH

        with nc.Block() as block:

            @block.sync
            def _(sp):
                with sp.Fori(0, E0 // 2) as i:
                    for k in range(2):
                        e = bass.ds(2 * i + k, 1)
                        sp.wait_ge(w_split, 4 * (2 * i + k) + 4)
                        sp.dma_start(w1f[:], inp["w1"][e, :, :].rearrange("a (c p) f -> p (a c) f", p=128))\
                          .then_inc(w_in, 16)
                        sp.dma_start(w2f[:], inp["w2"][e, :, :].rearrange("a (c p) f -> p (a c) f", p=128))\
                          .then_inc(w_in, 16)
                        sp.wait_ge(x_updated, B * (2 * i + k) + 2)
                        sp.dma_start(b1[:, k, :], inp["b1"][e, :, :].rearrange("a p c -> p (a c)")).then_inc(w_in, 16)
                        sp.dma_start(b2[:, k, :], inp["b2"][e, :].broadcast_to([128, D])).then_inc(w_in, 16)

            @block.gpsimd
            def _(pool):
                pool.sem_inc(w_split, 4)
                with pool.Fori(0, E0 // 2) as i:
                    for k in range(2):
                        n = 4 * (2 * i + k) + 4
                        pool.wait_ge(w_in, 64 * (2 * i + k) + 64)
                        w1r, w2r = (w[:].rearrange("p c f -> p (c f)") for w in (w1f, w2f))
                        pool.sem_inc(held, 1)
                        pool.tensor_copy(w1[:, k, 0, :], w1r).then_inc(w_split, 1)
                        pool.tensor_copy(w2[:, k, 0, :], w2r).then_inc(w_split, 1)
                        pool.wait_ge(w_split, n + 2)
                        pool.tensor_tensor(w1[:, k, 1, :], w1r, w1[:, k, 0, :], ALU.subtract).then_inc(w_split, 1)
                        pool.tensor_tensor(w2[:, k, 1, :], w2r, w2[:, k, 0, :], ALU.subtract).then_inc(w_split, 1)

            @block.vector
            def _(dve):
                dve.tensor_copy(identh[:], core.ident[0:S, 0:S]).then_inc(const, 1)
                dve.tensor_copy(iota[:], core.row("iota")).then_inc(const, 1)
                dve.wait_ge(const, 2)
                dve.sem_inc(x_updated, B + 2)
                dve.sem_inc(lo_ready, 2)
                dve.sem_inc(yf_ready, 2)
                dve.sem_inc(ylo_ready, 2)
                with dve.Fori(0, E0 // 2) as i:
                    for k in range(2):
                        e = 2 * i + k
                        at = core.place[:].rearrange("p (b e) -> p b e", e=E0)[:, :, bass.ds(e, 1)]
                        dve.wait_ge(picks_written, e + 1)
                        dve.tensor_tensor(pick[:], widen(iota[:], 1, B), at.broadcast_to([S, B, CAP]), ALU.is_equal)\
                           .then_inc(pick_ready, 1)
                        for g in range(1, G, 2):
                            dve.wait_ge(gat_written, G * e + g + 1)
                            dve.tensor_copy(xT[:, g // (DC * NH), g // NH % DC, g % NH * 512:(g % NH + 1) * 512],
                                            gat[1][:]).then_inc(xT1_ready, 1)
                        for j in range(NJ):
                            f, n = j % FC, j // FC
                            at = slice(n * 512, (n + 1) * 512)
                            dve.wait_ge(hi_ready, NJ * e + j + 1)
                            dve.tensor_tensor(hh[:, 1, f, at], h[:, j % 2, :], hh[:, 0, f, at], ALU.subtract)\
                               .then_inc(lo_ready, 1)
                        for t in range(NT + 1):
                            if t < NT:
                                dve.wait_ge(y_written, NT * e + t + 1)
                                dve.wait_ge(ylo_ready, NT * e + t + 1)
                                dve.tensor_tensor(yf[:, t % 2, :], yb[t % 2][:, 0:D], b2[:, k, :], ALU.add)\
                                   .then_inc(yf_ready, 1)
                            if t >= 1:
                                for q in range(2):
                                    b = 2 * (t - 1) + q
                                    dve.wait_ge(sc_written, B * e + b + 4)
                                    dve.scalar_tensor_tensor(
                                        out=core.x[:, b, :], in0=sc[q][0:S, 0:D],
                                        scalar=core.gates[:, bass.ds(b * E0 + e, 1)], in1=core.x[:, b, :],
                                        op0=ALU.mult, op1=ALU.add).then_inc(x_updated, 1)
                            if t < NT:
                                dve.wait_ge(yhi_ready, NT * e + t + 1)
                                dve.tensor_tensor(y[:, t % 2, 1, :], yf[:, t % 2, :], y[:, t % 2, 0, :], ALU.subtract)\
                                   .then_inc(ylo_ready, 1)

            @block.scalar
            def _(act):
                act.sem_inc(h_ready, 2)
                with act.Fori(0, E0 // 2) as i:
                    for k in range(2):
                        e = 2 * i + k
                        for g in range(0, G, 2):
                            act.wait_ge(gat_written, G * e + g + 1)
                            act.activation(xT[:, g // (DC * NH), g // NH % DC, g % NH * 512:(g % NH + 1) * 512],
                                           gat[0][:], ACT.Copy).then_inc(xT0_ready, 1)
                        act.wait_ge(picks_written, e + 2)
                        act.activation(pickT[:], pTb[:, 0:NT * S], ACT.Copy).then_inc(pickT_ready, 1)
                        act.wait_ge(w_in, 64 * e + 64)
                        for j in range(NJ):
                            f, n = j % FC, j // FC
                            at = slice(n * 512, (n + 1) * 512)
                            act.wait_ge(hid_written, NJ * e + j + 1)
                            act.wait_ge(lo_ready, NJ * e + j + 1)
                            act.activation(h[:, j % 2, :], hid[j % 2][:], ACT.Gelu_apprx_tanh, bias=b1[:, k, f:f + 1])\
                               .then_inc(h_ready, 1)
                            act.wait_ge(h_ready, NJ * e + j + 3)
                            act.activation(hh[:, 0, f, at], h[:, j % 2, :], ACT.Copy).then_inc(hi_ready, 1)
                        for t in range(NT):
                            act.wait_ge(yf_ready, NT * e + t + 3)
                            act.wait_ge(sc_written, B * e + 2 * t + 1)
                            act.activation(y[:, t % 2, 0, :], yf[:, t % 2, :], ACT.Copy).then_inc(yhi_ready, 1)

            @block.tensor
            def _(pe):
                pe.sem_inc(picks_written, 1)
                pe.sem_inc(sc_written, 3)
                pe.wait_ge(const, 2)
                with pe.Fori(0, E0 // 2) as i:
                    for k in range(2):
                        e = 2 * i + k
                        pe.wait_ge(pick_ready, e + 1)
                        for g in range(G):
                            src = (core.norm_hi, core.norm_lo)[g // (DC * NH)]
                            c, n = g // NH % DC, g % NH
                            if g >= 2:
                                pe.wait_ge((xT0_ready, xT1_ready)[g % 2], G // 2 * e + g // 2)
                            for b in range(SEQH):
                                last = pe.matmul(gat[g % 2][:, b * CAP:(b + 1) * CAP],
                                                 src[:, n * SEQH + b, c * 128:(c + 1) * 128],
                                                 pick[:, n * SEQH + b, :], start=True, stop=True)
                            last.then_inc(gat_written, 1)
                        pe.wait_ge(x_updated, B * e + B + 2)
                        for t in range(NT):
                            last = pe.transpose(pTb[:, t * S:(t + 1) * S],
                                                pick[:, 2 * t:2 * t + 2, :].rearrange("p a c -> p (a c)"), identh[:])
                        last.then_inc(picks_written, 1)
                        pe.wait_ge(w_split, 4 * e + 8)
                        pe.wait_ge(xT0_ready, G // 2 * (e + 1))
                        pe.wait_ge(xT1_ready, G // 2 * (e + 1))
                        for j in range(NJ):
                            f, n = j % FC, j // FC
                            pe.wait_ge(h_ready, NJ * e + j + 1)
                            terms = [(c, a, z) for c in range(DC) for a, z in ((0, 0), (0, 1), (1, 0))]
                            for q, (c, a, z) in enumerate(terms):
                                last = pe.matmul(hid[j % 2][:], w1[:, k, a, c * F0 + f * 128:c * F0 + (f + 1) * 128],
                                                 xT[:, z, c, n * 512:(n + 1) * 512], start=(q == 0),
                                                 stop=(q == len(terms) - 1))
                            last.then_inc(hid_written, 1)
                        for t in range(NT + 1):
                            if t < NT:
                                pe.wait_ge(lo_ready, NJ * e + (FC if t < NT // NH else NJ) + 2)
                                pe.wait_ge(yf_ready, NT * e + t + 1)
                                terms = [(f, a, z) for f in range(FC) for a, z in ((0, 0), (0, 1), (1, 0))]
                                for q, (f, a, z) in enumerate(terms):
                                    last = pe.matmul(yb[t % 2][:, 0:D], hh[:, a, f, t * 128:(t + 1) * 128],
                                                     w2[:, k, z, f * D:(f + 1) * D], start=(q == 0),
                                                     stop=(q == len(terms) - 1))
                                last.then_inc(y_written, 1)
                            if t >= 1:
                                pe.wait_ge(ylo_ready, NT * e + t + 2)
                                if t == 1:
                                    pe.wait_ge(pickT_ready, e + 1)
                                for q in range(2):
                                    pe.wait_ge(x_updated, B * e + B + 2 * (t - 1) + q + 1)
                                    for z in range(2):
                                        last = pe.matmul(sc[q][0:S, 0:D],
                                                         pickT[CAP * q:CAP * (q + 1), (t - 1) * S:t * S],
                                                         y[CAP * q:CAP * (q + 1), (t - 1) % 2, z, :],
                                                         start=(z == 0), stop=(z == 1))
                                    last.then_inc(sc_written, 1)



XA1_ORDER = [
    ("H", "st", 0), ("T", "hT", 0), ("F", "ctx", 0), ("H", "st", 1), ("H", "q2T", 1), ("H", "pv", 0),
    ("H", "st", 2), ("F", "xT", 0), ("H", "pv", 1), ("T", "wo", 0), ("H", "st", 3), ("F", "k", 0), ("H", "pv", 2),
    ("H", "st", 4), ("F", "q", 0), ("H", "pv", 3), ("H", "st", 5), ("F", "k", 1), ("H", "pv", 4),
    ("H", "st", 6), ("F", "q1T", 0), ("H", "pv", 5), ("H", "st", 7), ("F", "k", 2), ("H", "pv", 6),
    ("H", "st", 8), ("F", "max", 0), ("H", "pv", 7), ("H", "norm", 0), ("H", "st", 9), ("F", "k", 3), ("H", "pv", 8),
    ("H", "st", 10), ("F", "max", 1), ("H", "pv", 9), ("H", "st", 11), ("F", "v", 0), ("H", "pv", 10),
    ("H", "st", 12), ("F", "max", 2), ("H", "pv", 11), ("H", "st", 13), ("F", "v", 1), ("H", "pv", 12),
    ("H", "st", 14), ("F", "v", 2), ("H", "pv", 13), ("H", "st", 15), ("F", "max", 3), ("H", "pv", 14),
    ("F", "q2T", 0), ("H", "pv", 15),
]


def l1_xattn_stage(core, keep):
    nc, inp = core.nc, core.inp
    NC = H1 // HG
    VW = HD1 + 1
    NP = 4
    with Stage(core, "xa1") as st:
        mean, ve, rstd = (st.sb(n, [S, B]) for n in ("mean", "ve", "rstd"))
        stats_stage(core, "xa1_s", core.x, S, B, mean[:], ve[:], rstd[:])
        wq = st.sb("wq", [128, DC, D])
        wf = st.sb("wf", [CF, 2, H1 * PAD + D])
        wh, wl = (st.sb(n, [CF, 2, H1 * PAD + D], F16) for n in ("wh", "wl"))
        wo = st.sb("wo", [128, DC, D])
        bo, bq = st.sb("bo", [S, D]), st.sb("bq", [S, D])
        identh = st.sb("identh", [S, S], F16)
        cx = st.sb("cx", [CP, CT, CD])
        xn = st.sb("xn", [S, D])
        xT = st.sb("xT", [128, DC, S])
        cT = st.sb("cT", [CF, 2, 2, C], F16)
        qf = st.sb("qf", [S, D])
        q1 = st.sb("q1", [S, H1, PAD], F16)
        q2 = st.sb("q2", [S, H1, PAD], F16)
        q1T = st.sb("q1T", [128, 2, NC, S], F16)
        q2T = st.sb("q2T", [128, 2, NC, S], F16)
        khi = st.sb("khi", [128, 2, C], F16)
        klow = st.sb("klow", [128, 2, C], F16)
        k1 = st.sb("k1", [128, 2, NC, C], F16)
        k2 = st.sb("k2", [128, 2, NC, C], F16)
        v = st.sb("v", [CP, 2, CT, H1, 2 * VW], F16)
        vf = st.sb("vf", [CP, 2, D])
        top = st.sb("top", [S, H1])
        pT = st.sb("pT", [CP, NP, CT * S])
        ph, pl = (st.sb(n, [CP, NP, CT * S], F16) for n in ("ph", "pl"))
        rtotal = st.sb("rtotal", [S, H1])
        both = st.sb("both", [S, H1, HD1])
        heads = st.sb("heads", [S, D])
        headsT = st.sb("headsT", [128, DC, S])
        add = st.sb("add", [S, D])
        stb = [st.bank("st0"), st.bank("st1")]
        maxb = [st.bank("max0"), st.bank("max1")]
        front = [st.bank("front0"), st.bank("front1")]
        outb, mix = st.bank("outb"), st.bank("mix")
        mixh = mix[:].bitcast(F16)
        (loaded, cx_in, const, w_ready, normed, cT_written, cT_ready, cTl_ready, xT_written, xT_ready, q_written, q_step, q_ready,
         q1T_written, q1T_ready, k_written, khi_ready, klow_ready, k1_ready, k2_ready, v_written, v_ready,
         max_written, top_ready, m_ready, q2T_written, q2T_ready, st_written, probs_ready, ph_ready, pl_ready, pv_written,
         norm_step, heads_ready, v_step, headsT_written, headsT_ready, wo_written, x_updated) = (st.sem(n) for n in
            "loaded cx_in const w_ready normed cT_written cT_ready cTl_ready xT_written xT_ready q_written q_step q_ready "
            "q1T_written q1T_ready k_written khi_ready klow_ready k1_ready k2_ready v_written v_ready "
            "max_written top_ready m_ready q2T_written q2T_ready st_written probs_ready ph_ready pl_ready pv_written norm_step heads_ready v_step "
            "headsT_written headsT_ready wo_written x_updated".split())
        second, first, place = (core.col("pad_masks", n) for n in range(3))

        with nc.Block() as block:

            @block.sync
            def _(sp):
                sp.dma_start(wq[:], inp["w1q"].rearrange("(c p) n -> p c n", p=128)).then_inc(loaded, 16)
                sp.dma_start(wf[:], inp["w1kv"].rearrange("(c p) n -> p c n", p=CF)).then_inc(loaded, 16)
                sp.dma_start(wo[:], inp["w1o"].rearrange("(c p) n -> p c n", p=128)).then_inc(loaded, 16)
                sp.dma_start(cx[:], inp["ctx"][0, :, :].rearrange("(t p) d -> p t d", p=CP)).then_inc(cx_in, 16)
                with sp.Fori(1, B) as b:
                    sp.wait_ge(cT_written, 2 * b)
                    sp.dma_start(cx[:], inp["ctx"][bass.ds(b, 1), :, :].rearrange("a (t p) d -> p (a t) d", p=CP))\
                      .then_inc(cx_in, 16)

            @block.gpsimd
            def _(pool):
                def lows(b):
                    for h in range(H1):
                        pool.wait_ge(ph_ready, H1 * b + h + 1)
                        after(pool, pv_written, H1 * b + h + 1 - NP)
                        pool.tensor_tensor(pl[:, h % NP, :], pT[:, h % NP, :], ph[:, h % NP, :], ALU.subtract)\
                            .then_inc(pl_ready, 1)

                lows(0)
                with pool.Fori(1, B) as b:
                    lows(b)

            @block.vector
            def _(dve):
                dve.tensor_scalar(bo[:], core.row("bo1"), core.gate[0:S, 1:2], None, ALU.mult).then_inc(const, 1)
                dve.tensor_scalar(bq[:], core.row("bq1"), HD1 ** -0.5, None, ALU.mult).then_inc(const, 1)
                dve.tensor_copy(identh[:], core.ident[0:S, 0:S]).then_inc(const, 1)
                dve.memset(q2[:], 0.0).then_inc(const, 1)
                dve.memset(v[:], 0.0).then_inc(const, 1)
                dve.wait_ge(const, 5)
                dve.memset(v[:, :, :, :, HD1:VW], 1.0).then_inc(const, 1)
                dve.wait_ge(loaded, 48)
                dve.tensor_copy(wh[:], wf[:]).then_inc(w_ready, 1)
                dve.wait_ge(w_ready, 1)
                dve.tensor_tensor(wl[:], wf[:], wh[:], ALU.subtract).then_inc(w_ready, 1)

                def normalise(b, half):
                    n = H1 // 2
                    o = outb[0:S, 0:n * 2 * VW].rearrange("p (h d) -> p h d", d=2 * VW)
                    hs, of = slice(half * n, (half + 1) * n), slice(half * n * HD1, (half + 1) * n * HD1)
                    dve.wait_ge(pv_written, H1 * b + (half + 1) * n)
                    dve.reciprocal(rtotal[:, hs], o[:, :, HD1]).then_inc(norm_step, 1)
                    dve.tensor_copy(both[:, hs, :], o[:, :, 0:HD1]).then_inc(norm_step, 1)
                    dve.wait_ge(norm_step, 6 * b + 3 * half + 2)
                    dve.tensor_tensor(both[:, hs, :], both[:, hs, :], o[:, :, VW:VW + HD1], ALU.add)\
                       .then_inc(norm_step, 1)
                    dve.wait_ge(norm_step, 6 * b + 3 * half + 3)
                    dve.tensor_tensor(heads[:, of].rearrange("p (h d) -> p h d", d=HD1), both[:, hs, :],
                                      widen(rtotal[:, hs], 2, HD1), ALU.mult).then_inc(heads_ready, 1)

                def one_round(b, k, heads_on, front_on, tail_on):
                    n, m = b + 1, 1 - k
                    on = {"H": heads_on, "F": front_on, "T": tail_on}
                    for part, what, j in XA1_ORDER:
                        if not on[part]:
                            continue
                        if what == "hT":
                            normalise(b - 1, 1)
                            dve.wait_ge(heads_ready, 3 * b - 1)
                            dve.tensor_tensor(heads[:], heads[:], core.row("bv1"), ALU.add).then_inc(heads_ready, 1)
                        if what == "norm":
                            normalise(b, 0)
                        if what == "wo":
                            xb = core.x[:, bass.ds(b - 1, 1), :].rearrange("p a c -> p (a c)")
                            dve.wait_ge(wo_written, b)
                            dve.scalar_tensor_tensor(out=add[:], in0=mix[0:S, 0:D], scalar=core.gate[0:S, 1:2],
                                                     in1=bo[:], op0=ALU.mult, op1=ALU.add).then_inc(x_updated, 1)
                            dve.wait_ge(x_updated, 2 * b - 1)
                            dve.tensor_tensor(xb, xb, add[:], ALU.add).then_inc(x_updated, 1)
                        if what == "ctx":
                            xb = core.x[:, bass.ds(n, 1), :].rearrange("p a c -> p (a c)")
                            after(dve, xT_written, n)
                            dve.tensor_scalar(xn[:], xb, mean[:, bass.ds(n, 1)], rstd[:, bass.ds(n, 1)],
                                              ALU.subtract, ALU.mult).then_inc(normed, 1)
                            for c in range(2):
                                dve.wait_ge(cT_ready, 2 * n + c + 1)
                                dve.tensor_tensor(cT[:, c, 1, :], front[c][0:CF, 0:C], cT[:, c, 0, :], ALU.subtract)\
                                   .then_inc(cTl_ready, 1)
                        if what == "q":
                            dve.wait_ge(q_written, n + 1)
                            dve.scalar_tensor_tensor(out=qf[:], in0=mix[0:S, 0:D], scalar=HD1 ** -0.5, in1=bq[:],
                                                     op0=ALU.mult, op1=ALU.add).then_inc(q_step, 1)
                            dve.wait_ge(q_step, 2 * n + 1)
                            q3 = qf[:].rearrange("p (h d) -> p h d", d=HD1)
                            dve.tensor_copy(q1[:].rearrange("p h (two d) -> p h two d", two=2),
                                            widen(q3, 2, 2)).then_inc(q_step, 1)
                            dve.wait_ge(q_step, 2 * n + 2)
                            dve.tensor_tensor(q2[:, :, 0:HD1], q3, q1[:, :, 0:HD1], ALU.subtract).then_inc(q_ready, 1)
                        if what == "k":
                            dve.wait_ge(khi_ready, NC * n + j + 1)
                            dve.tensor_scalar(klow[:, j % 2, :], khi[:, j % 2, :], second, None, ALU.mult)\
                               .then_inc(klow_ready, 1)
                            dve.tensor_scalar(k2[:, m, j, :], khi[:, j % 2, :], first, place, ALU.mult, ALU.add)\
                               .then_inc(k2_ready, 1)
                            dve.wait_ge(klow_ready, NC * n + j + 1)
                            dve.scalar_tensor_tensor(out=k1[:, m, j, :], in0=front[j % 2][:, 0:C],
                                                     scalar=core.col("bk", j), in1=klow[:, j % 2, :], op0=ALU.add,
                                                     op1=ALU.subtract).then_inc(k1_ready, 1)
                        if what == "v":
                            dve.wait_ge(v_step, 2 * (CT * n + j) + 2)
                            dve.tensor_tensor(v[:, m, j, :, VW:VW + HD1],
                                              vf[:, j % 2, :].rearrange("p (h d) -> p h d", d=HD1),
                                              v[:, m, j, :, 0:HD1], ALU.subtract).then_inc(v_ready, 1)
                        if what == "max":
                            for r in range(HG):
                                h = HG * j + r
                                dve.wait_ge(max_written, H1 * n + h + 1)
                                dve.tensor_reduce(top[:, h:h + 1], maxb[r % 2][0:S, 0:C], AX.X, ALU.max, negate=True)\
                                   .then_inc(top_ready, 1)
                            dve.wait_ge(top_ready, H1 * n + HG * (j + 1))
                            dve.tensor_copy(q2[:, HG * j:HG * (j + 1), HD1], top[:, HG * j:HG * (j + 1)])\
                               .then_inc(m_ready, 1)

                rounds(dve, one_round, 0, B)

            @block.scalar
            def _(act):
                act.wait_ge(const, 6)

                def one_round(b, k, heads_on, front_on, tail_on):
                    n, m = b + 1, 1 - k
                    on = {"H": heads_on, "F": front_on, "T": tail_on}
                    for part, what, j in XA1_ORDER:
                        if not on[part]:
                            continue
                        if what == "st":
                            act.wait_ge(st_written, H1 * b + j + 1)
                            after(act, pv_written, H1 * b + j + 1 - NP)
                            act.activation(pT[:, j % NP, :], stb[j % 2][0:CP, 0:CT * S], ACT.Exp)\
                               .then_inc(probs_ready, 1)
                            act.wait_ge(probs_ready, H1 * b + j + 1)
                            act.activation(ph[:, j % NP, :], pT[:, j % NP, :], ACT.Copy).then_inc(ph_ready, 1)
                        if what == "hT":
                            act.wait_ge(headsT_written, b)
                            act.activation(headsT[:].rearrange("p c s -> p (c s)"), mix[:, 0:DC * S], ACT.Copy)\
                               .then_inc(headsT_ready, 1)
                        if what == "ctx":
                            for c in range(2):
                                act.wait_ge(cT_written, 2 * n + c + 1)
                                act.activation(cT[:, c, 0, :], front[c][0:CF, 0:C], ACT.Copy).then_inc(cT_ready, 1)
                        if what == "xT":
                            act.wait_ge(xT_written, n + 1)
                            act.activation(xT[:].rearrange("p c s -> p (c s)"), mix[:, 0:DC * S], ACT.Copy)\
                               .then_inc(xT_ready, 1)
                        if what == "q1T":
                            act.wait_ge(q1T_written, n + 1)
                            act.activation(q1T[:, m, :, :].rearrange("p c s -> p (c s)"), mixh[:, 0:NC * S],
                                           ACT.Copy).then_inc(q1T_ready, 1)
                        if what == "q2T":
                            at, par = (b, k) if j else (n, m)
                            act.wait_ge(q2T_written, 2 * at + j + 1)
                            act.activation(q2T[:, par, 2 * j:2 * j + 2, :].rearrange("p c s -> p (c s)"),
                                           mixh[:, 0:2 * S], ACT.Copy).then_inc(q2T_ready, 1)
                        if what == "k":
                            act.wait_ge(k_written, NC * n + j + 1)
                            after(act, k1_ready, NC * n + j - 1)
                            act.activation(khi[:, j % 2, :], front[j % 2][:, 0:C], ACT.Identity,
                                           bias=core.col("bk", j)).then_inc(khi_ready, 1)
                        if what == "v":
                            act.wait_ge(v_written, CT * n + j + 1)
                            after(act, v_ready, CT * n + j - 1)
                            act.activation(vf[:, j % 2, :], front[j % 2][0:CP, 0:D], ACT.Copy).then_inc(v_step, 1)
                            act.wait_ge(v_step, 2 * (CT * n + j) + 1)
                            act.activation(v[:, m, j, :, 0:HD1],
                                           vf[:, j % 2, :].rearrange("p (h d) -> p h d", d=HD1), ACT.Copy)\
                               .then_inc(v_step, 1)

                rounds(act, one_round, 0, B)

            @block.tensor
            def _(pe):
                idc, ids = core.ident[0:CP, 0:CP], core.ident[0:S, 0:S]
                terms = [(c, w, z) for c in range(2) for w, z in ((wh, 0), (wh, 1), (wl, 0))]
                pe.wait_ge(loaded, 48)
                pe.wait_ge(const, 6)
                pe.wait_ge(w_ready, 2)

                def one_round(b, k, heads_on, front_on, tail_on):
                    n, m = b + 1, 1 - k
                    on = {"H": heads_on, "F": front_on, "T": tail_on}
                    for part, what, j in XA1_ORDER:
                        if not on[part]:
                            continue
                        if what == "st":
                            r, c = PAD * (j % HG), j // HG
                            pe.wait_ge(q2T_ready, 2 * b + 1 + j // 8)
                            after(pe, probs_ready, H1 * b + j - 1)
                            for t in range(CT):
                                o, at = stb[j % 2][0:CP, t * S:(t + 1) * S], slice(t * CP, (t + 1) * CP)
                                pe.matmul(o, k1[r:r + PAD, k, c, at], q1T[r:r + PAD, k, c, :], start=True,
                                          stop=False, tile_position=(r, 0))
                                last = pe.matmul(o, k2[r:r + PAD, k, c, at], q2T[r:r + PAD, k, c, :], start=False,
                                                 stop=True, tile_position=(r, 0))
                            last.then_inc(st_written, 1)
                        if what == "pv":
                            pe.wait_ge(pl_ready, H1 * b + j + 1)
                            if j == 0:
                                pe.wait_ge(v_ready, CT * (b + 1))
                            if j == 0:
                                after(pe, heads_ready, 3 * b - 1)
                            if j == H1 // 2:
                                pe.wait_ge(heads_ready, 3 * b + 1)
                            o = outb[0:S, j % 8 * 2 * VW:(j % 8 + 1) * 2 * VW]
                            at = [slice(t * S, (t + 1) * S) for t in range(CT)]
                            for t in range(CT):
                                ends = (t == 0, t == CT - 1)
                                if t == CT - 1:
                                    pe.matmul(o[:, 0:VW], pl[:, j % NP, at[t]], v[:, k, t, j, 0:VW], start=False,
                                              stop=False, skip_group_check=True)
                                last = pe.matmul(o, ph[:, j % NP, at[t]], v[:, k, t, j, :], start=ends[0],
                                                 stop=ends[1])
                                if t < CT - 1:
                                    pe.matmul(o[:, 0:VW], pl[:, j % NP, at[t]], v[:, k, t, j, 0:VW], start=False,
                                              stop=False, skip_group_check=True)
                            last.then_inc(pv_written, 1)
                        if what == "hT":
                            pe.wait_ge(heads_ready, 3 * b)
                            if heads_on:
                                pe.wait_ge(q2T_ready, 2 * b + 1)
                            for c in range(DC):
                                last = pe.transpose(mix[:, c * S:(c + 1) * S], heads[:, c * 128:(c + 1) * 128], ids)
                            last.then_inc(headsT_written, 1)
                        if what == "wo":
                            pe.wait_ge(headsT_ready, b)
                            if front_on:
                                pe.wait_ge(xT_ready, n + 1)
                            elif heads_on:
                                pe.wait_ge(q2T_ready, 2 * b + 2)
                            for c in range(DC):
                                last = pe.matmul(mix[0:S, 0:D], headsT[:, c, :], wo[:, c, :], start=(c == 0),
                                                 stop=(c == DC - 1))
                            last.then_inc(wo_written, 1)
                        if what == "ctx":
                            pe.wait_ge(cx_in, 16 * n + 16)
                            after(pe, v_step, 2 * CT * n)
                            for c in range(2):
                                for t in range(CT):
                                    last = pe.transpose(front[c][0:CF, t * CP:(t + 1) * CP],
                                                        cx[:, t, c * CF:(c + 1) * CF], idc)
                                last.then_inc(cT_written, 1)
                        if what == "xT":
                            pe.wait_ge(normed, n + 1)
                            after(pe, q2T_ready, 2 * n)
                            for c in range(DC):
                                last = pe.transpose(mix[:, c * S:(c + 1) * S], xn[:, c * 128:(c + 1) * 128], ids)
                            last.then_inc(xT_written, 1)
                        if what == "q":
                            pe.wait_ge(xT_ready, n + 1)
                            if tail_on:
                                pe.wait_ge(x_updated, 2 * b - 1)
                            for c in range(DC):
                                last = pe.matmul(mix[0:S, 0:D], xT[:, c, :], wq[:, c, :], start=(c == 0),
                                                 stop=(c == DC - 1))
                            last.then_inc(q_written, 1)
                        if what == "q1T":
                            pe.wait_ge(q_ready, n + 1)
                            for c in range(NC):
                                last = pe.transpose(mixh[:, c * S:(c + 1) * S],
                                                    q1[:, HG * c:HG * (c + 1), :].rearrange("p h d -> p (h d)"),
                                                    identh[:])
                            last.then_inc(q1T_written, 1)
                        if what == "q2T":
                            at = b if j else n
                            pe.wait_ge(m_ready, NC * at + 2 * j + 2)
                            if j:
                                pe.wait_ge(q2T_ready, 2 * b + 1)
                                after(pe, headsT_ready, b)
                            else:
                                pe.wait_ge(q1T_ready, n + 1)
                            for c in range(2 * j, 2 * j + 2):
                                last = pe.transpose(mixh[:, (c - 2 * j) * S:(c - 2 * j + 1) * S],
                                                    q2[:, HG * c:HG * (c + 1), :].rearrange("p h d -> p (h d)"),
                                                    identh[:])
                            last.then_inc(q2T_written, 1)
                        if what == "k":
                            pe.wait_ge(cTl_ready, 2 * n + 2)
                            if j >= 2:
                                pe.wait_ge(k1_ready, NC * n + j - 1)
                            for q, (c, w, z) in enumerate(terms):
                                last = pe.matmul(front[j % 2][:, 0:C], w[:, c, j * 128:(j + 1) * 128],
                                                 cT[:, c, z, :], start=(q == 0), stop=(q == len(terms) - 1))
                            last.then_inc(k_written, 1)
                        if what == "v":
                            if j < 2:
                                pe.wait_ge(k1_ready, NC * n + 3 + j)
                            else:
                                pe.wait_ge(v_step, 2 * CT * n + 1)
                            for q, (c, w, z) in enumerate(terms):
                                last = pe.matmul(front[j % 2][0:CP, 0:D], cT[:, c, z, j * CP:(j + 1) * CP],
                                                 w[:, c, H1 * PAD:], start=(q == 0), stop=(q == len(terms) - 1))
                            last.then_inc(v_written, 1)
                        if what == "max":
                            pe.wait_ge(q1T_ready, n + 1)
                            pe.wait_ge(k1_ready, NC * n + j + 1)
                            pe.wait_ge(k2_ready, NC * n + j + 1)
                            for r in range(HG):
                                after(pe, top_ready, H1 * n + HG * j + r - 1)
                                at = slice(PAD * r, PAD * (r + 1))
                                pe.matmul(maxb[r % 2][0:S, 0:C], q1T[at, m, j, :], k1[at, m, j, :], start=True,
                                          stop=True, tile_position=(PAD * r, 0)).then_inc(max_written, 1)

                rounds(pe, one_round, 0, B)


SA_ORDER = [
    ("F", "norm", 0), ("H", "sc", 0), ("H", "sc", 1), ("T", "hT", 0), ("F", "x", 0), ("H", "sc", 2), ("T", "wo", 0), ("H", "pt", 0),
    ("F", "v", 0), ("F", "qk", 0), ("H", "sc", 3), ("H", "pv", 0), ("H", "pt", 1), ("T", "hn", 0), ("F", "qkT", 0),
    ("H", "pv", 1), ("H", "pt", 2), ("F", "qkT", 1), ("T", "router", 0), ("H", "pv", 2), ("H", "pt", 3),
    ("H", "pv", 3), ("H", "out", 0),
]


def l1_self_attn_stage(core, keep):
    nc, inp = core.nc, core.inp
    NC = H1 // HG
    core.base = keep("base", [S, B, D])
    core.hT = keep("hT", [128, 2, DC, B * S], F16)
    core.logits = keep("logits", [S, B, E1])
    with Stage(core, "sa") as st:
        mean, ve, rstd, ms, rms = (st.sb(n, [S, B]) for n in ("mean", "ve", "rstd", "ms", "rms"))
        stats_stage(core, "sa_s", core.x, S, B, mean[:], ve[:], rstd[:])
        wqk = st.sb("wqk", [128, DC, 2 * D])
        wv = st.sb("wv", [128, DC, D])
        wo = st.sb("wo", [128, DC, D])
        router = st.sb("router", [128, DC, E1])
        freqs = st.sb("freqs", [S, HD1])
        cosr, sinr = st.sb("cosr", [S, HD1]), st.sb("sinr", [S, HD1])
        causal = st.sb("causal", [S, S])
        xr = st.sb("xr", [S, D])
        xT = st.sb("xT", [128, DC, S])
        t1, t2 = st.sb("t1", [S, 2 * D]), st.sb("t2", [S, 2 * D])
        qk = st.sb("qk", [S, 2 * H1, PAD])
        qkT = st.sb("qkT", [128, 2, 2 * NC, S])
        v = st.sb("v", [S, 2, D])
        sm = st.sb("sm", [S, H1, S])
        top = st.sb("top", [S, H1])
        probs = st.sb("probs", [S, H1, S])
        total, rtotal = st.sb("total", [S, H1]), st.sb("rtotal", [S, H1])
        pT = st.sb("pT", [S, NC, HG * S])
        heads = st.sb("heads", [S, D])
        headsT = st.sb("headsT", [128, DC, S])
        sq = st.sb("sq", [S, D])
        hss, hrr = st.sb("hss", [S, 1]), st.sb("hrr", [S, 1])
        h = st.sb("h", [S, D])
        hn = st.sb("hn", [S, D])
        hTf = st.sb("hTf", [128, DC, S])
        scoreb = [st.bank("score0"), st.bank("score1")]
        probb = [st.bank("prob0"), st.bank("prob1")]
        fa, fb, po, pm = st.bank("fa"), st.bank("fb"), st.bank("po"), st.bank("pm")
        (loaded, ready_once, n_ready, xr_ready, xT_written, xT_ready, qk_written, qk_step, qk_ready, v_written,
         v_ready, qkT_written, qkT_ready, score_written, sm_ready, top_ready, probs_ready, pT_written, pT_ready,
         out_written, heads_ready, headsT_written, headsT_ready, wo_written, h_ready, hss_ready, hrr_ready, hn_ready,
         hnT_written, hTf_ready, hTh_ready, router_written, dve_step, hT_kept, held) = (st.sem(n) for n in
            "loaded ready_once n_ready xr_ready xT_written xT_ready qk_written qk_step qk_ready v_written "
            "v_ready qkT_written qkT_ready score_written sm_ready top_ready probs_ready pT_written pT_ready "
            "out_written heads_ready headsT_written headsT_ready wo_written h_ready hss_ready hrr_ready hn_ready "
            "hnT_written hTf_ready hTh_ready router_written dve_step hT_kept held".split())
        with nc.Block() as block:

            @block.sync
            def _(sp):
                for dst, src in ((wqk, "s_wqk"), (wv, "s_wv"), (wo, "s_wo"), (router, "router")):
                    sp.dma_start(dst[:], inp[src].rearrange("(c p) n -> p c n", p=128)).then_inc(loaded, 16)
                sp.dma_start(freqs[:], inp["freqs"][0:S, :]).then_inc(loaded, 16)
                sp.dma_start(causal[:], inp["causal"]).then_inc(loaded, 16)
                sp.wait_ge(loaded, 96)

            @block.vector
            def _(dve):
                step = Chain(dve, dve_step)
                dve.wait_ge(loaded, 96)
                pair = lambda a: a[:].rearrange("p (k two) -> p k two", two=2)
                cos, sin = pair(freqs)[:, :, 0:1], pair(freqs)[:, :, 1:2]
                step(dve.tensor_copy(pair(cosr), cos.broadcast_to([S, HD1 // 2, 2])))
                step(dve.tensor_scalar(pair(sinr)[:, :, 0:1], sin, -1.0, None, ALU.mult))
                step(dve.tensor_copy(pair(sinr)[:, :, 1:2], sin))
                step(dve.memset(qk[:], 0.0))
                step(dve.tensor_scalar(ms[:], ve[:], -LN_EPS, None, ALU.add))
                step(dve.tensor_tensor(ms[:], ms[:], rstd[:], ALU.mult))
                step(dve.tensor_tensor(ms[:], ms[:], rstd[:], ALU.mult))
                dve.tensor_scalar(ms[:], ms[:], RMS_EPS, None, ALU.add).then_inc(ready_once, 1)
                dve.wait_ge(ready_once, 2)

                def one_round(b, k, heads_on, front_on, tail_on):
                    n = b + 1
                    on = {"H": heads_on, "F": front_on, "T": tail_on}
                    for part, what, j in SA_ORDER:
                        if not on[part]:
                            continue
                        if what == "norm":
                            xb = core.x[:, bass.ds(n, 1), :].rearrange("p a c -> p (a c)")
                            nb = core.base[:, bass.ds(n, 1), :].rearrange("p a c -> p (a c)")
                            dve.tensor_scalar(nb, xb, mean[:, bass.ds(n, 1)], rstd[:, bass.ds(n, 1)],
                                              ALU.subtract, ALU.mult).then_inc(n_ready, 1)
                            after(dve, xT_written, n)
                            dve.wait_ge(n_ready, n + 1)
                            dve.tensor_scalar(xr[:], nb, rms[:, bass.ds(n, 1)], None, ALU.mult).then_inc(xr_ready, 1)
                        if what == "qk":
                            dve.wait_ge(qk_written, n + 1)
                            src = fa[0:S, :].rearrange("p (h d) -> p h d", d=HD1)
                            src2 = fa[0:S, :].rearrange("p (h k two) -> p h k two", k=HD1 // 2, two=2)
                            rot = t2[:].rearrange("p (h k two) -> p h k two", k=HD1 // 2, two=2)
                            dve.tensor_tensor(t1[:].rearrange("p (h d) -> p h d", d=HD1), src,
                                              widen(cosr[:], 1, 2 * H1), ALU.mult).then_inc(qk_step, 1)
                            for z in range(2):
                                dve.tensor_tensor(rot[:, :, :, z], src2[:, :, :, 1 - z],
                                                  widen(pair(sinr)[:, :, z], 1, 2 * H1), ALU.mult).then_inc(qk_step, 1)
                            dve.wait_ge(qk_step, 3 * n + 3)
                            dve.tensor_tensor(qk[:, :, 0:HD1], t1[:].rearrange("p (h d) -> p h d", d=HD1),
                                              t2[:].rearrange("p (h d) -> p h d", d=HD1), ALU.add)\
                               .then_inc(qk_ready, 1)
                        if what == "sc":
                            of = slice(j * NC, (j + 1) * NC)
                            dve.wait_ge(score_written, HG * b + j + 1)
                            dve.scalar_tensor_tensor(out=sm[:, of, :],
                                                     in0=scoreb[j % 2][0:S, 0:NC * S].rearrange(
                                                         "p (j s) -> p j s", j=NC),
                                                     scalar=HD1 ** -0.5, in1=widen(causal[:], 1, NC), op0=ALU.mult,
                                                     op1=ALU.add).then_inc(sm_ready, 1)
                            dve.wait_ge(sm_ready, HG * b + j + 1)
                            dve.tensor_reduce(top[:, of], sm[:, of, :], AX.X, ALU.max, negate=True)\
                               .then_inc(top_ready, 1)
                        if what == "pt":
                            dve.wait_ge(pT_written, HG * b + j + 1)
                            dve.tensor_copy(pT[:, j, :], probb[j % 2][0:S, 0:NC * S]).then_inc(pT_ready, 1)
                        if what == "out":
                            dve.wait_ge(probs_ready, H1 * b + H1)
                            dve.reciprocal(rtotal[:], total[:]).then_inc(heads_ready, 1)
                            dve.wait_ge(heads_ready, 2 * b + 1)
                            dve.wait_ge(out_written, b + 1)
                            dve.tensor_tensor(heads[:].rearrange("p (j r d) -> p r j d", r=HG, d=HD1),
                                              po[0:S, 0:D].rearrange("p (r j d) -> p r j d", r=HG, d=HD1),
                                              widen(rtotal[:].rearrange("p (r j) -> p r j", r=HG), 3, HD1), ALU.mult)\
                               .then_inc(heads_ready, 1)
                        if what == "wo":
                            nb = core.base[:, bass.ds(b - 1, 1), :].rearrange("p a c -> p (a c)")
                            dve.wait_ge(wo_written, b)
                            dve.tensor_tensor(h[:], nb, pm[0:S, 0:D], ALU.add).then_inc(h_ready, 1)
                            dve.wait_ge(h_ready, b)
                            dve.sem_inc(held, 1)
                            dve.tensor_tensor_reduce(out=sq[:], in0=h[:], in1=h[:], scale=1.0, scalar=0.0,
                                                     op0=ALU.mult, op1=ALU.add, accum_out=hss[:])\
                               .then_inc(hss_ready, 1)
                            dve.wait_ge(hss_ready, 2 * b - 1)
                            dve.tensor_scalar(hss[:], hss[:], 1.0 / D, RMS_EPS, ALU.mult, ALU.add)\
                               .then_inc(hss_ready, 1)
                            dve.tensor_scalar(nb, h[:], 1.0, None, ALU.mult)
                        if what == "pt" and j == 0 and tail_on:
                            dve.wait_ge(hrr_ready, b)
                            dve.tensor_scalar(hn[:], h[:], hrr[:], None, ALU.mult).then_inc(hn_ready, 1)
                        if what == "hn" and not heads_on:
                            dve.wait_ge(hrr_ready, b)
                            dve.tensor_scalar(hn[:], h[:], hrr[:], None, ALU.mult).then_inc(hn_ready, 1)
                        if what == "router":
                            dve.wait_ge(hTf_ready, 2 * b)
                            hi, lo = (core.hT[:, z, :, bass.ds((b - 1) * S, S)] for z in range(2))
                            dve.tensor_scalar(hi, hTf[:], 1.0, None, ALU.mult).then_inc(hTh_ready, 1)
                            dve.wait_ge(hTh_ready, b)
                            dve.tensor_tensor(lo, hTf[:], hi, ALU.subtract).then_inc(hT_kept, 1)
                            dve.wait_ge(router_written, b)
                            dve.tensor_scalar(core.logits[:, bass.ds(b - 1, 1), :].rearrange("p a e -> p (a e)"),
                                              pm[0:S, 0:E1], 1.0, None, ALU.mult).then_inc(hT_kept, 1)

                rounds(dve, one_round, 0, B)

            @block.gpsimd
            def _(pool):
                pool.wait_ge(ready_once, 1)
                pool.tensor_tensor(rms[:], ms[:], core.half[0:S, 0:B], ALU.pow).then_inc(ready_once, 1)
                with pool.Fori(0, B) as b:
                    pool.wait_ge(hss_ready, 2 * b + 2)
                    pool.tensor_tensor(hrr[:], hss[:], core.half[0:S, 0:1], ALU.pow).then_inc(hrr_ready, 1)

            @block.scalar
            def _(act):

                def one_round(b, k, heads_on, front_on, tail_on):
                    n, m = b + 1, 1 - k
                    on = {"H": heads_on, "F": front_on, "T": tail_on}
                    for part, what, j in SA_ORDER:
                        if not on[part]:
                            continue
                        if what == "x":
                            act.wait_ge(xT_written, n + 1)
                            for c in range(DC):
                                act.activation(xT[:, c, :], fb[:, c * S:(c + 1) * S], ACT.Copy,
                                               scale=core.col("attn_w", c)).then_inc(xT_ready, 1)
                        if what == "v":
                            act.wait_ge(v_written, n + 1)
                            act.activation(v[:, m, :], fb[0:S, 0:D], ACT.Copy).then_inc(v_ready, 1)
                        if what == "qkT":
                            act.wait_ge(qkT_written, 2 * n + j + 1)
                            act.activation(qkT[:, m, j * NC:(j + 1) * NC, :].rearrange("p c s -> p (c s)"),
                                           (fa, fb)[j][:, 0:NC * S], ACT.Copy).then_inc(qkT_ready, 1)
                        if what == "sc":
                            act.wait_ge(top_ready, HG * b + j + 1)
                            for h in range(NC * j, NC * (j + 1)):
                                act.activation(probs[:, h, :], sm[:, h, :], ACT.Exp, bias=top[:, h:h + 1],
                                               accum_out=total[:, h:h + 1]).then_inc(probs_ready, 1)
                        if what == "hT":
                            act.wait_ge(headsT_written, b)
                            act.activation(headsT[:].rearrange("p c s -> p (c s)"), pm[:, 0:DC * S], ACT.Copy)\
                               .then_inc(headsT_ready, 1)
                        if what == "hn":
                            act.wait_ge(hnT_written, b)
                            for c in range(DC):
                                act.activation(hTf[:, c, :], pm[:, c * S:(c + 1) * S], ACT.Copy,
                                               scale=core.col("ffn_w", c)).then_inc(hTf_ready, 1)

                rounds(act, one_round, 0, B)

            @block.tensor
            def _(pe):
                ids = core.ident[0:S, 0:S]
                pe.wait_ge(loaded, 96)

                def one_round(b, k, heads_on, front_on, tail_on):
                    n, m = b + 1, 1 - k
                    on = {"H": heads_on, "F": front_on, "T": tail_on}
                    for part, what, j in SA_ORDER:
                        if not on[part]:
                            continue
                        if what == "x":
                            pe.wait_ge(xr_ready, n + 1)
                            after(pe, qkT_ready, 2 * n)
                            for c in range(DC):
                                last = pe.transpose(fb[:, c * S:(c + 1) * S], xr[:, c * 128:(c + 1) * 128], ids)
                            last.then_inc(xT_written, 1)
                        if what == "v":
                            pe.wait_ge(xT_ready, 2 * n + 2)
                            for c in range(DC):
                                last = pe.matmul(fb[0:S, 0:D], xT[:, c, :], wv[:, c, :], start=(c == 0),
                                                 stop=(c == DC - 1))
                            last.then_inc(v_written, 1)
                        if what == "qk":
                            for c in range(DC):
                                last = pe.matmul(fa[0:S, :], xT[:, c, :], wqk[:, c, :], start=(c == 0),
                                                 stop=(c == DC - 1))
                            last.then_inc(qk_written, 1)
                        if what == "qkT":
                            pe.wait_ge(qk_ready if j == 0 else v_ready, n + 1)
                            for c in range(NC):
                                q = j * NC + c
                                last = pe.transpose((fa, fb)[j][:, c * S:(c + 1) * S],
                                                    qk[:, q * HG:(q + 1) * HG, :].rearrange("p h d -> p (h d)"), ids)
                            last.then_inc(qkT_written, 1)
                        if what == "sc":
                            if j == 0:
                                pe.wait_ge(qkT_ready, 2 * b + 2)
                            after(pe, sm_ready, HG * b + j - 1)
                            at = slice(PAD * j, PAD * j + HD1)
                            for c in range(NC):
                                last = pe.matmul(scoreb[j % 2][0:S, c * S:(c + 1) * S], qkT[at, k, c, :],
                                                 qkT[at, k, NC + c, :], start=True, stop=True,
                                                 tile_position=(PAD * j, 0))
                            last.then_inc(score_written, 1)
                        if what == "pt":
                            pe.wait_ge(probs_ready, H1 * b + NC * (j + 1))
                            after(pe, pT_ready, HG * b + j - 1)
                            for c in range(NC):
                                last = pe.transpose(probb[j % 2][0:S, c * S:(c + 1) * S], probs[:, j * NC + c, :],
                                                    ids)
                            last.then_inc(pT_written, 1)
                        if what == "pv":
                            pe.wait_ge(pT_ready, HG * b + j + 1)
                            if j == 0:
                                pe.wait_ge(v_ready, b + 1)
                                after(pe, heads_ready, 2 * b)
                            for c in range(NC):
                                h, o = HG * c + j, (j * NC + c) * HD1
                                last = pe.matmul(po[0:S, o:o + HD1], pT[:, j, c * S:(c + 1) * S],
                                                 v[:, k, h * HD1:(h + 1) * HD1], start=True, stop=True)
                            if j == HG - 1:
                                last.then_inc(out_written, 1)
                        if what == "hT":
                            pe.wait_ge(heads_ready, 2 * b)
                            after(pe, hT_kept, 2 * (b - 1))
                            for c in range(DC):
                                last = pe.transpose(pm[:, c * S:(c + 1) * S], heads[:, c * 128:(c + 1) * 128], ids)
                            last.then_inc(headsT_written, 1)
                        if what == "wo":
                            pe.wait_ge(headsT_ready, b)
                            for c in range(DC):
                                last = pe.matmul(pm[0:S, 0:D], headsT[:, c, :], wo[:, c, :], start=(c == 0),
                                                 stop=(c == DC - 1))
                            last.then_inc(wo_written, 1)
                        if what == "hn":
                            pe.wait_ge(hn_ready, b)
                            for c in range(DC):
                                last = pe.transpose(pm[:, c * S:(c + 1) * S], hn[:, c * 128:(c + 1) * 128], ids)
                            last.then_inc(hnT_written, 1)
                        if what == "router":
                            pe.wait_ge(hTf_ready, 2 * b)
                            for c in range(DC):
                                last = pe.matmul(pm[0:S, 0:E1], hTf[:, c, :], router[:, c, :], start=(c == 0),
                                                 stop=(c == DC - 1))
                            last.then_inc(router_written, 1)

                rounds(pe, one_round, 0, B)


def experts1_stage(core, keep):
    nc, inp = core.nc, core.inp
    FC = F1 // 128
    SEQ = 4
    NB = B // SEQ
    W = SEQ * S
    NJ = FC * NB
    with Stage(core, "ex1") as st:
        combine = st.sb("combine", [S, B, E1])
        l2, eq, run, sel = (st.sb(n, [S, B, E1]) for n in ("l2", "eq", "run", "sel"))
        mx, tot = st.sb("mx", [S, B]), st.sb("tot", [S, B])
        wf = [st.sb("w1f", [128, DC * F1]), st.sb("w3f", [128, DC * F1]), st.sb("w2f", [128, FC * D])]
        w = [st.sb(n, [128, 2, 2, 1024], F16) for n in ("w1", "w3", "w2")]
        g = st.sb("g", [128, 2, W])
        p = st.sb("p", [128, 2, W])
        ph = st.sb("ph", [128, 2, FC, B * S], F16)
        ub = [st.bank("u0"), st.bank("u1")]
        zb = [st.bank("z0"), st.bank("z1")]
        yb = [st.bank(f"y{n}") for n in range(4)]
        (w_in, w_split, u_written, z_written, g_ready, p_ready, ph_ready, pl_ready, y_written, x_updated, dve_step,
         exp_ready, diff_ready, held) = (st.sem(n) for n in
            "w_in w_split u_written z_written g_ready p_ready ph_ready pl_ready y_written x_updated dve_step "
            "exp_ready diff_ready held".split())
        with nc.Block() as block:

            @block.sync
            def _(sp):
                with sp.Fori(0, E1 // 2) as i:
                    for k in range(2):
                        e = 2 * i + k
                        sp.wait_ge(w_split, 6 * e + 6)
                        sp.wait_ge(x_updated, B * e + 4)
                        for dst, name in zip(wf, ("m_w1", "m_w3", "m_w2")):
                            sp.dma_start(dst[:].rearrange("p (c f) -> p c f", f=F1 if name != "m_w2" else D),
                                         inp[name][bass.ds(e, 1), :, :].rearrange("a (c p) f -> p (a c) f", p=128))\
                              .then_inc(w_in, 16)

            @block.gpsimd
            def _(pool):
                pool.sem_inc(w_split, 6)
                with pool.Fori(0, E1 // 2) as i:
                    for k in range(2):
                        e = 2 * i + k
                        pool.wait_ge(w_in, 48 * e + 48)
                        pool.sem_inc(held, 1)
                        for n in range(3):
                            pool.tensor_copy(w[n][:, k, 0, :], wf[n][:]).then_inc(w_split, 1)
                        pool.wait_ge(w_split, 6 * e + 9)
                        for n in range(3):
                            pool.tensor_tensor(w[n][:, k, 1, :], wf[n][:], w[n][:, k, 0, :], ALU.subtract)\
                                .then_inc(w_split, 1)

            @block.vector
            def _(dve):
                dve.sem_inc(x_updated, B + 4)
                dve.sem_inc(p_ready, 2)
                dve.sem_inc(pl_ready, 2)
                step = Chain(dve, dve_step)
                step(dve.tensor_reduce(mx[:], core.logits[:], AX.X, ALU.max))
                dve.tensor_tensor(l2[:], core.logits[:], widen(mx[:], 2, E1), ALU.subtract).then_inc(diff_ready, 1)
                dve.wait_ge(diff_ready, 1)
                step(dve.memset(sel[:], 0.0))
                for n in range(TOP):
                    step(dve.tensor_reduce(mx[:], l2[:], AX.X, ALU.max))
                    step(dve.tensor_tensor(eq[:], l2[:], widen(mx[:], 2, E1), ALU.is_equal))
                    step(dve.tensor_copy(run[:, :, 0:1], eq[:, :, 0:1]))
                    for c in range(1, E1):
                        step(dve.tensor_tensor(run[:, :, c:c + 1], run[:, :, c - 1:c], eq[:, :, c:c + 1], ALU.add))
                    step(dve.tensor_scalar(run[:], run[:], 1.0, None, ALU.is_equal))
                    step(dve.tensor_tensor(eq[:], eq[:], run[:], ALU.mult))
                    step(dve.tensor_tensor(sel[:], sel[:], eq[:], ALU.add))
                    if n == 0:
                        dve.wait_ge(exp_ready, 1)
                    step(dve.scalar_tensor_tensor(out=l2[:], in0=eq[:], scalar=-MASKED, in1=l2[:], op0=ALU.mult,
                                                  op1=ALU.add))
                step(dve.tensor_tensor(combine[:], combine[:], sel[:], ALU.mult))
                step(dve.tensor_reduce(tot[:], combine[:], AX.X, ALU.add))
                step(dve.reciprocal(tot[:], tot[:]))
                step(dve.tensor_scalar(tot[:], tot[:], core.gate[0:S, 3:4], None, ALU.mult))
                step(dve.tensor_tensor(combine[:], combine[:], widen(tot[:], 2, E1), ALU.mult))
                step(dve.scalar_tensor_tensor(out=core.x[:], in0=core.base[:], scalar=core.gate[0:S, 3:4],
                                              in1=core.x[:], op0=ALU.mult, op1=ALU.add))
                with dve.Fori(0, E1 // 2) as i:
                    for k in range(2):
                        e = 2 * i + k

                        def low_half(j):
                            f, n = j % FC, j // FC
                            at = slice(n * W, (n + 1) * W)
                            dve.wait_ge(ph_ready, NJ * e + j + 1)
                            dve.tensor_tensor(ph[:, 1, f, at], p[:, j % 2, :], ph[:, 0, f, at], ALU.subtract)\
                               .then_inc(pl_ready, 1)

                        for j in range(NJ):
                            dve.wait_ge(z_written, NJ * e + j + 1)
                            dve.wait_ge(g_ready, NJ * e + j + 3)
                            dve.wait_ge(pl_ready, NJ * e + j + 1)
                            dve.tensor_tensor(p[:, j % 2, :], zb[j % 2][:, 0:W], g[:, j % 2, :], ALU.mult)\
                               .then_inc(p_ready, 1)
                            if j >= 1:
                                low_half(j - 1)
                        low_half(NJ - 1)
                        for b in range(B):
                            dve.wait_ge(y_written, B * e + b + 1)
                            dve.scalar_tensor_tensor(
                                out=core.x[:, b, :], in0=yb[b % 4][0:S, 0:D],
                                scalar=combine[:, b, :][:, bass.ds(e, 1)], in1=core.x[:, b, :],
                                op0=ALU.mult, op1=ALU.add).then_inc(x_updated, 1)

            @block.scalar
            def _(act):
                act.sem_inc(g_ready, 2)
                act.wait_ge(diff_ready, 1)
                act.activation(combine[:], l2[:], ACT.Exp).then_inc(exp_ready, 1)
                with act.Fori(0, E1 // 2) as i:
                    for k in range(2):
                        e = 2 * i + k

                        def silu(j):
                            act.wait_ge(u_written, NJ * e + j + 1)
                            act.wait_ge(p_ready, NJ * e + j + 1)
                            act.activation(g[:, j % 2, :], ub[j % 2][:, 0:W], ACT.Silu).then_inc(g_ready, 1)

                        silu(0)
                        for j in range(NJ):
                            if j + 1 < NJ:
                                silu(j + 1)
                            f, n = j % FC, j // FC
                            act.wait_ge(p_ready, NJ * e + j + 3)
                            act.activation(ph[:, 0, f, n * W:(n + 1) * W], p[:, j % 2, :], ACT.Copy)\
                               .then_inc(ph_ready, 1)

            @block.tensor
            def _(pe):
                three = ((0, 0), (0, 1), (1, 0))
                with pe.Fori(0, E1 // 2) as i:
                    for k in range(2):
                        e = 2 * i + k
                        pe.wait_ge(w_split, 6 * e + 12)
                        for j in range(NJ):
                            f, n = j % FC, j // FC
                            terms = [(c, a, z) for c in range(DC) for a, z in three]
                            for m, banks, ready, written in ((0, ub, g_ready, u_written), (1, zb, p_ready, z_written)):
                                pe.wait_ge(ready, NJ * e + j + 1)
                                for q, (c, a, z) in enumerate(terms):
                                    last = pe.matmul(banks[j % 2][:, 0:W],
                                                     w[m][:, k, a, c * F1 + f * 128:c * F1 + (f + 1) * 128],
                                                     core.hT[:, z, c, n * W:(n + 1) * W], start=(q == 0),
                                                     stop=(q == len(terms) - 1))
                                last.then_inc(written, 1)
                        for b in range(B):
                            pe.wait_ge(pl_ready, NJ * e + FC * (b // SEQ + 1) + 2)
                            pe.wait_ge(x_updated, B * e + B + b + 1)
                            terms = [(f, a, z) for f in range(FC) for a, z in three]
                            for q, (f, a, z) in enumerate(terms):
                                last = pe.matmul(yb[b % 4][0:S, 0:D], ph[:, a, f, b * S:(b + 1) * S],
                                                 w[2][:, k, z, f * D:(f + 1) * D], start=(q == 0),
                                                 stop=(q == len(terms) - 1))
                            last.then_inc(y_written, 1)



def build(nc, inputs, out):
    core = Core(nc, inputs, out)
    with core.stack:
        with core.ctx_stack:
            load_stage(core)
            l0_xattn_stage(core)
        for stages in ((routing_stage, experts0_stage), (l1_xattn_stage,), (l1_self_attn_stage, experts1_stage)):
            with ExitStack() as kept:
                def keep(name, shape, dt=F32):
                    return kept.enter_context(nc.sbuf_tensor(name, shape, dt))

                for stage in stages:
                    stage(core, keep)
            core.clear_semaphores()
        store_stage(core)


def store_stage(core):
    with core.nc.Block() as block:

        @block.sync
        def _(sp):
            sp.dma_start(core.out.rearrange("b s d -> s b d"), core.x[:]).then_inc(core.stored, 16)
            sp.wait_ge(core.stored, 16)


def kernel(**inputs):
    import numpy as _np
    import concourse.bacc as _bacc
    from concourse import mybir as _mybir
    from concourse.bass_utils import run_bass_kernel_spmd as _run

    def take(name):
        return _np.asarray(inputs[name])

    def column(a, parts):
        out = _np.zeros((128, a.size // parts), _np.float32)
        out[:parts] = a.reshape(-1, parts).T
        return out

    def doubled(a):
        heads = a.reshape(*a.shape[:-1], H1, 1, HD1)
        return _np.repeat(heads, 2, -2).reshape(*a.shape[:-1], H1 * PAD)

    places = _np.arange(128) % PAD
    cols = {
        "lnx_g": column(take("L0_xattn_ln_x_g"), CF), "lnx_b": column(take("L0_xattn_ln_x_b"), CF),
        "lnl_g": column(take("L0_xattn_ln_l_g"), 128), "lnl_b": column(take("L0_xattn_ln_l_b"), 128),
        "qn_g": _np.tile(take("L0_xattn_qn_g"), 2)[:, None], "kn_g": _np.tile(take("L0_xattn_kn_g"), 2)[:, None],
        "bk": column(doubled(take("L1_xattn_bk")), 128),
        "pad_masks": _np.stack([places >= HD1, places < HD1, places == HD1], 1).astype(_np.float32),
        "attn_w": column(take("L1_ffn_attn_norm_w"), 128), "ffn_w": column(take("L1_ffn_ffn_norm_w"), 128),
    }
    rows = {
        "g_xattn": take("g_xattn"), "g_ffn": take("g_ffn"), "log_temp": take("L0_ffn_log_temp").reshape(1),
        "bo0": take("L0_xattn_bo"), "bo1": take("L1_xattn_bo"), "bv1": take("L1_xattn_bv"), "bq1": take("L1_xattn_bq"),
        "iota": _np.arange(CAP, dtype=_np.float32),
    }
    wlkv = take("L0_xattn_Wlkv")
    arrays = {
        "x": take("x"),
        "ctx": take("ctx_768"),
        "mask": take("mask_BxS2_bk0").reshape(1, B * C),
        "ident": _np.eye(128, dtype=_np.float32),
        "cols": _np.concatenate([cols[n] for n in COLS], 1),
        "rows": _np.concatenate([rows[n] for n in ROWS])[None, :],
        "w0kv": take("L0_xattn_Wkv").T,
        "w0l": _np.concatenate([wlkv[:D], take("L0_xattn_Wq"), wlkv[D:]]).T,
        "w0o": take("L0_xattn_Wo").T,
    }
    arrays.update(more_arrays(take, doubled, _np))
    arrays = {f"in_{n}": _np.ascontiguousarray(a) for n, a in arrays.items()}
    nc = _bacc.Bacc("TRN2", target_bir_lowering=False, num_devices=1)
    given = {n[3:]: nc.dram_tensor(n, a.shape, _mybir.dt.from_np(a.dtype), kind="ExternalInput").ap()
             for n, a in arrays.items()}
    out = nc.dram_tensor("out", (B, S, D), F32, kind="ExternalOutput").ap()
    build(nc, given, out)
    r = _run(nc, [arrays], core_ids=[0])
    return r.results[0]["out"]


def more_arrays(take, doubled, np):
    return {
        "w1q": take("L1_xattn_Wq"), "w1kv": np.concatenate([doubled(take("L1_xattn_Wk")), take("L1_xattn_Wv")], 1),
        "w1o": take("L1_xattn_Wo"),
        "s_wqk": np.concatenate([take("L1_ffn_wq"), take("L1_ffn_wk")], 1), "s_wv": take("L1_ffn_wv"),
        "s_wo": take("L1_ffn_wo"), "router": take("L1_ffn_router_w"), "freqs": take("L1_ffn_freqs_cis"),
        "causal": np.triu(np.full((S, S), NEG, np.float32), 1),
        "m_w1": take("L1_ffn_w1"), "m_w3": take("L1_ffn_w3"), "m_w2": take("L1_ffn_w2"),
        "gate_query": take("L0_ffn_gate_query").T,
        "w1": take("L0_ffn_w1"), "w2": take("L0_ffn_w2"),
        "b1": take("L0_ffn_b1").reshape(E0, F0 // 128, 128).transpose(0, 2, 1), "b2": take("L0_ffn_b2"),
    }
```

```python
from contextlib import ExitStack

import concourse.bass as bass
from concourse import mybir

F32 = mybir.dt.float32
F16 = mybir.dt.float16
U8 = mybir.dt.uint8
ALU = mybir.AluOpType
ACT = mybir.ActivationFunctionType
AX = mybir.AxisListType

B, S, D = 16, 112, 256
C, CD = 375, 192
CT, CP = 3, 125
CF = CD // 2
DC = D // 128
H0, HD0 = 4, 64
KEYS0 = C + S
H1, HD1 = 16, 16
PAD = 32
HG = 128 // PAD
E0, F0, CAP = 16, 1024, 64
SINKHORN = 6
E1, F1, TOP = 8, 512, 2
LN_EPS = 1e-5
RMS_EPS = 1e-6
RMS_MIN_SQ = 1e-16
NEG = -1e9
MASKED = 1e30

COLS, ROWS = {}, {}
for _name, _n in (("lnx_g", 2), ("lnx_b", 2), ("lnl_g", 2), ("lnl_b", 2), ("qn_g", 1), ("kn_g", 1),
                  ("bk", 4), ("pad_masks", 3), ("attn_w", 2), ("ffn_w", 2)):
    COLS[_name] = (sum(n for _, n in COLS.values()), _n)
for _name, _n in (("g_xattn", 2), ("g_ffn", 2), ("log_temp", 1), ("bo0", D), ("bo1", D), ("bv1", D), ("bq1", D),
                  ("iota", CAP)):
    ROWS[_name] = (sum(n for _, n in ROWS.values()), _n)
NCOLS = sum(n for _, n in COLS.values())
NROWS = sum(n for _, n in ROWS.values())


def widen(ap, axis, n):
    ap = ap.unsqueeze(axis)
    shape = list(ap.shape)
    shape[axis] = n
    return ap.broadcast_to(shape)


class Chain:

    def __init__(self, eng, sem, base=0):
        self.eng, self.sem, self.base, self.n = eng, sem, base, 0

    def __call__(self, instruction):
        self.n += 1
        instruction.then_inc(self.sem, 1)
        self.eng.wait_ge(self.sem, self.base + self.n)


class Core:

    def __init__(self, nc, inputs, out):
        self.nc, self.inp, self.out = nc, inputs, out
        self.stack, self.ctx_stack = ExitStack(), ExitStack()
        self.spent = []

    def clear_semaphores(self):
        self.nc.clear_and_free_semaphores(self.spent)
        self.nc.all_engine_barrier()
        self.spent = []

    def col(self, name, c=0, n=1, parts=128):
        at = COLS[name][0] + c
        return self.cols[0:parts, at:at + n]

    def row(self, name, c=0, n=None, parts=S):
        at, width = ROWS[name]
        return self.rows[0:parts, at + c:at + c + (width - c if n is None else n)]


class Stage:

    def __init__(self, core, name):
        self.core, self.nc, self.name, self.stack = core, core.nc, name, ExitStack()

    def __enter__(self):
        self.stack.__enter__()
        return self

    def __exit__(self, *a):
        return self.stack.__exit__(*a)

    def sb(self, name, shape, dt=F32):
        return self.stack.enter_context(self.nc.sbuf_tensor(f"{self.name}_{name}", shape, dt))

    def bank(self, name, dt=F32, cols=512):
        return self.stack.enter_context(self.nc.psum_tensor(f"{self.name}_{name}", [128, cols], dt))

    def sem(self, name):
        self.core.spent.append(self.nc.alloc_semaphore(name=f"{self.name}_{name}"))
        return self.core.spent[-1]

    def block(self):
        return self.stack.enter_context(self.nc.Block())


def load_stage(core):
    nc, inp = core.nc, core.inp

    def keep(name, shape, dt=F32):
        return core.stack.enter_context(nc.sbuf_tensor(name, shape, dt))

    core.stored = core.stack.enter_context(nc.semaphore("stored"))
    core.x = keep("x_tokens", [S, B, D])
    core.x_sums = keep("x_sums", [S, B, 6])
    core.ident = keep("ident", [128, 128])
    core.cols = keep("cols", [128, NCOLS])
    core.rows = keep("rows", [128, NROWS])
    core.half = keep("minus_half", [128, 64])
    core.gate = keep("gate_tanh", [128, 4])
    core.ctx = core.ctx_stack.enter_context(nc.sbuf_tensor("ctx_tokens", [CP, B * CT, CD], F32))
    core.ctx_sums = core.ctx_stack.enter_context(nc.sbuf_tensor("ctx_sums", [CP, B * CT, 6], F32))
    PARTS = 4
    SEQ = B // PARTS
    with Stage(core, "load") as st:
        loaded, x_in = st.sem("loaded"), st.sem("x_in")
        ctx_in = [st.sem(f"ctx_in{n}") for n in range(PARTS)]
        with nc.Block() as block:

            @block.sync
            def _(sp):
                sp.dma_start(core.x[:], inp["x"].rearrange("b s d -> s b d")).then_inc(x_in, 16)
                for n in range(PARTS):
                    sp.dma_start(core.ctx[:, n * SEQ * CT:(n + 1) * SEQ * CT, :].rearrange("p (b t) d -> p b t d", t=CT),
                                 inp["ctx"][n * SEQ:(n + 1) * SEQ, :, :].rearrange("b (t p) d -> p b t d", p=CP))\
                      .then_inc(ctx_in[n], 16)
                sp.dma_start(core.ident[:], inp["ident"]).then_inc(loaded, 16)
                sp.dma_start(core.cols[:], inp["cols"]).then_inc(loaded, 16)
                sp.dma_start(core.rows[:], inp["rows"].broadcast_to([128, NROWS])).then_inc(loaded, 16)
                sp.wait_ge(loaded, 48)

            @block.gpsimd
            def _(pool):
                pool.memset(core.half[:], -0.5)

            @block.scalar
            def _(act):
                act.wait_ge(loaded, 48)
                act.activation(core.gate[:], core.rows[:, 0:4], ACT.Tanh)

            @block.vector
            def _(dve):
                dve.wait_ge(x_in, 16)
                sums(dve, core.x_sums, core.x, 0, B)
                for n in range(PARTS):
                    dve.wait_ge(ctx_in[n], 16)
                    sums(dve, core.ctx_sums, core.ctx, n * SEQ * CT, SEQ * CT)


def sums(dve, out, x, first, tiles):
    with dve.Fori(0, tiles // 4) as i:
        for k in range(4):
            t = bass.ds(i * 4 + (first + k), 1)
            dve.bn_stats(out[:, t, :].rearrange("p a b -> p (a b)"), x[:, t, :].rearrange("p a b -> p (a b)"))


def stats_stage(core, name, raw, n, parts, tiles, mean, var_eps, rstd, loads=None):
    nc = core.nc
    with Stage(core, name) as st:
        tmp = st.sb("tmp", [parts, tiles])
        dev = st.sb("dev", [parts, tiles])
        dve_step, var_ready = st.sem("dve_step"), st.sem("var_ready")
        with nc.Block() as block:

            if loads is not None:
                @block.sync
                def _(sp):
                    loads(sp)

            @block.vector
            def _(dve):
                step = Chain(dve, dve_step)
                step(dve.tensor_tensor(mean, raw[:, :, 1], raw[:, :, 4], ALU.add))
                step(dve.tensor_scalar(mean, mean, 0.5, None, ALU.mult))
                step(dve.tensor_tensor(dev[:], raw[:, :, 1], raw[:, :, 4], ALU.subtract))
                step(dve.scalar_tensor_tensor(out=dev[:], in0=dev[:], scalar=0.25, in1=dev[:],
                                              op0=ALU.mult, op1=ALU.mult))
                step(dve.tensor_tensor(tmp[:], raw[:, :, 2], raw[:, :, 5], ALU.add))
                step(dve.scalar_tensor_tensor(out=dev[:], in0=tmp[:], scalar=1.0 / n, in1=dev[:],
                                              op0=ALU.mult, op1=ALU.add))
                dve.tensor_scalar(var_eps, dev[:], LN_EPS, None, ALU.add).then_inc(var_ready, 1)

            @block.gpsimd
            def _(pool):
                pool.wait_ge(var_ready, 1)
                pool.tensor_tensor(rstd, var_eps, core.half[0:parts, 0:tiles], ALU.pow)


def after(eng, sem, value):
    if not (isinstance(value, int) and value <= 0):
        eng.wait_ge(sem, value)


def rounds(eng, one_round):
    one_round(-1, 1, False, True, False)
    one_round(0, 0, True, True, False)
    with eng.Fori(0, B // 2 - 1) as i:
        one_round(2 * i + 1, 1, True, True, True)
        one_round(2 * i + 2, 0, True, True, True)
    one_round(B - 1, 1, True, False, True)
    one_round(B, 0, False, False, True)


def xa0_rounds(eng, one_round):
    one_round(-2, 0, "N")
    one_round(-1, 1, "FN")
    one_round(0, 0, "HFN")
    with eng.Fori(0, B // 2 - 2) as i:
        one_round(2 * i + 1, 1, "HFNT")
        one_round(2 * i + 2, 0, "HFNT")
    one_round(B - 3, 1, "HFNT")
    one_round(B - 2, 0, "HFT")
    one_round(B - 1, 1, "HT")
    one_round(B, 0, "T")


XA0_ORDER = [
    ("H", "kqT", 0), ("T", "hT", 0), ("F", "xT", 0), ("F", "tr", 0), ("H", "sc", 0), ("T", "wo", 0), ("H", "sc", 1),
    ("F", "kv", 0), ("H", "pt", 0), ("F", "kv", 1), ("H", "pv", 0), ("H", "sc", 2), ("F", "kv", 2), ("H", "pt", 1),
    ("F", "ssc", 0), ("F", "lat", 0), ("H", "pv", 1), ("H", "sc", 3), ("F", "ssl", 0), ("F", "lat", 1),
    ("H", "pt", 2), ("N", "norm", 0), ("H", "pv", 2), ("H", "pt", 3), ("F", "unit", 0), ("H", "pv", 3),
    ("H", "out", 0),
]


def l0_xattn_stage(core):
    nc, inp = core.nc, core.inp
    with Stage(core, "xa0") as st:
        xmean, xve, xrstd = (st.sb(n, [S, B]) for n in ("xmean", "xve", "xrstd"))
        cmean, cve, crstd = (st.sb(n, [CP, B * CT]) for n in ("cmean", "cve", "crstd"))
        wkv = st.sb("wkv", [CF, 2, 2 * D])
        wl = st.sb("wl", [128, DC, 3 * D])
        wo = st.sb("wo", [128, DC, D])
        masks = st.sb("masks", [S, B, C], U8)
        maskadd = st.sb("maskadd", [S, 2, KEYS0])
        bo = st.sb("bo", [S, D])
        gq = st.sb("gq", [128, 1])
        cn = st.sb("cn", [CP, CT, CD])
        xn = st.sb("xn", [S, D])
        cT = st.sb("cT", [CF, 2, C])
        xT = st.sb("xT", [128, DC, S])
        kv = st.sb("kv", [CP, 2, CT, 2 * D])
        lat = st.sb("lat", [S, 2, 3 * D])
        sqc = st.sb("sqc", [CP, CT, D])
        sql = st.sb("sql", [S, 2 * D])
        ssc, rrc = st.sb("ssc", [CP, CT * H0]), st.sb("rrc", [CP, CT * H0])
        ssl, rrl = st.sb("ssl", [S, 2 * H0]), st.sb("rrl", [S, 2 * H0])
        kT = st.sb("kT", [128, DC, KEYS0])
        qT = st.sb("qT", [128, DC, S])
        scores = st.sb("scores", [S, 2, KEYS0])
        top = st.sb("top", [S, H0])
        probs = st.sb("probs", [S, 2, KEYS0])
        total, rtotal = st.sb("total", [S, H0]), st.sb("rtotal", [S, H0])
        pT = st.sb("pT", [CP, 2, 4 * S])
        heads = st.sb("heads", [S, D])
        headsT = st.sb("headsT", [128, DC, S])
        add = st.sb("add", [S, D])
        trans = [st.bank("trans0"), st.bank("trans1")]
        proj = [st.bank("proj0"), st.bank("proj1")]
        score = [st.bank("score0"), st.bank("score1")]
        ptb, outb = st.bank("ptb"), st.bank("outb")

        (weights_in, dve_step, ready_once, mask_ready, cn_ready, trans_written, cT_ready, xT_ready, proj_written,
         kv_ready, sq_ready, ss_ready, rr_ready, kqn_ready, kT_written, kT_ready, qT_ready, score_written,
         scores_ready, probs_ready, pT_written, pT_ready, out_written, heads_ready, headsT_written,
         headsT_ready, wo_written, x_updated, held) = (st.sem(n) for n in
            "weights_in dve_step ready_once mask_ready cn_ready trans_written cT_ready xT_ready proj_written "
            "kv_ready sq_ready ss_ready rr_ready kqn_ready kT_written kT_ready qT_ready score_written "
            "scores_ready probs_ready pT_written pT_ready out_written heads_ready headsT_written "
            "headsT_ready wo_written x_updated held".split())

        def loads(sp):
            sp.dma_start(wkv[:], inp["w0kv"].rearrange("(c p) n -> p c n", p=CF)).then_inc(weights_in, 16)
            sp.dma_start(wl[:], inp["w0l"].rearrange("(c p) n -> p c n", p=128)).then_inc(weights_in, 16)
            sp.dma_start(wo[:], inp["w0o"].rearrange("(c p) n -> p c n", p=128)).then_inc(weights_in, 16)
            sp.dma_start(masks[:].rearrange("p b c -> p (b c)"),
                         inp["mask"].broadcast_to([S, B * C])).then_inc(weights_in, 16)

        stats_stage(core, "xa0_xs", core.x_sums, D, S, B, xmean[:], xve[:], xrstd[:], loads)
        stats_stage(core, "xa0_cs", core.ctx_sums, CD, CP, B * CT, cmean[:], cve[:], crstd[:])
        with nc.Block() as block:

            @block.vector
            def _(dve):
                step = Chain(dve, dve_step)
                dve.wait_ge(weights_in, 64)
                step(dve.tensor_scalar(xve[:], xve[:], -LN_EPS, None, ALU.add))
                step(dve.tensor_tensor(xve[:], xve[:], xrstd[:], ALU.mult))
                step(dve.tensor_tensor(xve[:], xve[:], xrstd[:], ALU.mult))
                dve.tensor_scalar(xve[:], xve[:], LN_EPS, None, ALU.add).then_inc(ready_once, 1)
                dve.tensor_scalar(gq[:], core.col("qn_g"), HD0 ** -0.5, None, ALU.mult).then_inc(ready_once, 1)
                dve.memset(maskadd[:], 0.0).then_inc(ready_once, 1)
                dve.tensor_scalar(bo[:], core.row("bo0"), core.gate[0:S, 0:1], None, ALU.mult)\
                   .then_inc(ready_once, 1)
                dve.memset(ptb[:], 0.0).then_inc(ready_once, 1)
                dve.wait_ge(ready_once, 6)
                step(dve.tensor_tensor(xrstd[:], xrstd[:], xve[:], ALU.mult))

                def one_round(b, k, on):
                    n, m = b + 1, 1 - k
                    for part, what, j in XA0_ORDER:
                        if part not in on:
                            continue
                        if what == "norm":
                            after(dve, trans_written, 3 * (b + 2))
                            for t in range(CT):
                                dve.tensor_scalar(cn[:, t, :],
                                                  core.ctx[:, bass.ds((b + 2) * CT + t, 1), :].rearrange("p a c -> p (a c)"),
                                                  cmean[:, bass.ds((b + 2) * CT + t, 1)], crstd[:, bass.ds((b + 2) * CT + t, 1)],
                                                  ALU.subtract, ALU.mult).then_inc(cn_ready, 1)
                            dve.tensor_scalar(xn[:], core.x[:, bass.ds(b + 2, 1), :].rearrange("p a c -> p (a c)"),
                                              xmean[:, bass.ds(b + 2, 1)], xrstd[:, bass.ds(b + 2, 1)],
                                              ALU.subtract, ALU.mult).then_inc(cn_ready, 1)
                        if what == "ssc":
                            dve.tensor_scalar(maskadd[:, m, 0:C],
                                              masks[:, bass.ds(n, 1), :].rearrange("p a c -> p (a c)"),
                                              -1.0, MASKED, ALU.add, ALU.mult).then_inc(mask_ready, 1)
                            dve.wait_ge(kv_ready, 5 * n + 3)
                            kc = kv[:, m, :, 0:D]
                            if "H" in on:
                                dve.wait_ge(kT_written, 3 * b + 3)
                            dve.tensor_tensor(sqc[:], kc, kc, ALU.mult).then_inc(sq_ready, 1)
                            dve.wait_ge(sq_ready, 2 * n + 1)
                            dve.tensor_reduce(ssc[:], sqc[:].rearrange("p t (h d) -> p (t h) d", h=H0), AX.X,
                                              ALU.add).then_inc(ss_ready, 1)
                            dve.wait_ge(ss_ready, 4 * n + 1)
                            dve.tensor_scalar(ssc[:], ssc[:], 1.0 / HD0, RMS_MIN_SQ, ALU.mult, ALU.max)\
                               .then_inc(ss_ready, 1)
                        if what == "ssl":
                            dve.wait_ge(kv_ready, 5 * n + 4)
                            kq = lat[:, m, 0:2 * D]
                            dve.tensor_tensor(sql[:], kq, kq, ALU.mult).then_inc(sq_ready, 1)
                            dve.wait_ge(sq_ready, 2 * n + 2)
                            dve.tensor_reduce(ssl[:], sql[:].rearrange("p (h d) -> p h d", h=2 * H0), AX.X, ALU.add)\
                               .then_inc(ss_ready, 1)
                            dve.wait_ge(ss_ready, 4 * n + 3)
                            dve.tensor_scalar(ssl[:], ssl[:], 1.0 / HD0, RMS_MIN_SQ, ALU.mult, ALU.max)\
                               .then_inc(ss_ready, 1)
                        if what == "unit":
                            dve.wait_ge(rr_ready, 2 * n + 1)
                            for t in range(CT):
                                k4 = kv[:, m, t, 0:D].rearrange("p (h d) -> p h d", h=H0)
                                dve.tensor_tensor(sqc[:, t, :].rearrange("p (h d) -> p h d", h=H0), k4,
                                                  widen(rrc[:, t * H0:(t + 1) * H0], 2, HD0), ALU.mult)\
                                   .then_inc(kqn_ready, 1)
                            dve.wait_ge(rr_ready, 2 * n + 2)
                            dve.tensor_tensor(sql[:].rearrange("p (h d) -> p h d", h=2 * H0),
                                              lat[:, m, 0:2 * D].rearrange("p (h d) -> p h d", h=2 * H0),
                                              widen(rrl[:], 2, HD0), ALU.mult).then_inc(kqn_ready, 1)
                        if what == "sc":
                            dve.wait_ge(score_written, H0 * b + j + 1)
                            dve.wait_ge(mask_ready, b + 1)
                            after(dve, probs_ready, H0 * b + j - 1)
                            dve.sem_inc(held, 1)
                            dve.tensor_tensor_reduce(out=scores[:, j % 2, :], in0=score[j % 2][0:S, 0:KEYS0],
                                                     in1=maskadd[:, k, :], scale=-1.0, scalar=3e38, op0=ALU.add,
                                                     op1=ALU.min, accum_out=top[:, j:j + 1]).then_inc(scores_ready, 1)
                        if what == "pt":
                            dve.wait_ge(pT_written, H0 * b + j + 1)
                            dve.tensor_copy(pT[:, j % 2, :], ptb[0:CP, 0:4 * S]).then_inc(pT_ready, 1)
                        if what == "out":
                            dve.wait_ge(probs_ready, H0 * b + H0)
                            dve.reciprocal(rtotal[:], total[:]).then_inc(heads_ready, 1)
                            dve.wait_ge(heads_ready, 2 * b + 1)
                            dve.wait_ge(out_written, b + 1)
                            dve.tensor_tensor(heads[:].rearrange("p (h d) -> p h d", h=H0),
                                              outb[0:S, 0:D].rearrange("p (h d) -> p h d", h=H0),
                                              widen(rtotal[:], 2, HD0), ALU.mult).then_inc(heads_ready, 1)
                        if what == "wo":
                            dve.wait_ge(wo_written, b)
                            dve.scalar_tensor_tensor(out=add[:], in0=outb[0:S, 0:D], scalar=core.gate[0:S, 0:1],
                                                     in1=bo[:], op0=ALU.mult, op1=ALU.add).then_inc(x_updated, 1)
                            dve.wait_ge(x_updated, 2 * b - 1)
                            xb = core.x[:, bass.ds(b - 1, 1), :].rearrange("p a c -> p (a c)")
                            dve.tensor_tensor(xb, xb, add[:], ALU.add).then_inc(x_updated, 1)
                            dve.wait_ge(x_updated, 2 * b)
                            dve.bn_stats(core.x_sums[:, bass.ds(b - 1, 1), :].rearrange("p a b -> p (a b)"), xb)

                xa0_rounds(dve, one_round)

            @block.gpsimd
            def _(pool):
                pool.wait_ge(ready_once, 1)
                pool.tensor_tensor(xve[:], xve[:], core.half[0:S, 0:B], ALU.pow).then_inc(ready_once, 1)
                with pool.Fori(0, B) as b:
                    pool.wait_ge(ss_ready, 4 * b + 2)
                    pool.tensor_tensor(rrc[:], ssc[:], core.half[0:CP, 0:CT * H0], ALU.pow).then_inc(rr_ready, 1)
                    pool.wait_ge(ss_ready, 4 * b + 4)
                    pool.tensor_tensor(rrl[:], ssl[:], core.half[0:S, 0:2 * H0], ALU.pow).then_inc(rr_ready, 1)

            @block.scalar
            def _(act):
                act.wait_ge(ready_once, 6)

                def one_round(b, k, on):
                    n, m = b + 1, 1 - k
                    for part, what, j in XA0_ORDER:
                        if part not in on:
                            continue
                        if what == "tr":
                            for c in range(2):
                                act.wait_ge(trans_written, 3 * n + c + 2)
                                act.activation(cT[:, c, :], trans[c][0:CF, 0:C], ACT.Identity,
                                               scale=core.col("lnx_g", c, parts=CF),
                                               bias=core.col("lnx_b", c, parts=CF)).then_inc(cT_ready, 1)
                        if what == "xT":
                            act.wait_ge(trans_written, 3 * n + 1)
                            for c in range(DC):
                                act.activation(xT[:, c, :], proj[0][:, c * S:(c + 1) * S], ACT.Identity,
                                               scale=core.col("lnl_g", c), bias=core.col("lnl_b", c))\
                                   .then_inc(xT_ready, 1)
                        if what == "kv":
                            act.wait_ge(proj_written, 5 * n + j + 1)
                            act.activation(kv[:, m, j, :], proj[(j + 1) % 2][0:CP, :], ACT.Copy).then_inc(kv_ready, 1)
                        if what == "lat" and j == 0:
                            act.wait_ge(proj_written, 5 * n + 4)
                            act.activation(lat[:, m, 0:2 * D], proj[0][0:S, :], ACT.Copy).then_inc(kv_ready, 1)
                        if what == "lat" and j == 1:
                            act.wait_ge(proj_written, 5 * n + 5)
                            act.activation(lat[:, m, 2 * D:3 * D], proj[1][0:S, 0:D], ACT.Copy).then_inc(kv_ready, 1)
                        if what == "kqT":
                            for c in range(DC):
                                act.wait_ge(kT_written, 3 * b + c + 1)
                                act.activation(kT[:, c, :], trans[c][:, 0:KEYS0], ACT.Copy, scale=core.col("kn_g"))\
                                   .then_inc(kT_ready, 1)
                            act.wait_ge(kT_written, 3 * b + 3)
                            act.activation(qT[:].rearrange("p c s -> p (c s)"), ptb[:, 0:DC * S],
                                           ACT.Copy, scale=gq[:]).then_inc(qT_ready, 1)
                        if what == "sc":
                            act.wait_ge(scores_ready, H0 * b + j + 1)
                            after(act, pT_written, H0 * b + j - 1)
                            act.activation(probs[:, j % 2, :], scores[:, j % 2, :], ACT.Exp, scale=-1.0,
                                           bias=top[:, j:j + 1], accum_out=total[:, j:j + 1]).then_inc(probs_ready, 1)
                        if what == "hT":
                            act.wait_ge(headsT_written, b)
                            act.activation(headsT[:].rearrange("p c s -> p (c s)"), outb[:, 0:DC * S], ACT.Copy)\
                               .then_inc(headsT_ready, 1)

                xa0_rounds(act, one_round)

            @block.tensor
            def _(pe):
                idc, ids = core.ident[0:CP, 0:CP], core.ident[0:S, 0:S]
                pe.wait_ge(weights_in, 64)
                pe.wait_ge(ready_once, 6)

                def one_round(b, k, on):
                    n, m = b + 1, 1 - k
                    for part, what, j in XA0_ORDER:
                        if part not in on:
                            continue
                        if what == "xT":
                            pe.wait_ge(cn_ready, 4 * n + 4)
                            after(pe, kv_ready, 5 * n - 1)
                            for c in range(DC):
                                last = pe.transpose(proj[0][:, c * S:(c + 1) * S], xn[:, c * 128:(c + 1) * 128], ids)
                            last.then_inc(trans_written, 1)
                        if what == "tr":
                            after(pe, kT_ready, 2 * n)
                            for c in range(2):
                                for t in range(CT):
                                    last = pe.transpose(trans[c][0:CF, t * CP:(t + 1) * CP],
                                                        cn[:, t, c * CF:(c + 1) * CF], idc)
                                last.then_inc(trans_written, 1)
                        if what == "kv":
                            if j == 0:
                                pe.wait_ge(cT_ready, 2 * n + 2)
                                after(pe, kv_ready, 5 * n)
                            if j == 1:
                                pe.wait_ge(xT_ready, 2 * n + 2)
                            if j == 2:
                                pe.wait_ge(kv_ready, 5 * n + 1)
                            for c in range(2):
                                last = pe.matmul(proj[(j + 1) % 2][0:CP, :], cT[:, c, j * CP:(j + 1) * CP],
                                                 wkv[:, c, :], start=(c == 0), stop=(c == 1))
                            last.then_inc(proj_written, 1)
                        if what == "lat":
                            pe.wait_ge(kv_ready, 5 * n + 2 + j)
                            o, of = ((proj[0][0:S, :], slice(0, 2 * D)), (proj[1][0:S, 0:D], slice(2 * D, 3 * D)))[j]
                            for c in range(DC):
                                last = pe.matmul(o, xT[:, c, :], wl[:, c, of], start=(c == 0), stop=(c == DC - 1))
                            last.then_inc(proj_written, 1)
                        if what == "kqT":
                            pe.wait_ge(kqn_ready, 4 * b + 4)
                            pe.wait_ge(cT_ready, 2 * b + 2)
                            after(pe, pT_ready, H0 * b)
                            for c in range(DC):
                                for t in range(CT):
                                    pe.transpose(trans[c][:, t * CP:(t + 1) * CP], sqc[:, t, c * 128:(c + 1) * 128],
                                                 idc)
                                pe.transpose(trans[c][:, C:KEYS0], sql[:, c * 128:(c + 1) * 128], ids)\
                                  .then_inc(kT_written, 1)
                            for c in range(DC):
                                last = pe.transpose(ptb[:, c * S:(c + 1) * S],
                                                    sql[:, D + c * 128:D + (c + 1) * 128], ids)
                            last.then_inc(kT_written, 1)
                        if what == "sc":
                            if j == 0:
                                pe.wait_ge(kT_ready, 2 * b + 2)
                                pe.wait_ge(qT_ready, b + 1)
                            after(pe, scores_ready, H0 * b + j - 1)
                            r = HD0 * (j % 2)
                            pe.matmul(score[j % 2][0:S, 0:KEYS0], qT[r:r + HD0, j // 2, :],
                                      kT[r:r + HD0, j // 2, :], start=True, stop=True).then_inc(score_written, 1)
                        if what == "pt":
                            pe.wait_ge(probs_ready, H0 * b + j + 1)
                            after(pe, pT_ready, H0 * b + j)
                            for t in range(CT):
                                pe.transpose(ptb[0:CP, t * S:(t + 1) * S], probs[:, j % 2, t * CP:(t + 1) * CP], ids)
                            pe.transpose(ptb[0:S, CT * S:(CT + 1) * S], probs[:, j % 2, C:KEYS0], ids)\
                              .then_inc(pT_written, 1)
                        if what == "pv":
                            pe.wait_ge(pT_ready, H0 * b + j + 1)
                            if j == 0:
                                pe.wait_ge(kv_ready, 5 * b + 5)
                                after(pe, x_updated, 2 * b - 1)
                            o = outb[0:S, j * HD0:(j + 1) * HD0]
                            for t in range(CT):
                                pe.matmul(o, pT[:, j % 2, t * S:(t + 1) * S],
                                          kv[:, k, t, D + j * HD0:D + (j + 1) * HD0], start=(t == 0), stop=False)
                            last = pe.matmul(o, pT[0:S, j % 2, CT * S:(CT + 1) * S],
                                             lat[:, k, 2 * D + j * HD0:2 * D + (j + 1) * HD0], start=False, stop=True)
                            if j == H0 - 1:
                                last.then_inc(out_written, 1)
                        if what == "hT":
                            pe.wait_ge(heads_ready, 2 * b)
                            for c in range(DC):
                                last = pe.transpose(outb[:, c * S:(c + 1) * S], heads[:, c * 128:(c + 1) * 128], ids)
                            last.then_inc(headsT_written, 1)
                        if what == "wo":
                            pe.wait_ge(headsT_ready, b)
                            for c in range(DC):
                                last = pe.matmul(outb[0:S, 0:D], headsT[:, c, :], wo[:, c, :], start=(c == 0),
                                                 stop=(c == DC - 1))
                            last.then_inc(wo_written, 1)

                xa0_rounds(pe, one_round)


def split_weights(core, pool, e, k):
    n = 4 * e
    pool.wait_ge(core.w_in, 32 * e + 32)
    w1r, w2r = (w[:].rearrange("p c f -> p (c f)") for w in (core.w1f, core.w2f))
    pool.sem_inc(core.w_held, 1)
    pool.tensor_copy(core.w1[:, k, 0, :], w1r).then_inc(core.w_split, 1)
    pool.tensor_copy(core.w2[:, k, 0, :], w2r).then_inc(core.w_split, 1)
    pool.wait_ge(core.w_split, n + 2)
    pool.tensor_tensor(core.w1[:, k, 1, :], w1r, core.w1[:, k, 0, :], ALU.subtract).then_inc(core.w_split, 1)
    pool.tensor_tensor(core.w2[:, k, 1, :], w2r, core.w2[:, k, 0, :], ALU.subtract).then_inc(core.w_split, 1)


def routing_stage(core, keep):
    nc, inp = core.nc, core.inp
    BE = B * E0
    HALF = BE // 2
    core.norm_hi = keep("norm_hi", [S, B, D], F16)
    core.norm_lo = keep("norm_lo", [S, B, D], F16)
    core.place = keep("place", [S, BE])
    core.gates = keep("gates", [S, BE])
    FC = F0 // 128
    core.w1f, core.w2f = keep("w1f", [128, DC, F0]), keep("w2f", [128, FC, D])
    core.w1 = keep("w1", [128, 2, 2, DC * F0], F16)
    core.w2 = keep("w2", [128, 2, 2, FC * D], F16)
    with Stage(core, "route") as st:
        mean, ve, rstd = (st.sb(n, [S, B]) for n in ("mean", "ve", "rstd"))
        gq = st.sb("gq", [128, DC, E0])
        xn = st.sb("xn", [S, 2, D])
        xT = st.sb("xT", [128, 2, DC * S])
        invt = st.sb("invt", [S, 1])
        t = st.sb("t", [S, BE])
        e = st.sb("e", [S, BE])
        m, s, ln = (st.sb(n, [S, B]) for n in ("m", "s", "ln"))
        u = st.sb("u", [HALF, 2, S])
        v = st.sb("v", [HALF, 2, S])
        um, us, ul = (st.sb(n, [HALF, 2]) for n in ("um", "us", "ul"))
        aff = st.sb("aff", [HALF, 2, S])
        left = st.sb("left", [HALF, 2, S])
        best = st.sb("best", [HALF, 2, 8])
        taken = st.sb("taken", [HALF, 2, S])
        order = st.sb("order", [HALF, 2, S])
        ones = st.sb("ones", [HALF, S])
        logits = st.bank("logits")
        xTb = [st.bank("xTb0"), st.bank("xTb1")]
        by_row = st.bank("by_row")
        by_token = st.bank("by_token")
        by_token2 = st.bank("by_token2")
        (loaded, dve_step, normed, split, xT_written, xT_ready, logits_written, t_ready, row_ready, row_written,
         m_ready, e_ready, s_ready, l_ready, token_written, aff_ready, place_written, tscale) = (
            st.sem(n) for n in "loaded dve_step normed split xT_written xT_ready logits_written t_ready row_ready "
            "row_written m_ready e_ready s_ready l_ready token_written aff_ready place_written tscale".split())
        core.w_in, core.w_split, core.w_held = st.sem("w_in"), st.sem("w_split"), st.sem("w_held")

        def loads(sp):
            sp.dma_start(gq[:], inp["gate_query"].rearrange("(c p) n -> p c n", p=128)).then_inc(loaded, 16)
            sp.dma_start(core.w1f[:], inp["w1"][0, :, :].rearrange("(c p) f -> p c f", p=128)).then_inc(core.w_in, 16)
            sp.dma_start(core.w2f[:], inp["w2"][0, :, :].rearrange("(c p) f -> p c f", p=128)).then_inc(core.w_in, 16)

        stats_stage(core, "route_s", core.x_sums, D, S, B, mean[:], ve[:], rstd[:], loads)
        with nc.Block() as block:

            @block.gpsimd
            def _(pool):
                split_weights(core, pool, 0, 0)

            @block.vector
            def _(dve):
                with dve.Fori(0, B // 2) as i:
                    for k in range(2):
                        xb = core.x[:, bass.ds(2 * i + k, 1), :].rearrange("p a c -> p (a c)")
                        hi = core.norm_hi[:, bass.ds(2 * i + k, 1), :].rearrange("p a c -> p (a c)")
                        lo = core.norm_lo[:, bass.ds(2 * i + k, 1), :].rearrange("p a c -> p (a c)")
                        dve.wait_ge(xT_written, 2 * i + k + 1)
                        dve.tensor_scalar(xn[:, k, :], xb, mean[:, bass.ds(2 * i + k, 1)],
                                          rstd[:, bass.ds(2 * i + k, 1)], ALU.subtract, ALU.mult).then_inc(normed, 1)
                        dve.wait_ge(normed, 2 * i + k + 1)
                        dve.tensor_scalar(hi, xn[:, k, :], 1.0, None, ALU.mult).then_inc(split, 1)
                        dve.wait_ge(split, 2 * i + k + 1)
                        dve.tensor_tensor(lo, xn[:, k, :], hi, ALU.subtract)
                step = Chain(dve, dve_step)
                step(dve.memset(ones[:], 1.0))
                dve.wait_ge(logits_written, B)
                dve.wait_ge(tscale, 1)
                dve.tensor_scalar(t[:], logits[0:S, 0:BE], invt[:], None, ALU.mult).then_inc(t_ready, 1)
                fixed = step.n
                PER = 2
                with dve.Fori(0, SINKHORN) as i:
                    step = Chain(dve, dve_step, PER * i + fixed)
                    dve.wait_ge(t_ready, 2 * i + 1)
                    t3 = t[:].rearrange("p (b e) -> p b e", e=E0)
                    step(dve.tensor_reduce(m[:], t3, AX.X, ALU.max))
                    dve.tensor_tensor(t3, t3, widen(m[:], 2, E0), ALU.subtract).then_inc(t_ready, 1)
                    dve.wait_ge(e_ready, 2 * i + 1)
                    dve.tensor_reduce(s[:], e[:].rearrange("p (b e) -> p b e", e=E0), AX.X, ALU.add)\
                       .then_inc(s_ready, 1)
                    dve.wait_ge(l_ready, 2 * i + 1)
                    dve.tensor_tensor(t3, t3, widen(ln[:], 2, E0), ALU.subtract).then_inc(row_ready, 1)
                    dve.wait_ge(row_written, i + 1)
                    r3 = by_row[0:HALF, 0:2 * S].rearrange("p (c s) -> p c s", c=2)
                    step(dve.tensor_reduce(um[:], r3, AX.X, ALU.max))
                    dve.tensor_tensor(u[:], r3, widen(um[:], 2, S), ALU.subtract).then_inc(row_ready, 1)
                    dve.wait_ge(e_ready, 2 * i + 2)
                    dve.tensor_reduce(us[:], v[:], AX.X, ALU.add).then_inc(s_ready, 1)
                    dve.wait_ge(l_ready, 2 * i + 2)
                    dve.tensor_tensor(u[:], u[:], widen(ul[:], 2, S), ALU.subtract).then_inc(row_ready, 1)
                    dve.wait_ge(token_written, i + 1)
                    dve.tensor_copy(t[:], by_token[0:S, 0:BE]).then_inc(t_ready, 1)
                    assert step.n == PER
                step = Chain(dve, dve_step, 0)
                step.n = PER * SINKHORN + fixed
                dve.wait_ge(aff_ready, 1)
                step(dve.tensor_copy(left[:], aff[:]))
                for r in range(CAP // 8):
                    for c in range(2):
                        last = dve.max(best[:, c, :], left[:, c, :])
                    step(last)
                    for c in range(2):
                        last = dve.match_replace(left[:, c, :], best[:, c, :], left[:, c, :], -1.0)
                    step(last)
                step(dve.tensor_scalar(taken[:], left[:], 0.0, None, ALU.is_lt))
                for c in range(2):
                    last = dve.tensor_tensor_scan(order[:, c, :], ones[:], taken[:, c, :], 0.0, ALU.mult, ALU.add)
                step(last)
                step(dve.tensor_tensor(order[:], order[:], taken[:], ALU.mult))
                step(dve.tensor_tensor(taken[:], aff[:], taken[:], ALU.mult))
                dve.tensor_scalar(order[:], order[:], -1.0, None, ALU.add).then_inc(aff_ready, 1)
                dve.wait_ge(place_written, 1)
                dve.tensor_copy(core.place[:], by_token[0:S, 0:BE])
                dve.wait_ge(place_written, 2)
                dve.tensor_scalar(core.gates[:], by_token2[0:S, 0:BE], core.gate[0:S, 2:3], None, ALU.mult)

            @block.scalar
            def _(act):
                act.preload_act_table_set("natural_log_exp_and_others")
                act.activation(invt[:], core.row("log_temp"), ACT.Exp, scale=-1.0).then_inc(tscale, 1)
                with act.Fori(0, B // 2) as i:
                    for k in range(2):
                        act.wait_ge(xT_written, 2 * i + k + 3)
                        act.activation(xT[:, k, :], xTb[k][:, 0:DC * S], ACT.Copy).then_inc(xT_ready, 1)
                with act.Fori(0, SINKHORN) as i:
                    act.wait_ge(t_ready, 2 * i + 2)
                    act.activation(e[:], t[:], ACT.Exp).then_inc(e_ready, 1)
                    act.wait_ge(s_ready, 2 * i + 1)
                    act.activation(ln[:], s[:], ACT.Ln).then_inc(l_ready, 1)
                    act.wait_ge(row_ready, 3 * i + 2)
                    act.activation(v[:], u[:], ACT.Exp).then_inc(e_ready, 1)
                    act.wait_ge(s_ready, 2 * i + 2)
                    act.activation(ul[:], us[:], ACT.Ln).then_inc(l_ready, 1)
                act.wait_ge(row_ready, 3 * SINKHORN)
                act.activation(aff[:], u[:], ACT.Exp).then_inc(aff_ready, 1)

            @block.tensor
            def _(pe):
                ids, idn = core.ident[0:S, 0:S], core.ident[:]
                pe.sem_inc(xT_written, 2)
                pe.wait_ge(loaded, 16)
                with pe.Fori(0, B // 2) as i:
                    for k in range(2):
                        pe.wait_ge(normed, 2 * i + k + 1)
                        for c in range(DC):
                            last = pe.transpose(xTb[k][:, c * S:(c + 1) * S], xn[:, k, c * 128:(c + 1) * 128], ids)
                        last.then_inc(xT_written, 1)
                        pe.wait_ge(xT_ready, 2 * i + k + 1)
                        for c in range(DC):
                            last = pe.matmul(logits[0:S, bass.ds((2 * i + k) * E0, E0)], xT[:, k, c * S:(c + 1) * S],
                                             gq[:, c, :], start=(c == 0), stop=(c == DC - 1))
                        last.then_inc(logits_written, 1)
                with pe.Fori(0, SINKHORN) as i:
                    pe.wait_ge(row_ready, 3 * i + 1)
                    for c in range(2):
                        last = pe.transpose(by_row[0:HALF, c * S:(c + 1) * S], t[:, c * HALF:(c + 1) * HALF], ids)
                    last.then_inc(row_written, 1)
                    pe.wait_ge(row_ready, 3 * i + 3)
                    for c in range(2):
                        last = pe.transpose(by_token[0:S, c * HALF:(c + 1) * HALF], u[:, c, :], idn)
                    last.then_inc(token_written, 1)
                pe.wait_ge(aff_ready, 2)
                pe.wait_ge(t_ready, 2 * SINKHORN + 1)
                for c in range(2):
                    last = pe.transpose(by_token[0:S, c * HALF:(c + 1) * HALF], order[:, c, :], idn)
                last.then_inc(place_written, 1)
                for c in range(2):
                    last = pe.transpose(by_token2[0:S, c * HALF:(c + 1) * HALF], taken[:, c, :], idn)
                last.then_inc(place_written, 1)


def each_expert(eng, count, one_expert):
    with eng.Fori(0, count // 2 - 1) as i:
        one_expert(2 * i, 0, True)
        one_expert(2 * i + 1, 1, True)
    one_expert(count - 2, 0, True)
    one_expert(count - 1, 1, False)


def experts0_stage(core, keep):
    nc, inp = core.nc, core.inp
    FC = F0 // 128
    SLOTS = B * CAP
    NH = SLOTS // 512
    SEQH = B // NH
    NT = SLOTS // 128
    G = 2 * DC * NH
    with Stage(core, "ex0") as st:
        w1f, w2f, w1, w2, w_in, w_split = core.w1f, core.w2f, core.w1, core.w2, core.w_in, core.w_split
        b1 = st.sb("b1", [128, 2, FC])
        b2 = st.sb("b2", [128, 2, D])
        pick = st.sb("pick", [S, B, CAP], F16)
        iota = st.sb("iota16", [S, CAP])
        pickT = st.sb("pickT", [128, NT * S], F16)
        identh = st.sb("identh", [S, S], F16)
        xT = st.sb("xT", [128, 2, DC, SLOTS], F16)
        h = st.sb("h", [128, 2, 512])
        hh = st.sb("hh", [128, 2, FC, SLOTS], F16)
        yf = st.sb("yf", [128, 2, D])
        y = st.sb("y", [128, 2, 2, D], F16)
        gat = [st.bank("gat0"), st.bank("gat1")]
        hid = [st.bank("hid0"), st.bank("hid1")]
        yb = [st.bank("y0"), st.bank("y1")]
        sc = [st.bank("sc0"), st.bank("sc1")]
        pTb = sc[0][:].bitcast(F16)
        (b0_in, b1_in, pick_ready, gat_written, xT0_ready, xT1_ready, picks_written, pickT_ready, hid_written,
         h_ready, hi_ready, lo_ready, y_written, yf_ready, yhi_ready, ylo_ready, sc_written, x_updated, const,
         held) = (st.sem(n) for n in
            "b0_in b1_in pick_ready gat_written xT0_ready xT1_ready picks_written pickT_ready hid_written "
            "h_ready hi_ready lo_ready y_written yf_ready yhi_ready ylo_ready sc_written x_updated const held".split())
        NJ = FC * NH

        with nc.Block() as block:

            @block.sync
            def _(sp):
                def biases(e, k):
                    at = bass.ds(e, 1)
                    sp.wait_ge(x_updated, B * e + 2)
                    sp.dma_start(b1[:, k, :], inp["b1"][at, :, :].rearrange("a p c -> p (a c)")).then_inc((b0_in, b1_in)[k], 16)
                    sp.dma_start(b2[:, k, :], inp["b2"][at, :].broadcast_to([128, D])).then_inc((b0_in, b1_in)[k], 16)

                def weights(e):
                    at = bass.ds(e, 1)
                    sp.wait_ge(w_split, 4 * e)
                    sp.dma_start(w1f[:], inp["w1"][at, :, :].rearrange("a (c p) f -> p (a c) f", p=128))\
                      .then_inc(w_in, 16)
                    sp.dma_start(w2f[:], inp["w2"][at, :, :].rearrange("a (c p) f -> p (a c) f", p=128))\
                      .then_inc(w_in, 16)

                biases(0, 0)
                with sp.Fori(0, E0 // 2 - 1) as i:
                    for e, k in ((2 * i + 1, 1), (2 * i + 2, 0)):
                        weights(e)
                        biases(e, k)
                weights(E0 - 1)
                biases(E0 - 1, 1)

            @block.gpsimd
            def _(pool):
                with pool.Fori(0, E0 // 2 - 1) as i:
                    for e, k in ((2 * i + 1, 1), (2 * i + 2, 0)):
                        pool.wait_ge(x_updated, B * e + 2)
                        split_weights(core, pool, e, k)
                pool.wait_ge(x_updated, B * (E0 - 1) + 2)
                split_weights(core, pool, E0 - 1, 1)

            @block.vector
            def _(dve):
                dve.tensor_copy(identh[:], core.ident[0:S, 0:S]).then_inc(const, 1)
                dve.tensor_copy(iota[:], core.row("iota")).then_inc(const, 1)
                dve.wait_ge(const, 2)
                dve.sem_inc(x_updated, B + 2)
                dve.sem_inc(lo_ready, 2)
                dve.sem_inc(yf_ready, 2)
                dve.sem_inc(ylo_ready, 2)

                def choose(e):
                    at = core.place[:].rearrange("p (b e) -> p b e", e=E0)[:, :, bass.ds(e, 1)]
                    dve.wait_ge(picks_written, e + 1)
                    dve.tensor_tensor(pick[:], widen(iota[:], 1, B), at.broadcast_to([S, B, CAP]), ALU.is_equal)\
                       .then_inc(pick_ready, 1)

                def gathered(e, g):
                    dve.wait_ge(gat_written, G * e + g + 1)
                    dve.tensor_copy(xT[:, g // (DC * NH), g // NH % DC, g % NH * 512:(g % NH + 1) * 512],
                                    gat[1][:]).then_inc(xT1_ready, 1)

                def one_expert(e, k, another):
                    for j in range(NJ):
                        f, n = j % FC, j // FC
                        at = slice(n * 512, (n + 1) * 512)
                        dve.wait_ge(hi_ready, NJ * e + j + 1)
                        dve.tensor_tensor(hh[:, 1, f, at], h[:, j % 2, :], hh[:, 0, f, at], ALU.subtract)\
                           .then_inc(lo_ready, 1)
                        if j == 2:
                            dve.wait_ge(picks_written, e + 2)
                            dve.tensor_copy(pickT[:], pTb[:, 0:NT * S]).then_inc(pickT_ready, 1)
                        if j == FC and another:
                            choose(e + 1)
                    for t in range(NT + 1):
                        if t < NT:
                            dve.wait_ge(y_written, NT * e + t + 1)
                            dve.wait_ge(ylo_ready, NT * e + t + 1)
                            dve.tensor_tensor(yf[:, t % 2, :], yb[t % 2][:, 0:D], b2[:, k, :], ALU.add)\
                               .then_inc(yf_ready, 1)
                        if t >= 1:
                            for q in range(2):
                                b = 2 * (t - 1) + q
                                dve.wait_ge(sc_written, B * e + b + 4)
                                dve.scalar_tensor_tensor(
                                    out=core.x[:, b, :], in0=sc[q][0:S, 0:D],
                                    scalar=core.gates[:, bass.ds(b * E0 + e, 1)], in1=core.x[:, b, :],
                                    op0=ALU.mult, op1=ALU.add).then_inc(x_updated, 1)
                        if t < NT:
                            dve.wait_ge(yhi_ready, NT * e + t + 1)
                            dve.tensor_tensor(y[:, t % 2, 1, :], yf[:, t % 2, :], y[:, t % 2, 0, :], ALU.subtract)\
                               .then_inc(ylo_ready, 1)
                        if another and t < G and t % 2 == 1:
                            gathered(e + 1, t)
                        if not another and t >= 1:
                            dve.wait_ge(x_updated, B * e + B + 2 + 2 * t)
                            for b in (2 * t - 2, 2 * t - 1):
                                dve.bn_stats(core.x_sums[:, b, :], core.x[:, b, :])

                choose(0)
                for g in range(1, G, 2):
                    gathered(0, g)
                each_expert(dve, E0, one_expert)

            @block.scalar
            def _(act):
                act.sem_inc(h_ready, 2)

                def gathered(e, g):
                    act.wait_ge(gat_written, G * e + g + 1)
                    act.activation(xT[:, g // (DC * NH), g // NH % DC, g % NH * 512:(g % NH + 1) * 512],
                                   gat[0][:], ACT.Copy).then_inc(xT0_ready, 1)

                def one_expert(e, k, another):
                    act.wait_ge((b0_in, b1_in)[k], 16 * e + 16 * (2 - k))
                    for j in range(NJ):
                        f, n = j % FC, j // FC
                        at = slice(n * 512, (n + 1) * 512)
                        act.wait_ge(hid_written, NJ * e + j + 1)
                        act.wait_ge(lo_ready, NJ * e + j + 1)
                        act.activation(h[:, j % 2, :], hid[j % 2][:], ACT.Gelu_apprx_tanh, bias=b1[:, k, f:f + 1])\
                            .then_inc(h_ready, 1)
                        act.wait_ge(h_ready, NJ * e + j + 3)
                        act.activation(hh[:, 0, f, at], h[:, j % 2, :], ACT.Copy).then_inc(hi_ready, 1)
                    for t in range(NT):
                        act.wait_ge(yf_ready, NT * e + t + 3)
                        act.wait_ge(sc_written, B * e + 2 * t + 1)
                        act.activation(y[:, t % 2, 0, :], yf[:, t % 2, :], ACT.Copy).then_inc(yhi_ready, 1)
                        if another and t < G and t % 2 == 0:
                            gathered(e + 1, t)

                for g in range(0, G, 2):
                    gathered(0, g)
                each_expert(act, E0, one_expert)

            @block.tensor
            def _(pe):
                pe.sem_inc(picks_written, 1)
                pe.sem_inc(sc_written, 3)
                pe.wait_ge(const, 2)

                def gather(e, g):
                    src = (core.norm_hi, core.norm_lo)[g // (DC * NH)]
                    c, n = g // NH % DC, g % NH
                    if g == 0:
                        pe.wait_ge(pick_ready, e + 1)
                    if g >= 2:
                        pe.wait_ge((xT0_ready, xT1_ready)[g % 2], G // 2 * e + g // 2)
                    for b in range(SEQH):
                        last = pe.matmul(gat[g % 2][:, b * CAP:(b + 1) * CAP],
                                         src[:, n * SEQH + b, c * 128:(c + 1) * 128],
                                         pick[:, n * SEQH + b, :], start=True, stop=True)
                    last.then_inc(gat_written, 1)

                def one_expert(e, k, another):
                    pe.wait_ge(w_split, 4 * e + 4)
                    pe.wait_ge(xT0_ready, G // 2 * (e + 1))
                    for j in range(NJ):
                        f, n = j % FC, j // FC
                        if j == FC:
                            pe.wait_ge(xT1_ready, G // 2 * (e + 1))
                        pe.wait_ge(h_ready, NJ * e + j + 1)
                        terms = [(c, a, z) for c in range(DC) for a, z in ((0, 0), (0, 1), (1, 0))]
                        for q, (c, a, z) in enumerate(terms):
                            last = pe.matmul(hid[j % 2][:], w1[:, k, a, c * F0 + f * 128:c * F0 + (f + 1) * 128],
                                             xT[:, z, c, n * 512:(n + 1) * 512], start=(q == 0),
                                             stop=(q == len(terms) - 1))
                        last.then_inc(hid_written, 1)
                        if j == 1:
                            pe.wait_ge(x_updated, B * e + B + 2)
                            for t in range(NT):
                                last = pe.transpose(pTb[:, t * S:(t + 1) * S],
                                                    pick[:, 2 * t:2 * t + 2, :].rearrange("p a c -> p (a c)"),
                                                    identh[:])
                            last.then_inc(picks_written, 1)
                    for t in range(NT + 1):
                        if t < NT:
                            pe.wait_ge(lo_ready, NJ * e + (FC if t < NT // NH else NJ) + 2)
                            pe.wait_ge(yf_ready, NT * e + t + 1)
                            terms = [(f, a, z) for f in range(FC) for a, z in ((0, 0), (0, 1), (1, 0))]
                            for q, (f, a, z) in enumerate(terms):
                                last = pe.matmul(yb[t % 2][:, 0:D], hh[:, a, f, t * 128:(t + 1) * 128],
                                                 w2[:, k, z, f * D:(f + 1) * D], start=(q == 0),
                                                 stop=(q == len(terms) - 1))
                            last.then_inc(y_written, 1)
                        if t >= 1:
                            pe.wait_ge(ylo_ready, NT * e + t + 2)
                            if t == 1:
                                pe.wait_ge(pickT_ready, e + 1)
                            for q in range(2):
                                pe.wait_ge(x_updated, B * e + B + 2 * (t - 1) + q + 1)
                                for z in range(2):
                                    last = pe.matmul(sc[q][0:S, 0:D], pickT[CAP * q:CAP * (q + 1), (t - 1) * S:t * S],
                                                     y[CAP * q:CAP * (q + 1), (t - 1) % 2, z, :],
                                                     start=(z == 0), stop=(z == 1))
                                last.then_inc(sc_written, 1)
                        if another and t < G:
                            gather(e + 1, t)

                for g in range(G):
                    gather(0, g)
                each_expert(pe, E0, one_expert)



XA1_BETWEEN = [
    [("T", "norm", 1), ("F", "ctx", 0), ("T", "hT", 0)], [("H", "q2T", 1)], [("F", "xT", 0)],
    [("T", "wo", 0), ("F", "k", 0), ("F", "k", 1), ("F", "q", 0)], [("F", "k", 2)], [("F", "k", 3)],
    [("F", "q1T", 0), ("F", "v", 0)], [("F", "max", 0)], [("F", "v", 1)], [("F", "max", 1)],
    [("F", "v", 2)], [("F", "max", 2)], [("F", "max", 3)], [("F", "max", 4)],
    [("F", "max", 5), ("F", "q2T", 0)], [("F", "max", 6), ("F", "max", 7)],
]
LAG = 2


def xa1_order():
    order = []
    for j in range(H1 + LAG):
        if j < H1:
            order += [("H", "st", j)] + XA1_BETWEEN[j]
        if j >= LAG:
            order.append(("H", "pv", j - LAG))
        if j - LAG == H1 // 2 - 1:
            order.append(("H", "norm", 0))
    return order


XA1_ORDER = xa1_order()


def l1_xattn_stage(core, keep):
    nc, inp = core.nc, core.inp
    NC = H1 // HG
    VW = HD1 + 1
    NP = 4
    with Stage(core, "xa1") as st:
        mean, ve, rstd = (st.sb(n, [S, B]) for n in ("mean", "ve", "rstd"))
        wq = st.sb("wq", [128, DC, D])
        wf = st.sb("wf", [CF, 2, H1 * PAD + D])
        wh, wl = (st.sb(n, [CF, 2, H1 * PAD + D], F16) for n in ("wh", "wl"))
        wo = st.sb("wo", [128, DC, D])
        bo, bq = st.sb("bo", [S, D]), st.sb("bq", [S, D])
        identh = st.sb("identh", [S, S], F16)
        cx = st.sb("cx", [CP, CT, CD])
        xn = st.sb("xn", [S, D])
        xT = st.sb("xT", [128, DC, S])
        cT = st.sb("cT", [CF, 2, 2, C], F16)
        qf = st.sb("qf", [S, D])
        q1 = st.sb("q1", [S, H1, PAD], F16)
        q2 = st.sb("q2", [S, H1, PAD], F16)
        q1T = st.sb("q1T", [128, 2, NC, S], F16)
        q2T = st.sb("q2T", [128, 2, NC, S], F16)
        khi = st.sb("khi", [128, 2, C], F16)
        klow = st.sb("klow", [128, 2, C], F16)
        k1 = st.sb("k1", [128, 2, NC, C], F16)
        k2 = st.sb("k2", [128, 2, NC, C], F16)
        v = st.sb("v", [CP, 2, CT, H1, 2 * VW], F16)
        vf = st.sb("vf", [CP, 2, D])
        top = st.sb("top", [S, H1])
        pT = st.sb("pT", [CP, NP, CT * S])
        ph, pl = (st.sb(n, [CP, NP, CT * S], F16) for n in ("ph", "pl"))
        rtotal = st.sb("rtotal", [S, H1])
        both = st.sb("both", [S, H1, HD1])
        heads = st.sb("heads", [S, D])
        headsT = st.sb("headsT", [128, DC, S])
        add = st.sb("add", [S, D])
        stb = [st.bank("st0"), st.bank("st1")]
        maxb = [st.bank("max0"), st.bank("max1")]
        front = [st.bank("front0"), st.bank("front1")]
        outb, mix = st.bank("outb"), st.bank("mix")
        mixh = mix[:].bitcast(F16)
        (loaded, wf_in, cx_in, const, w_ready, normed, cT_written, cT_ready, cTl_ready, xT_written, xT_ready, q_written, q_step, q_ready,
         q1T_written, q1T_ready, k_written, khi_ready, klow_ready, k1_ready, k2_ready, v_written, v_ready,
         max_written, top_ready, m_ready, q2T_written, q2T_ready, st_written, probs_ready, ph_ready, pl_ready, pv_written,
         norm_step, heads_ready, v_step, headsT_written, headsT_ready, wo_written, x_updated) = (st.sem(n) for n in
            "loaded wf_in cx_in const w_ready normed cT_written cT_ready cTl_ready xT_written xT_ready q_written q_step q_ready "
            "q1T_written q1T_ready k_written khi_ready klow_ready k1_ready k2_ready v_written v_ready "
            "max_written top_ready m_ready q2T_written q2T_ready st_written probs_ready ph_ready pl_ready pv_written norm_step heads_ready v_step "
            "headsT_written headsT_ready wo_written x_updated".split())
        second, first, place = (core.col("pad_masks", n) for n in range(3))

        def loads(sp):
            sp.dma_start(wf[:], inp["w1kv"].rearrange("(c p) n -> p c n", p=CF)).then_inc(wf_in, 16)
            sp.dma_start(cx[:], inp["ctx"][0, :, :].rearrange("(t p) d -> p t d", p=CP)).then_inc(cx_in, 16)
            sp.dma_start(wq[:], inp["w1q"].rearrange("(c p) n -> p c n", p=128)).then_inc(loaded, 16)
            sp.dma_start(wo[:], inp["w1o"].rearrange("(c p) n -> p c n", p=128)).then_inc(loaded, 16)

        stats_stage(core, "xa1_s", core.x_sums, D, S, B, mean[:], ve[:], rstd[:], loads)
        with nc.Block() as block:

            @block.sync
            def _(sp):
                with sp.Fori(1, B) as b:
                    sp.wait_ge(cT_written, 2 * b)
                    sp.dma_start(cx[:], inp["ctx"][bass.ds(b, 1), :, :].rearrange("a (t p) d -> p (a t) d", p=CP))\
                      .then_inc(cx_in, 16)

            @block.gpsimd
            def _(pool):
                def lows(b):
                    for h in range(H1):
                        pool.wait_ge(ph_ready, H1 * b + h + 1)
                        after(pool, pv_written, H1 * b + h + 1 - NP)
                        pool.tensor_tensor(pl[:, h % NP, :], pT[:, h % NP, :], ph[:, h % NP, :], ALU.subtract)\
                            .then_inc(pl_ready, 1)

                lows(0)
                with pool.Fori(1, B) as b:
                    lows(b)

            @block.vector
            def _(dve):
                dve.tensor_scalar(bo[:], core.row("bo1"), core.gate[0:S, 1:2], None, ALU.mult).then_inc(const, 1)
                dve.tensor_scalar(bq[:], core.row("bq1"), HD1 ** -0.5, None, ALU.mult).then_inc(const, 1)
                dve.tensor_copy(identh[:], core.ident[0:S, 0:S]).then_inc(const, 1)
                dve.memset(q2[:], 0.0).then_inc(const, 1)
                dve.memset(v[:], 0.0).then_inc(const, 1)
                dve.wait_ge(const, 5)
                dve.memset(v[:, :, :, :, HD1:VW], 1.0).then_inc(const, 1)
                dve.wait_ge(wf_in, 16)
                dve.tensor_copy(wh[:], wf[:]).then_inc(w_ready, 1)
                dve.wait_ge(w_ready, 1)
                dve.tensor_tensor(wl[:], wf[:], wh[:], ALU.subtract).then_inc(w_ready, 1)

                def normalise(b, half):
                    n = H1 // 2
                    o = outb[0:S, 0:n * 2 * VW].rearrange("p (h d) -> p h d", d=2 * VW)
                    hs, of = slice(half * n, (half + 1) * n), slice(half * n * HD1, (half + 1) * n * HD1)
                    dve.wait_ge(pv_written, H1 * b + (half + 1) * n)
                    dve.reciprocal(rtotal[:, hs], o[:, :, HD1]).then_inc(norm_step, 1)
                    dve.tensor_copy(both[:, hs, :], o[:, :, 0:HD1]).then_inc(norm_step, 1)
                    dve.wait_ge(norm_step, 6 * b + 3 * half + 2)
                    dve.tensor_tensor(both[:, hs, :], both[:, hs, :], o[:, :, VW:VW + HD1], ALU.add)\
                       .then_inc(norm_step, 1)
                    dve.wait_ge(norm_step, 6 * b + 3 * half + 3)
                    dve.tensor_tensor(heads[:, of].rearrange("p (h d) -> p h d", d=HD1), both[:, hs, :],
                                      widen(rtotal[:, hs], 2, HD1), ALU.mult).then_inc(heads_ready, 1)

                def one_round(b, k, heads_on, front_on, tail_on):
                    n, m = b + 1, 1 - k
                    on = {"H": heads_on, "F": front_on, "T": tail_on}
                    for part, what, j in XA1_ORDER:
                        if not on[part]:
                            continue
                        if what == "norm":
                            normalise(b - j, j)
                            if j:
                                dve.wait_ge(heads_ready, 3 * b - 1)
                                dve.tensor_tensor(heads[:], heads[:], core.row("bv1"), ALU.add)\
                                   .then_inc(heads_ready, 1)
                        if what == "wo":
                            xb = core.x[:, bass.ds(b - 1, 1), :].rearrange("p a c -> p (a c)")
                            dve.wait_ge(wo_written, b)
                            dve.scalar_tensor_tensor(out=add[:], in0=mix[0:S, 0:D], scalar=core.gate[0:S, 1:2],
                                                     in1=bo[:], op0=ALU.mult, op1=ALU.add).then_inc(x_updated, 1)
                            dve.wait_ge(x_updated, 2 * b - 1)
                            dve.tensor_tensor(xb, xb, add[:], ALU.add).then_inc(x_updated, 1)
                            dve.wait_ge(x_updated, 2 * b)
                            dve.bn_stats(core.x_sums[:, bass.ds(b - 1, 1), :].rearrange("p a b -> p (a b)"), xb)
                        if what == "ctx":
                            xb = core.x[:, bass.ds(n, 1), :].rearrange("p a c -> p (a c)")
                            after(dve, xT_written, n)
                            dve.tensor_scalar(xn[:], xb, mean[:, bass.ds(n, 1)], rstd[:, bass.ds(n, 1)],
                                              ALU.subtract, ALU.mult).then_inc(normed, 1)
                            for c in range(2):
                                dve.wait_ge(cT_ready, 2 * n + c + 1)
                                dve.tensor_tensor(cT[:, c, 1, :], front[c][0:CF, 0:C], cT[:, c, 0, :], ALU.subtract)\
                                   .then_inc(cTl_ready, 1)
                        if what == "q":
                            dve.wait_ge(q_written, n + 1)
                            dve.scalar_tensor_tensor(out=qf[:], in0=mix[0:S, 0:D], scalar=HD1 ** -0.5, in1=bq[:],
                                                     op0=ALU.mult, op1=ALU.add).then_inc(q_step, 1)
                            dve.wait_ge(q_step, 2 * n + 1)
                            q3 = qf[:].rearrange("p (h d) -> p h d", d=HD1)
                            dve.tensor_copy(q1[:].rearrange("p h (two d) -> p h two d", two=2),
                                            widen(q3, 2, 2)).then_inc(q_step, 1)
                            dve.wait_ge(q_step, 2 * n + 2)
                            dve.tensor_tensor(q2[:, :, 0:HD1], q3, q1[:, :, 0:HD1], ALU.subtract).then_inc(q_ready, 1)
                        if what == "k":
                            dve.wait_ge(khi_ready, NC * n + j + 1)
                            dve.tensor_scalar(klow[:, j % 2, :], khi[:, j % 2, :], second, None, ALU.mult)\
                               .then_inc(klow_ready, 1)
                            dve.tensor_scalar(k2[:, m, j, :], khi[:, j % 2, :], first, place, ALU.mult, ALU.add)\
                               .then_inc(k2_ready, 1)
                            dve.wait_ge(klow_ready, NC * n + j + 1)
                            dve.scalar_tensor_tensor(out=k1[:, m, j, :], in0=front[j % 2][:, 0:C],
                                                     scalar=core.col("bk", j), in1=klow[:, j % 2, :], op0=ALU.add,
                                                     op1=ALU.subtract).then_inc(k1_ready, 1)
                        if what == "v":
                            dve.wait_ge(v_step, 2 * (CT * n + j) + 2)
                            dve.tensor_tensor(v[:, m, j, :, VW:VW + HD1],
                                              vf[:, j % 2, :].rearrange("p (h d) -> p h d", d=HD1),
                                              v[:, m, j, :, 0:HD1], ALU.subtract).then_inc(v_ready, 1)
                        if what == "max":
                            for h in (2 * j, 2 * j + 1):
                                dve.wait_ge(max_written, H1 * n + h + 1)
                                dve.tensor_reduce(top[:, h:h + 1], maxb[h % 2][0:S, 0:C], AX.X, ALU.max, negate=True)\
                                   .then_inc(top_ready, 1)
                            if j % 2:
                                c = j // 2
                                dve.wait_ge(top_ready, H1 * n + HG * (c + 1))
                                dve.tensor_copy(q2[:, HG * c:HG * (c + 1), HD1], top[:, HG * c:HG * (c + 1)])\
                                   .then_inc(m_ready, 1)

                rounds(dve, one_round)

            @block.scalar
            def _(act):
                act.wait_ge(const, 6)

                def one_round(b, k, heads_on, front_on, tail_on):
                    n, m = b + 1, 1 - k
                    on = {"H": heads_on, "F": front_on, "T": tail_on}
                    for part, what, j in XA1_ORDER:
                        if not on[part]:
                            continue
                        if what == "st":
                            act.wait_ge(st_written, H1 * b + j + 1)
                            after(act, pv_written, H1 * b + j + 1 - NP)
                            act.activation(pT[:, j % NP, :], stb[j % 2][0:CP, 0:CT * S], ACT.Exp)\
                               .then_inc(probs_ready, 1)
                            act.wait_ge(probs_ready, H1 * b + j + 1)
                            act.activation(ph[:, j % NP, :], pT[:, j % NP, :], ACT.Copy).then_inc(ph_ready, 1)
                        if what == "hT":
                            act.wait_ge(headsT_written, b)
                            act.activation(headsT[:].rearrange("p c s -> p (c s)"), mix[:, 0:DC * S], ACT.Copy)\
                               .then_inc(headsT_ready, 1)
                        if what == "ctx":
                            for c in range(2):
                                act.wait_ge(cT_written, 2 * n + c + 1)
                                act.activation(cT[:, c, 0, :], front[c][0:CF, 0:C], ACT.Copy).then_inc(cT_ready, 1)
                        if what == "xT":
                            act.wait_ge(xT_written, n + 1)
                            act.activation(xT[:].rearrange("p c s -> p (c s)"), mix[:, 0:DC * S], ACT.Copy)\
                               .then_inc(xT_ready, 1)
                        if what == "q1T":
                            act.wait_ge(q1T_written, n + 1)
                            act.activation(q1T[:, m, :, :].rearrange("p c s -> p (c s)"), mixh[:, 0:NC * S],
                                           ACT.Copy).then_inc(q1T_ready, 1)
                        if what == "q2T":
                            at, par = (b, k) if j else (n, m)
                            act.wait_ge(q2T_written, 2 * at + j + 1)
                            act.activation(q2T[:, par, 2 * j:2 * j + 2, :].rearrange("p c s -> p (c s)"),
                                           mixh[:, 0:2 * S], ACT.Copy).then_inc(q2T_ready, 1)
                        if what == "k":
                            act.wait_ge(k_written, NC * n + j + 1)
                            after(act, k1_ready, NC * n + j - 1)
                            act.activation(khi[:, j % 2, :], front[j % 2][:, 0:C], ACT.Identity,
                                           bias=core.col("bk", j)).then_inc(khi_ready, 1)
                        if what == "v":
                            act.wait_ge(v_written, CT * n + j + 1)
                            after(act, v_ready, CT * n + j - 1)
                            act.activation(vf[:, j % 2, :], front[j % 2][0:CP, 0:D], ACT.Copy).then_inc(v_step, 1)
                            act.wait_ge(v_step, 2 * (CT * n + j) + 1)
                            act.activation(v[:, m, j, :, 0:HD1],
                                           vf[:, j % 2, :].rearrange("p (h d) -> p h d", d=HD1), ACT.Copy)\
                               .then_inc(v_step, 1)

                rounds(act, one_round)

            @block.tensor
            def _(pe):
                idc, ids = core.ident[0:CP, 0:CP], core.ident[0:S, 0:S]
                terms = [(c, w, z) for c in range(2) for w, z in ((wh, 0), (wh, 1), (wl, 0))]
                pe.wait_ge(loaded, 32)
                pe.wait_ge(const, 6)
                pe.wait_ge(w_ready, 2)

                def one_round(b, k, heads_on, front_on, tail_on):
                    n, m = b + 1, 1 - k
                    on = {"H": heads_on, "F": front_on, "T": tail_on}
                    for part, what, j in XA1_ORDER:
                        if not on[part]:
                            continue
                        if what == "st":
                            r, c = PAD * (j % HG), j // HG
                            pe.wait_ge(q2T_ready, 2 * b + 1 + j // 8)
                            after(pe, probs_ready, H1 * b + j - 1)
                            for t in range(CT):
                                o, at = stb[j % 2][0:CP, t * S:(t + 1) * S], slice(t * CP, (t + 1) * CP)
                                pe.matmul(o, k1[r:r + PAD, k, c, at], q1T[r:r + PAD, k, c, :], start=True,
                                          stop=False, tile_position=(r, 0))
                                last = pe.matmul(o, k2[r:r + PAD, k, c, at], q2T[r:r + PAD, k, c, :], start=False,
                                                 stop=True, tile_position=(r, 0))
                            last.then_inc(st_written, 1)
                        if what == "pv":
                            pe.wait_ge(pl_ready, H1 * b + j + 1)
                            if j == 0:
                                pe.wait_ge(v_ready, CT * (b + 1))
                            if j == 0:
                                after(pe, heads_ready, 3 * b - 1)
                            if j == H1 // 2:
                                pe.wait_ge(heads_ready, 3 * b + 1)
                            o = outb[0:S, j % 8 * 2 * VW:(j % 8 + 1) * 2 * VW]
                            at = [slice(t * S, (t + 1) * S) for t in range(CT)]
                            for t in range(CT):
                                ends = (t == 0, t == CT - 1)
                                if t == CT - 1:
                                    pe.matmul(o[:, 0:VW], pl[:, j % NP, at[t]], v[:, k, t, j, 0:VW], start=False,
                                              stop=False, skip_group_check=True)
                                last = pe.matmul(o, ph[:, j % NP, at[t]], v[:, k, t, j, :], start=ends[0],
                                                 stop=ends[1])
                                if t < CT - 1:
                                    pe.matmul(o[:, 0:VW], pl[:, j % NP, at[t]], v[:, k, t, j, 0:VW], start=False,
                                              stop=False, skip_group_check=True)
                            last.then_inc(pv_written, 1)
                        if what == "hT":
                            pe.wait_ge(heads_ready, 3 * b)
                            if heads_on:
                                pe.wait_ge(q2T_ready, 2 * b + 1)
                            for c in range(DC):
                                last = pe.transpose(mix[:, c * S:(c + 1) * S], heads[:, c * 128:(c + 1) * 128], ids)
                            last.then_inc(headsT_written, 1)
                        if what == "wo":
                            pe.wait_ge(headsT_ready, b)
                            if front_on:
                                pe.wait_ge(xT_ready, n + 1)
                            elif heads_on:
                                pe.wait_ge(q2T_ready, 2 * b + 2)
                            for c in range(DC):
                                last = pe.matmul(mix[0:S, 0:D], headsT[:, c, :], wo[:, c, :], start=(c == 0),
                                                 stop=(c == DC - 1))
                            last.then_inc(wo_written, 1)
                        if what == "ctx":
                            pe.wait_ge(cx_in, 16 * n + 16)
                            after(pe, v_step, 2 * CT * n)
                            for c in range(2):
                                for t in range(CT):
                                    last = pe.transpose(front[c][0:CF, t * CP:(t + 1) * CP],
                                                        cx[:, t, c * CF:(c + 1) * CF], idc)
                                last.then_inc(cT_written, 1)
                        if what == "xT":
                            pe.wait_ge(normed, n + 1)
                            after(pe, q2T_ready, 2 * n)
                            for c in range(DC):
                                last = pe.transpose(mix[:, c * S:(c + 1) * S], xn[:, c * 128:(c + 1) * 128], ids)
                            last.then_inc(xT_written, 1)
                        if what == "q":
                            pe.wait_ge(xT_ready, n + 1)
                            if tail_on:
                                pe.wait_ge(x_updated, 2 * b - 1)
                            for c in range(DC):
                                last = pe.matmul(mix[0:S, 0:D], xT[:, c, :], wq[:, c, :], start=(c == 0),
                                                 stop=(c == DC - 1))
                            last.then_inc(q_written, 1)
                        if what == "q1T":
                            pe.wait_ge(q_ready, n + 1)
                            for c in range(NC):
                                last = pe.transpose(mixh[:, c * S:(c + 1) * S],
                                                    q1[:, HG * c:HG * (c + 1), :].rearrange("p h d -> p (h d)"),
                                                    identh[:])
                            last.then_inc(q1T_written, 1)
                        if what == "q2T":
                            at = b if j else n
                            pe.wait_ge(m_ready, NC * at + 2 * j + 2)
                            if j:
                                pe.wait_ge(q2T_ready, 2 * b + 1)
                                after(pe, headsT_ready, b)
                            else:
                                pe.wait_ge(q1T_ready, n + 1)
                            for c in range(2 * j, 2 * j + 2):
                                last = pe.transpose(mixh[:, (c - 2 * j) * S:(c - 2 * j + 1) * S],
                                                    q2[:, HG * c:HG * (c + 1), :].rearrange("p h d -> p (h d)"),
                                                    identh[:])
                            last.then_inc(q2T_written, 1)
                        if what == "k":
                            pe.wait_ge(cTl_ready, 2 * n + 2)
                            if j >= 2:
                                pe.wait_ge(k1_ready, NC * n + j - 1)
                            for q, (c, w, z) in enumerate(terms):
                                last = pe.matmul(front[j % 2][:, 0:C], w[:, c, j * 128:(j + 1) * 128],
                                                 cT[:, c, z, :], start=(q == 0), stop=(q == len(terms) - 1))
                            last.then_inc(k_written, 1)
                        if what == "v":
                            if j < 2:
                                pe.wait_ge(k1_ready, NC * n + 3 + j)
                            else:
                                pe.wait_ge(v_step, 2 * CT * n + 1)
                            for q, (c, w, z) in enumerate(terms):
                                last = pe.matmul(front[j % 2][0:CP, 0:D], cT[:, c, z, j * CP:(j + 1) * CP],
                                                 w[:, c, H1 * PAD:], start=(q == 0), stop=(q == len(terms) - 1))
                            last.then_inc(v_written, 1)
                        if what == "max":
                            c = 2 * j // HG
                            pe.wait_ge(q1T_ready, n + 1)
                            pe.wait_ge(k1_ready, NC * n + c + 1)
                            pe.wait_ge(k2_ready, NC * n + c + 1)
                            for h in (2 * j, 2 * j + 1):
                                r = PAD * (h % HG)
                                after(pe, top_ready, H1 * n + h - 1)
                                pe.matmul(maxb[h % 2][0:S, 0:C], q1T[r:r + PAD, m, c, :], k1[r:r + PAD, m, c, :],
                                          start=True, stop=True, tile_position=(r, 0)).then_inc(max_written, 1)

                rounds(pe, one_round)


def load_mixture(core, sp, e):
    for dst, name in zip(core.mf, ("m_w1", "m_w3", "m_w2")):
        sp.dma_start(dst[:].rearrange("p (c f) -> p c f", f=F1 if name != "m_w2" else D),
                     core.inp[name][bass.ds(e, 1), :, :].rearrange("a (c p) f -> p (a c) f", p=128))\
          .then_inc(core.m_in, 16)


def split_mixture(core, pool, e, k):
    pool.wait_ge(core.m_in, 48 * e + 48)
    pool.sem_inc(core.m_held, 1)
    for n in range(3):
        pool.tensor_copy(core.mw[n][:, k, 0, :], core.mf[n][:]).then_inc(core.m_split, 1)
    pool.wait_ge(core.m_split, 6 * e + 3)
    for n in range(3):
        pool.tensor_tensor(core.mw[n][:, k, 1, :], core.mf[n][:], core.mw[n][:, k, 0, :], ALU.subtract)\
            .then_inc(core.m_split, 1)


SA_ORDER = [
    ("F", "norm", 0), ("H", "sc", 0), ("T", "hT", 0), ("H", "sc", 1), ("F", "x", 0), ("H", "sc", 2), ("T", "wo", 0),
    ("F", "v", 0), ("H", "pt", 0), ("H", "sc", 3), ("H", "pv", 0), ("H", "pt", 1), ("F", "qk", 0), ("F", "rot", 0),
    ("T", "hn", 0), ("H", "pv", 1), ("H", "pt", 2), ("T", "router", 0), ("F", "qkT", 0), ("H", "pv", 2),
    ("H", "pt", 3), ("F", "qkT", 1), ("H", "pv", 3), ("H", "out", 0),
]


def l1_self_attn_stage(core, keep):
    nc, inp = core.nc, core.inp
    NC = H1 // HG
    core.base = keep("base", [S, B, D])
    core.hT = keep("hT", [128, 2, DC, B * S], F16)
    core.logits = keep("logits", [S, B, E1])
    core.mf = [keep(n, [128, 2 * F1]) for n in ("m_w1f", "m_w3f", "m_w2f")]
    core.mw = [keep(n, [128, 2, 2, 2 * F1], F16) for n in ("m_w1", "m_w3", "m_w2")]
    with Stage(core, "sa") as st:
        mean, ve, rstd, ms, rms = (st.sb(n, [S, B]) for n in ("mean", "ve", "rstd", "ms", "rms"))
        wqk = st.sb("wqk", [128, DC, 2 * D])
        wv = st.sb("wv", [128, DC, D])
        wo = st.sb("wo", [128, DC, D])
        router = st.sb("router", [128, DC, E1])
        freqs = st.sb("freqs", [S, HD1])
        cosr, sinr = st.sb("cosr", [S, HD1]), st.sb("sinr", [S, HD1])
        causal = st.sb("causal", [S, S])
        xr = st.sb("xr", [S, D])
        xT = st.sb("xT", [128, DC, S])
        t1, t2 = st.sb("t1", [S, 2 * D]), st.sb("t2", [S, 2 * D])
        qk = st.sb("qk", [S, 2 * H1, PAD])
        qkT = st.sb("qkT", [128, 2, 2 * NC, S])
        v = st.sb("v", [S, 2, D])
        sm = st.sb("sm", [S, H1, S])
        top = st.sb("top", [S, H1])
        probs = st.sb("probs", [S, H1, S])
        total, rtotal = st.sb("total", [S, H1]), st.sb("rtotal", [S, H1])
        pT = st.sb("pT", [S, NC, HG * S])
        heads = st.sb("heads", [S, D])
        headsT = st.sb("headsT", [128, DC, S])
        sq = st.sb("sq", [S, D])
        hss, hrr = st.sb("hss", [S, 1]), st.sb("hrr", [S, 1])
        h = st.sb("h", [S, D])
        hn = st.sb("hn", [S, D])
        hTf = st.sb("hTf", [128, DC, S])
        scoreb = [st.bank("score0"), st.bank("score1")]
        probb = [st.bank("prob0"), st.bank("prob1")]
        fa, fb, po, pm = st.bank("fa"), st.bank("fb"), st.bank("po"), st.bank("pm")
        (loaded, ready_once, n_ready, xr_ready, xT_written, xT_ready, qk_written, qk_step, qk_ready, v_written,
         v_ready, qkT_written, qkT_ready, score_written, sm_ready, top_ready, probs_ready, pT_written, pT_ready,
         out_written, heads_ready, headsT_written, headsT_ready, wo_written, h_ready, hss_ready, hrr_ready, hn_ready,
         hnT_written, hTf_ready, hTh_ready, router_written, dve_step, hT_kept, held) = (st.sem(n) for n in
            "loaded ready_once n_ready xr_ready xT_written xT_ready qk_written qk_step qk_ready v_written "
            "v_ready qkT_written qkT_ready score_written sm_ready top_ready probs_ready pT_written pT_ready "
            "out_written heads_ready headsT_written headsT_ready wo_written h_ready hss_ready hrr_ready hn_ready "
            "hnT_written hTf_ready hTh_ready router_written dve_step hT_kept held".split())
        core.m_in, core.m_split, core.m_held = st.sem("m_in"), st.sem("m_split"), st.sem("m_held")

        def loads(sp):
            for dst, src in ((wqk, "s_wqk"), (wv, "s_wv"), (wo, "s_wo"), (router, "router")):
                sp.dma_start(dst[:], inp[src].rearrange("(c p) n -> p c n", p=128)).then_inc(loaded, 16)
            sp.dma_start(freqs[:], inp["freqs"][0:S, :]).then_inc(loaded, 16)
            sp.dma_start(causal[:], inp["causal"]).then_inc(loaded, 16)
            load_mixture(core, sp, 0)

        stats_stage(core, "sa_s", core.x_sums, D, S, B, mean[:], ve[:], rstd[:], loads)
        with nc.Block() as block:

            @block.vector
            def _(dve):
                step = Chain(dve, dve_step)
                dve.wait_ge(loaded, 96)
                pair = lambda a: a[:].rearrange("p (k two) -> p k two", two=2)
                cos, sin = pair(freqs)[:, :, 0:1], pair(freqs)[:, :, 1:2]
                step(dve.tensor_copy(pair(cosr), cos.broadcast_to([S, HD1 // 2, 2])))
                step(dve.tensor_scalar(pair(sinr)[:, :, 0:1], sin, -1.0, None, ALU.mult))
                step(dve.tensor_copy(pair(sinr)[:, :, 1:2], sin))
                step(dve.memset(qk[:], 0.0))
                step(dve.tensor_scalar(ms[:], ve[:], -LN_EPS, None, ALU.add))
                step(dve.tensor_tensor(ms[:], ms[:], rstd[:], ALU.mult))
                step(dve.tensor_tensor(ms[:], ms[:], rstd[:], ALU.mult))
                dve.tensor_scalar(ms[:], ms[:], RMS_EPS, None, ALU.add).then_inc(ready_once, 1)
                dve.wait_ge(ready_once, 2)

                def one_round(b, k, heads_on, front_on, tail_on):
                    n = b + 1
                    on = {"H": heads_on, "F": front_on, "T": tail_on}
                    for part, what, j in SA_ORDER:
                        if not on[part]:
                            continue
                        if what == "norm":
                            xb = core.x[:, bass.ds(n, 1), :].rearrange("p a c -> p (a c)")
                            nb = core.base[:, bass.ds(n, 1), :].rearrange("p a c -> p (a c)")
                            dve.tensor_scalar(nb, xb, mean[:, bass.ds(n, 1)], rstd[:, bass.ds(n, 1)],
                                              ALU.subtract, ALU.mult).then_inc(n_ready, 1)
                            after(dve, xT_written, n)
                            dve.wait_ge(n_ready, n + 1)
                            dve.tensor_scalar(xr[:], nb, rms[:, bass.ds(n, 1)], None, ALU.mult).then_inc(xr_ready, 1)
                        if what == "rot":
                            dve.wait_ge(qk_written, n + 1)
                            src = fa[0:S, :].rearrange("p (h d) -> p h d", d=HD1)
                            src2 = fa[0:S, :].rearrange("p (h k two) -> p h k two", k=HD1 // 2, two=2)
                            rot = t2[:].rearrange("p (h k two) -> p h k two", k=HD1 // 2, two=2)
                            dve.tensor_tensor(t1[:].rearrange("p (h d) -> p h d", d=HD1), src,
                                              widen(cosr[:], 1, 2 * H1), ALU.mult).then_inc(qk_step, 1)
                            for z in range(2):
                                dve.tensor_tensor(rot[:, :, :, z], src2[:, :, :, 1 - z],
                                                  widen(pair(sinr)[:, :, z], 1, 2 * H1), ALU.mult).then_inc(qk_step, 1)
                            dve.wait_ge(qk_step, 3 * n + 3)
                            dve.tensor_tensor(qk[:, :, 0:HD1], t1[:].rearrange("p (h d) -> p h d", d=HD1),
                                              t2[:].rearrange("p (h d) -> p h d", d=HD1), ALU.add)\
                               .then_inc(qk_ready, 1)
                        if what == "sc":
                            of = slice(j * NC, (j + 1) * NC)
                            dve.wait_ge(score_written, HG * b + j + 1)
                            dve.scalar_tensor_tensor(out=sm[:, of, :],
                                                     in0=scoreb[j % 2][0:S, 0:NC * S].rearrange(
                                                         "p (j s) -> p j s", j=NC),
                                                     scalar=HD1 ** -0.5, in1=widen(causal[:], 1, NC), op0=ALU.mult,
                                                     op1=ALU.add).then_inc(sm_ready, 1)
                            dve.wait_ge(sm_ready, HG * b + j + 1)
                            dve.tensor_reduce(top[:, of], sm[:, of, :], AX.X, ALU.max, negate=True)\
                               .then_inc(top_ready, 1)
                        if what == "pt":
                            dve.wait_ge(pT_written, HG * b + j + 1)
                            dve.tensor_copy(pT[:, j, :], probb[j % 2][0:S, 0:NC * S]).then_inc(pT_ready, 1)
                        if what == "out":
                            dve.wait_ge(probs_ready, H1 * b + H1)
                            dve.reciprocal(rtotal[:], total[:]).then_inc(heads_ready, 1)
                            dve.wait_ge(heads_ready, 2 * b + 1)
                            dve.wait_ge(out_written, b + 1)
                            dve.tensor_tensor(heads[:].rearrange("p (j r d) -> p r j d", r=HG, d=HD1),
                                              po[0:S, 0:D].rearrange("p (r j d) -> p r j d", r=HG, d=HD1),
                                              widen(rtotal[:].rearrange("p (r j) -> p r j", r=HG), 3, HD1), ALU.mult)\
                               .then_inc(heads_ready, 1)
                        if what == "wo":
                            nb = core.base[:, bass.ds(b - 1, 1), :].rearrange("p a c -> p (a c)")
                            dve.wait_ge(wo_written, b)
                            dve.tensor_tensor(h[:], nb, pm[0:S, 0:D], ALU.add).then_inc(h_ready, 1)
                            dve.wait_ge(h_ready, b)
                            dve.sem_inc(held, 1)
                            dve.tensor_tensor_reduce(out=sq[:], in0=h[:], in1=h[:], scale=1.0, scalar=0.0,
                                                     op0=ALU.mult, op1=ALU.add, accum_out=hss[:])\
                               .then_inc(hss_ready, 1)
                            dve.wait_ge(hss_ready, 2 * b - 1)
                            dve.tensor_scalar(hss[:], hss[:], 1.0 / D, RMS_EPS, ALU.mult, ALU.add)\
                               .then_inc(hss_ready, 1)
                            dve.tensor_scalar(nb, h[:], 1.0, None, ALU.mult)
                        if what == "pt" and j == 0 and tail_on:
                            dve.wait_ge(hrr_ready, b)
                            dve.tensor_scalar(hn[:], h[:], hrr[:], None, ALU.mult).then_inc(hn_ready, 1)
                        if what == "hn" and not heads_on:
                            dve.wait_ge(hrr_ready, b)
                            dve.tensor_scalar(hn[:], h[:], hrr[:], None, ALU.mult).then_inc(hn_ready, 1)
                        if what == "router":
                            dve.wait_ge(hTf_ready, 2 * b)
                            hi, lo = (core.hT[:, z, :, bass.ds((b - 1) * S, S)] for z in range(2))
                            dve.tensor_scalar(hi, hTf[:], 1.0, None, ALU.mult).then_inc(hTh_ready, 1)
                            dve.wait_ge(hTh_ready, b)
                            dve.tensor_tensor(lo, hTf[:], hi, ALU.subtract).then_inc(hT_kept, 1)
                            dve.wait_ge(router_written, b)
                            dve.tensor_scalar(core.logits[:, bass.ds(b - 1, 1), :].rearrange("p a e -> p (a e)"),
                                              pm[0:S, 0:E1], 1.0, None, ALU.mult).then_inc(hT_kept, 1)

                rounds(dve, one_round)

            @block.gpsimd
            def _(pool):
                pool.wait_ge(ready_once, 1)
                pool.tensor_tensor(rms[:], ms[:], core.half[0:S, 0:B], ALU.pow).then_inc(ready_once, 1)
                split_mixture(core, pool, 0, 0)
                with pool.Fori(0, B) as b:
                    pool.wait_ge(hss_ready, 2 * b + 2)
                    pool.tensor_tensor(hrr[:], hss[:], core.half[0:S, 0:1], ALU.pow).then_inc(hrr_ready, 1)

            @block.scalar
            def _(act):

                def one_round(b, k, heads_on, front_on, tail_on):
                    n, m = b + 1, 1 - k
                    on = {"H": heads_on, "F": front_on, "T": tail_on}
                    for part, what, j in SA_ORDER:
                        if not on[part]:
                            continue
                        if what == "x":
                            act.wait_ge(xT_written, n + 1)
                            for c in range(DC):
                                act.activation(xT[:, c, :], fb[:, c * S:(c + 1) * S], ACT.Copy,
                                               scale=core.col("attn_w", c)).then_inc(xT_ready, 1)
                        if what == "v":
                            act.wait_ge(v_written, n + 1)
                            act.activation(v[:, m, :], fb[0:S, 0:D], ACT.Copy).then_inc(v_ready, 1)
                        if what == "qkT":
                            act.wait_ge(qkT_written, 2 * n + j + 1)
                            act.activation(qkT[:, m, j * NC:(j + 1) * NC, :].rearrange("p c s -> p (c s)"),
                                           (fa, fb)[j][:, 0:NC * S], ACT.Copy).then_inc(qkT_ready, 1)
                        if what == "sc":
                            act.wait_ge(top_ready, HG * b + j + 1)
                            for h in range(NC * j, NC * (j + 1)):
                                act.activation(probs[:, h, :], sm[:, h, :], ACT.Exp, bias=top[:, h:h + 1],
                                               accum_out=total[:, h:h + 1]).then_inc(probs_ready, 1)
                        if what == "hT":
                            act.wait_ge(headsT_written, b)
                            act.activation(headsT[:].rearrange("p c s -> p (c s)"), pm[:, 0:DC * S], ACT.Copy)\
                               .then_inc(headsT_ready, 1)
                        if what == "hn":
                            act.wait_ge(hnT_written, b)
                            for c in range(DC):
                                act.activation(hTf[:, c, :], pm[:, c * S:(c + 1) * S], ACT.Copy,
                                               scale=core.col("ffn_w", c)).then_inc(hTf_ready, 1)

                rounds(act, one_round)

            @block.tensor
            def _(pe):
                ids = core.ident[0:S, 0:S]
                pe.wait_ge(loaded, 96)

                def one_round(b, k, heads_on, front_on, tail_on):
                    n, m = b + 1, 1 - k
                    on = {"H": heads_on, "F": front_on, "T": tail_on}
                    for part, what, j in SA_ORDER:
                        if not on[part]:
                            continue
                        if what == "x":
                            pe.wait_ge(xr_ready, n + 1)
                            after(pe, qkT_ready, 2 * n)
                            for c in range(DC):
                                last = pe.transpose(fb[:, c * S:(c + 1) * S], xr[:, c * 128:(c + 1) * 128], ids)
                            last.then_inc(xT_written, 1)
                        if what == "v":
                            pe.wait_ge(xT_ready, 2 * n + 2)
                            for c in range(DC):
                                last = pe.matmul(fb[0:S, 0:D], xT[:, c, :], wv[:, c, :], start=(c == 0),
                                                 stop=(c == DC - 1))
                            last.then_inc(v_written, 1)
                        if what == "qk":
                            for c in range(DC):
                                last = pe.matmul(fa[0:S, :], xT[:, c, :], wqk[:, c, :], start=(c == 0),
                                                 stop=(c == DC - 1))
                            last.then_inc(qk_written, 1)
                        if what == "qkT":
                            pe.wait_ge(qk_ready if j == 0 else v_ready, n + 1)
                            for c in range(NC):
                                q = j * NC + c
                                last = pe.transpose((fa, fb)[j][:, c * S:(c + 1) * S],
                                                    qk[:, q * HG:(q + 1) * HG, :].rearrange("p h d -> p (h d)"), ids)
                            last.then_inc(qkT_written, 1)
                        if what == "sc":
                            if j == 0:
                                pe.wait_ge(qkT_ready, 2 * b + 2)
                            after(pe, sm_ready, HG * b + j - 1)
                            at = slice(PAD * j, PAD * j + HD1)
                            for c in range(NC):
                                last = pe.matmul(scoreb[j % 2][0:S, c * S:(c + 1) * S], qkT[at, k, c, :],
                                                 qkT[at, k, NC + c, :], start=True, stop=True,
                                                 tile_position=(PAD * j, 0))
                            last.then_inc(score_written, 1)
                        if what == "pt":
                            pe.wait_ge(probs_ready, H1 * b + NC * (j + 1))
                            after(pe, pT_ready, HG * b + j - 1)
                            for c in range(NC):
                                last = pe.transpose(probb[j % 2][0:S, c * S:(c + 1) * S], probs[:, j * NC + c, :],
                                                    ids)
                            last.then_inc(pT_written, 1)
                        if what == "pv":
                            pe.wait_ge(pT_ready, HG * b + j + 1)
                            if j == 0:
                                pe.wait_ge(v_ready, b + 1)
                                after(pe, heads_ready, 2 * b)
                            for c in range(NC):
                                h, o = HG * c + j, (j * NC + c) * HD1
                                last = pe.matmul(po[0:S, o:o + HD1], pT[:, j, c * S:(c + 1) * S],
                                                 v[:, k, h * HD1:(h + 1) * HD1], start=True, stop=True)
                            if j == HG - 1:
                                last.then_inc(out_written, 1)
                        if what == "hT":
                            pe.wait_ge(heads_ready, 2 * b)
                            after(pe, hT_kept, 2 * (b - 1))
                            for c in range(DC):
                                last = pe.transpose(pm[:, c * S:(c + 1) * S], heads[:, c * 128:(c + 1) * 128], ids)
                            last.then_inc(headsT_written, 1)
                        if what == "wo":
                            pe.wait_ge(headsT_ready, b)
                            for c in range(DC):
                                last = pe.matmul(pm[0:S, 0:D], headsT[:, c, :], wo[:, c, :], start=(c == 0),
                                                 stop=(c == DC - 1))
                            last.then_inc(wo_written, 1)
                        if what == "hn":
                            pe.wait_ge(hn_ready, b)
                            for c in range(DC):
                                last = pe.transpose(pm[:, c * S:(c + 1) * S], hn[:, c * 128:(c + 1) * 128], ids)
                            last.then_inc(hnT_written, 1)
                        if what == "router":
                            pe.wait_ge(hTf_ready, 2 * b)
                            for c in range(DC):
                                last = pe.matmul(pm[0:S, 0:E1], hTf[:, c, :], router[:, c, :], start=(c == 0),
                                                 stop=(c == DC - 1))
                            last.then_inc(router_written, 1)

                rounds(pe, one_round)


def experts1_stage(core, keep):
    nc, inp = core.nc, core.inp
    FC = F1 // 128
    SEQ = 4
    NB = B // SEQ
    W = SEQ * S
    NJ = FC * NB
    with Stage(core, "ex1") as st:
        combine = st.sb("combine", [S, B, E1])
        l2, eq, run, sel = (st.sb(n, [S, B, E1]) for n in ("l2", "eq", "run", "sel"))
        mx, tot = st.sb("mx", [S, B]), st.sb("tot", [S, B])
        w, w_split = core.mw, core.m_split
        g = st.sb("g", [128, 2, W])
        p = st.sb("p", [128, 2, W])
        ph = st.sb("ph", [128, 2, FC, B * S], F16)
        ub = [st.bank("u0"), st.bank("u1")]
        zb = [st.bank("z0"), st.bank("z1")]
        yb = [st.bank(f"y{n}") for n in range(4)]
        (u_written, z_written, g_ready, p_ready, ph_ready, pl_ready, y_written, x_updated, dve_step,
         exp_ready, diff_ready, held) = (st.sem(n) for n in
            "u_written z_written g_ready p_ready ph_ready pl_ready y_written x_updated dve_step "
            "exp_ready diff_ready held".split())
        with nc.Block() as block:

            @block.sync
            def _(sp):
                with sp.Fori(1, E1) as e:
                    sp.wait_ge(w_split, 6 * e)
                    load_mixture(core, sp, e)

            @block.gpsimd
            def _(pool):
                with pool.Fori(0, E1 // 2 - 1) as i:
                    for e, k in ((2 * i + 1, 1), (2 * i + 2, 0)):
                        pool.wait_ge(x_updated, B * e + 4)
                        split_mixture(core, pool, e, k)
                pool.wait_ge(x_updated, B * (E1 - 1) + 4)
                split_mixture(core, pool, E1 - 1, 1)

            @block.vector
            def _(dve):
                dve.sem_inc(x_updated, B + 4)
                dve.sem_inc(p_ready, 2)
                dve.sem_inc(pl_ready, 2)
                step = Chain(dve, dve_step)
                step(dve.tensor_reduce(mx[:], core.logits[:], AX.X, ALU.max))
                dve.tensor_tensor(l2[:], core.logits[:], widen(mx[:], 2, E1), ALU.subtract).then_inc(diff_ready, 1)
                dve.wait_ge(diff_ready, 1)
                step(dve.memset(sel[:], 0.0))
                for n in range(TOP):
                    step(dve.tensor_reduce(mx[:], l2[:], AX.X, ALU.max))
                    step(dve.tensor_tensor(eq[:], l2[:], widen(mx[:], 2, E1), ALU.is_equal))
                    step(dve.tensor_copy(run[:, :, 0:1], eq[:, :, 0:1]))
                    for c in range(1, E1):
                        step(dve.tensor_tensor(run[:, :, c:c + 1], run[:, :, c - 1:c], eq[:, :, c:c + 1], ALU.add))
                    step(dve.tensor_scalar(run[:], run[:], 1.0, None, ALU.is_equal))
                    step(dve.tensor_tensor(eq[:], eq[:], run[:], ALU.mult))
                    step(dve.tensor_tensor(sel[:], sel[:], eq[:], ALU.add))
                    if n == 0:
                        dve.wait_ge(exp_ready, 1)
                    step(dve.scalar_tensor_tensor(out=l2[:], in0=eq[:], scalar=-MASKED, in1=l2[:], op0=ALU.mult,
                                                  op1=ALU.add))
                step(dve.tensor_tensor(combine[:], combine[:], sel[:], ALU.mult))
                step(dve.tensor_reduce(tot[:], combine[:], AX.X, ALU.add))
                step(dve.reciprocal(tot[:], tot[:]))
                step(dve.tensor_scalar(tot[:], tot[:], core.gate[0:S, 3:4], None, ALU.mult))
                step(dve.tensor_tensor(combine[:], combine[:], widen(tot[:], 2, E1), ALU.mult))
                step(dve.scalar_tensor_tensor(out=core.x[:], in0=core.base[:], scalar=core.gate[0:S, 3:4],
                                              in1=core.x[:], op0=ALU.mult, op1=ALU.add))
                with dve.Fori(0, E1 // 2) as i:
                    for k in range(2):
                        e = 2 * i + k

                        def low_half(j):
                            f, n = j % FC, j // FC
                            at = slice(n * W, (n + 1) * W)
                            dve.wait_ge(ph_ready, NJ * e + j + 1)
                            dve.tensor_tensor(ph[:, 1, f, at], p[:, j % 2, :], ph[:, 0, f, at], ALU.subtract)\
                               .then_inc(pl_ready, 1)

                        for j in range(NJ):
                            dve.wait_ge(z_written, NJ * e + j + 1)
                            dve.wait_ge(g_ready, NJ * e + j + 3)
                            dve.wait_ge(pl_ready, NJ * e + j + 1)
                            dve.tensor_tensor(p[:, j % 2, :], zb[j % 2][:, 0:W], g[:, j % 2, :], ALU.mult)\
                               .then_inc(p_ready, 1)
                            if j >= 1:
                                low_half(j - 1)
                        low_half(NJ - 1)
                        for b in range(B):
                            dve.wait_ge(y_written, B * e + b + 1)
                            dve.scalar_tensor_tensor(
                                out=core.x[:, b, :], in0=yb[b % 4][0:S, 0:D],
                                scalar=combine[:, b, :][:, bass.ds(e, 1)], in1=core.x[:, b, :],
                                op0=ALU.mult, op1=ALU.add).then_inc(x_updated, 1)

            @block.scalar
            def _(act):
                act.sem_inc(g_ready, 2)
                act.wait_ge(diff_ready, 1)
                act.activation(combine[:], l2[:], ACT.Exp).then_inc(exp_ready, 1)
                with act.Fori(0, E1 // 2) as i:
                    for k in range(2):
                        e = 2 * i + k

                        def silu(j):
                            act.wait_ge(u_written, NJ * e + j + 1)
                            act.wait_ge(p_ready, NJ * e + j + 1)
                            act.activation(g[:, j % 2, :], ub[j % 2][:, 0:W], ACT.Silu).then_inc(g_ready, 1)

                        silu(0)
                        for j in range(NJ):
                            if j + 1 < NJ:
                                silu(j + 1)
                            f, n = j % FC, j // FC
                            act.wait_ge(p_ready, NJ * e + j + 3)
                            act.activation(ph[:, 0, f, n * W:(n + 1) * W], p[:, j % 2, :], ACT.Copy)\
                               .then_inc(ph_ready, 1)

            @block.tensor
            def _(pe):
                three = ((0, 0), (0, 1), (1, 0))
                with pe.Fori(0, E1 // 2) as i:
                    for k in range(2):
                        e = 2 * i + k
                        pe.wait_ge(w_split, 6 * e + 6)
                        for j in range(NJ):
                            f, n = j % FC, j // FC
                            terms = [(c, a, z) for c in range(DC) for a, z in three]
                            for m, banks, ready, written in ((0, ub, g_ready, u_written), (1, zb, p_ready, z_written)):
                                pe.wait_ge(ready, NJ * e + j + 1)
                                for q, (c, a, z) in enumerate(terms):
                                    last = pe.matmul(banks[j % 2][:, 0:W],
                                                     w[m][:, k, a, c * F1 + f * 128:c * F1 + (f + 1) * 128],
                                                     core.hT[:, z, c, n * W:(n + 1) * W], start=(q == 0),
                                                     stop=(q == len(terms) - 1))
                                last.then_inc(written, 1)
                        for b in range(B):
                            pe.wait_ge(pl_ready, NJ * e + FC * (b // SEQ + 1) + 2)
                            pe.wait_ge(x_updated, B * e + B + b + 1)
                            terms = [(f, a, z) for f in range(FC) for a, z in three]
                            for q, (f, a, z) in enumerate(terms):
                                last = pe.matmul(yb[b % 4][0:S, 0:D], ph[:, a, f, b * S:(b + 1) * S],
                                                 w[2][:, k, z, f * D:(f + 1) * D], start=(q == 0),
                                                 stop=(q == len(terms) - 1))
                            last.then_inc(y_written, 1)



def build(nc, inputs, out):
    core = Core(nc, inputs, out)
    with core.stack:
        with core.ctx_stack:
            load_stage(core)
            l0_xattn_stage(core)
        for stages in ((routing_stage, experts0_stage), (l1_xattn_stage,), (l1_self_attn_stage, experts1_stage)):
            with ExitStack() as kept:
                def keep(name, shape, dt=F32):
                    return kept.enter_context(nc.sbuf_tensor(name, shape, dt))

                for stage in stages:
                    stage(core, keep)
            core.clear_semaphores()
        store_stage(core)


def store_stage(core):
    with core.nc.Block() as block:

        @block.sync
        def _(sp):
            sp.dma_start(core.out.rearrange("b s d -> s b d"), core.x[:]).then_inc(core.stored, 16)
            sp.wait_ge(core.stored, 16)


def kernel(**inputs):
    import numpy as _np
    import concourse.bacc as _bacc
    from concourse import mybir as _mybir
    from concourse.bass_utils import run_bass_kernel_spmd as _run

    def take(name):
        return _np.asarray(inputs[name])

    def column(a, parts):
        out = _np.zeros((128, a.size // parts), _np.float32)
        out[:parts] = a.reshape(-1, parts).T
        return out

    def doubled(a):
        heads = a.reshape(*a.shape[:-1], H1, 1, HD1)
        return _np.repeat(heads, 2, -2).reshape(*a.shape[:-1], H1 * PAD)

    places = _np.arange(128) % PAD
    cols = {
        "lnx_g": column(take("L0_xattn_ln_x_g"), CF), "lnx_b": column(take("L0_xattn_ln_x_b"), CF),
        "lnl_g": column(take("L0_xattn_ln_l_g"), 128), "lnl_b": column(take("L0_xattn_ln_l_b"), 128),
        "qn_g": _np.tile(take("L0_xattn_qn_g"), 2)[:, None], "kn_g": _np.tile(take("L0_xattn_kn_g"), 2)[:, None],
        "bk": column(doubled(take("L1_xattn_bk")), 128),
        "pad_masks": _np.stack([places >= HD1, places < HD1, places == HD1], 1).astype(_np.float32),
        "attn_w": column(take("L1_ffn_attn_norm_w"), 128), "ffn_w": column(take("L1_ffn_ffn_norm_w"), 128),
    }
    rows = {
        "g_xattn": take("g_xattn"), "g_ffn": take("g_ffn"), "log_temp": take("L0_ffn_log_temp").reshape(1),
        "bo0": take("L0_xattn_bo"), "bo1": take("L1_xattn_bo"), "bv1": take("L1_xattn_bv"), "bq1": take("L1_xattn_bq"),
        "iota": _np.arange(CAP, dtype=_np.float32),
    }
    wlkv = take("L0_xattn_Wlkv")
    arrays = {
        "x": take("x"),
        "ctx": take("ctx_768"),
        "mask": take("mask_BxS2_bk0").reshape(1, B * C),
        "ident": _np.eye(128, dtype=_np.float32),
        "cols": _np.concatenate([cols[n] for n in COLS], 1),
        "rows": _np.concatenate([rows[n] for n in ROWS])[None, :],
        "w0kv": take("L0_xattn_Wkv").T,
        "w0l": _np.concatenate([wlkv[:D], take("L0_xattn_Wq"), wlkv[D:]]).T,
        "w0o": take("L0_xattn_Wo").T,
    }
    arrays.update(more_arrays(take, doubled, _np))
    arrays = {f"in_{n}": _np.ascontiguousarray(a) for n, a in arrays.items()}
    nc = _bacc.Bacc("TRN2", target_bir_lowering=False, num_devices=1)
    given = {n[3:]: nc.dram_tensor(n, a.shape, _mybir.dt.from_np(a.dtype), kind="ExternalInput").ap()
             for n, a in arrays.items()}
    out = nc.dram_tensor("out", (B, S, D), F32, kind="ExternalOutput").ap()
    build(nc, given, out)
    r = _run(nc, [arrays], core_ids=[0])
    return r.results[0]["out"]


def more_arrays(take, doubled, np):
    return {
        "w1q": take("L1_xattn_Wq"), "w1kv": np.concatenate([doubled(take("L1_xattn_Wk")), take("L1_xattn_Wv")], 1),
        "w1o": take("L1_xattn_Wo"),
        "s_wqk": np.concatenate([take("L1_ffn_wq"), take("L1_ffn_wk")], 1), "s_wv": take("L1_ffn_wv"),
        "s_wo": take("L1_ffn_wo"), "router": take("L1_ffn_router_w"), "freqs": take("L1_ffn_freqs_cis"),
        "causal": np.triu(np.full((S, S), NEG, np.float32), 1),
        "m_w1": take("L1_ffn_w1"), "m_w3": take("L1_ffn_w3"), "m_w2": take("L1_ffn_w2"),
        "gate_query": take("L0_ffn_gate_query").T,
        "w1": take("L0_ffn_w1"), "w2": take("L0_ffn_w2"),
        "b1": take("L0_ffn_b1").reshape(E0, F0 // 128, 128).transpose(0, 2, 1), "b2": take("L0_ffn_b2"),
    }
```
